# Optimizing a Trainium2 kernel written in Bass

```python
import numpy as np
import jax
import jax.numpy as jnp

def _softmax(x, axis=-1):
    return jax.nn.softmax(x, axis=axis)

def _gelu(x):
    return jax.nn.gelu(x, approximate=True)

def _silu(x):
    return jax.nn.silu(x)

def _sigmoid(x):
    return jax.nn.sigmoid(x)

def _layernorm(x, axis=-1, eps=1e-05):
    m = jnp.mean(x, axis=axis, keepdims=True)
    v = jnp.var(x, axis=axis, keepdims=True)
    return (x - m) / jnp.sqrt(v + eps)

def _scatter_add(tgt, idx, src, axis=0):
    return tgt.at[idx].add(src)

def _segment_sum(src, seg, n):
    return jax.ops.segment_sum(src, seg, n)
kernel_name = 'mk_decoder_postln_d2_seqx_r8_086ed8'

def setup_inputs(seed: int=0):
    np.random.seed(seed)
    _w = jnp.asarray

    def _rec_inputs():
        import jax
        import jax.numpy as jnp
        _rk = jax.random.key(seed)
        x = 0.0002417 + 0.9998 * jax.random.normal(jax.random.fold_in(_rk, 1), (32, 56, 128), jnp.float32)
        _lenS = 56 - jax.random.randint(jax.random.fold_in(_rk, 7), (32,), 0, max(1, 56 // 4) + 1, jnp.int32)
        _lenS2 = 1500 - jax.random.randint(jax.random.fold_in(_rk, 8), (32,), 0, max(1, 1500 // 4) + 1, jnp.int32)
        _ctx_1024P = jax.random.normal(jax.random.fold_in(_rk, 11), (32, 16, 128), jnp.float32)
        _ctx_1024c = jax.random.dirichlet(jax.random.fold_in(_rk, 511), 0.3 * jnp.ones((16,), jnp.float32), (32, 1500))
        _ctx_1024t = jnp.einsum('bsk,bkd->bsd', _ctx_1024c, _ctx_1024P)
        _ctx_1024t = _ctx_1024t * jax.lax.rsqrt(jnp.mean(jnp.square(_ctx_1024t)) + 1e-12) * 0.953939
        ctx_1024 = 7.22013e-05 + 1.00017 * (_ctx_1024t + 0.3 * jax.random.normal(jax.random.fold_in(_rk, 611), (32, 1500, 128), jnp.float32))
        return (x, ctx_1024)
    x, ctx_1024 = _rec_inputs()

    def _L0_attn_setup():
        import jax, jax.numpy as jnp
        import numpy as np
        N_HEADS = 16
        WINDOW = 32

        def _sliding_window_bias(seq_len: int) -> jnp.ndarray:
            i = jnp.arange(seq_len)[:, None]
            j = jnp.arange(seq_len)[None, :]
            allowed = jnp.abs(i - j) <= WINDOW
            return jnp.where(allowed, 0.0, -jnp.inf).astype(jnp.float32)
        key = jax.random.key(seed)
        ks = jax.random.split(key, 6)
        B, S, D = (2, 256, 128)
        std = 0.02
        x = jax.random.normal(ks[0], (B, S, D), dtype=jnp.float32)
        wq = jax.random.normal(ks[1], (D, D), dtype=jnp.float32) * std
        wk = jax.random.normal(ks[2], (D, D), dtype=jnp.float32) * std
        wv = jax.random.normal(ks[3], (D, D), dtype=jnp.float32) * std
        wo = jax.random.normal(ks[4], (D, D), dtype=jnp.float32) * std
        bq = jnp.zeros((D,), jnp.float32)
        bk = jnp.zeros((D,), jnp.float32)
        bv = jnp.zeros((D,), jnp.float32)
        bo = jnp.zeros((D,), jnp.float32)
        return {'x': x, 'wq': wq, 'bq': bq, 'wk': wk, 'bk': bk, 'wv': wv, 'bv': bv, 'wo': wo, 'bo': bo}
    _L0_attn_all = _L0_attn_setup()
    _L0_attn_in = {k: v for k, v in _L0_attn_all.items() if k in ('wq', 'bq', 'wk', 'bk', 'wv', 'bv', 'wo', 'bo')}
    del _L0_attn_all

    def _L0_xattn_setup():
        import jax, jax.numpy as jnp
        import numpy as np
        D_MODEL = 128
        B, S = (4, 256)
        key = jax.random.key(seed)
        ks = jax.random.split(key, 10)
        s = 1.0 / np.sqrt(D_MODEL)
        return {'k': jax.random.normal(ks[0], (B, S, D_MODEL), jnp.float32), 'v': jax.random.normal(ks[1], (B, S, D_MODEL), jnp.float32), 'q': jax.random.normal(ks[2], (B, S, D_MODEL), jnp.float32), 'Wk': jax.random.normal(ks[3], (D_MODEL, D_MODEL), jnp.float32) * s, 'Wv': jax.random.normal(ks[4], (D_MODEL, D_MODEL), jnp.float32) * s, 'bv': jnp.zeros((D_MODEL,), jnp.float32), 'Wq': jax.random.normal(ks[5], (D_MODEL, D_MODEL), jnp.float32) * s, 'bq': jnp.zeros((D_MODEL,), jnp.float32), 'Wo': jax.random.normal(ks[6], (D_MODEL, D_MODEL), jnp.float32) * s, 'bo': jnp.zeros((D_MODEL,), jnp.float32)}
    _L0_xattn_all = _L0_xattn_setup()
    _L0_xattn_in = {k: v for k, v in _L0_xattn_all.items() if k in ('Wk', 'Wv', 'bv', 'Wq', 'bq', 'Wo', 'bo')}
    del _L0_xattn_all

    def _L0_ffn_setup():
        import jax, jax.numpy as jnp
        import numpy as np
        TOP_K = 2
        key = jax.random.key(seed)
        ks = jax.random.split(key, 6)
        B, S, D, U, E = (4, 128, 128, 512, 8)
        return {'x': jax.random.normal(ks[0], (B, S, D), dtype=jnp.float32), 'w_up': jax.random.normal(ks[1], (E, U, D), dtype=jnp.float32), 'w_down': jax.random.normal(ks[2], (E, D, U), dtype=jnp.float32), 'b_up': jax.random.normal(ks[3], (E, U), dtype=jnp.float32), 'b_down': jax.random.normal(ks[4], (E, D), dtype=jnp.float32), 'w_router': jax.random.normal(ks[5], (E, D), dtype=jnp.float32)}
    _L0_ffn_all = _L0_ffn_setup()
    _L0_ffn_in = {k: v for k, v in _L0_ffn_all.items() if k in ('w_up', 'w_down', 'b_up', 'b_down', 'w_router')}
    del _L0_ffn_all

    def _L1_attn_setup():
        import jax, jax.numpy as jnp
        import numpy as np
        B, S, DIM, SDIM = (4, 512, 128, 32)
        key = jax.random.key(seed)
        ks = jax.random.split(key, 10)

        def lin(k, din, dout):
            return jax.random.normal(k, (din, dout), jnp.float32) / np.float32(np.sqrt(din))
        return {'x': jax.random.normal(ks[0], (B, S, DIM), jnp.float32), 'ln_g': jnp.ones((DIM,), jnp.float32), 'ln_b': jnp.zeros((DIM,), jnp.float32), 'mix_w': jax.random.normal(ks[1], (DIM, 1, 3), jnp.float32) * 0.3, 'mix_b': jnp.zeros((DIM,), jnp.float32), 'Wi': lin(ks[2], DIM, DIM), 'bi': jnp.zeros((DIM,), jnp.float32), 'Wsin': lin(ks[3], DIM, SDIM), 'bsin': jnp.zeros((SDIM,), jnp.float32), 'Wd': lin(ks[4], DIM, SDIM), 'bd': jnp.zeros((SDIM,), jnp.float32), 'Wsel': lin(ks[5], DIM, SDIM), 'bsel': jnp.zeros((SDIM,), jnp.float32), 'Wso': lin(ks[6], SDIM, DIM), 'bso': jnp.zeros((DIM,), jnp.float32), 'Wg': lin(ks[7], DIM, DIM), 'bg': jnp.zeros((DIM,), jnp.float32), 'Wout': lin(ks[8], DIM, DIM), 'bout': jnp.zeros((DIM,), jnp.float32)}
    _L1_attn_all = _L1_attn_setup()
    _L1_attn_in = {k: v for k, v in _L1_attn_all.items() if k in ('ln_g', 'ln_b', 'mix_w', 'mix_b', 'Wi', 'bi', 'Wsin', 'bsin', 'Wd', 'bd', 'Wsel', 'bsel', 'Wso', 'bso', 'Wg', 'bg', 'Wout', 'bout')}
    del _L1_attn_all

    def _L1_xattn_setup():
        import jax, jax.numpy as jnp
        import numpy as np
        DIM = 128
        NUM_HEADS = 16
        DIM_HEAD = 64
        INNER = NUM_HEADS * DIM_HEAD
        SCALE = DIM_HEAD ** (-0.5)

        def _layernorm(x, gamma, beta, eps=1e-05):
            mu = jnp.mean(x, axis=-1, keepdims=True)
            var = jnp.mean(jnp.square(x - mu), axis=-1, keepdims=True)
            return (x - mu) * jax.lax.rsqrt(var + eps) * gamma + beta
        key = jax.random.key(seed)
        ks = jax.random.split(key, 8)
        B, SQ, SK = (2, 256, 512)
        x = jax.random.normal(ks[0], (B, SQ, DIM), dtype=jnp.float32)
        context = jax.random.normal(ks[1], (B, SK, DIM), dtype=jnp.float32)
        ln_gamma = jnp.ones((DIM,), jnp.float32)
        ln_beta = jnp.zeros((DIM,), jnp.float32)
        w_q = jax.random.normal(ks[2], (DIM, INNER), dtype=jnp.float32) / np.sqrt(DIM)
        w_kv = jax.random.normal(ks[3], (DIM, 2 * INNER), dtype=jnp.float32) / np.sqrt(DIM)
        w_out = jax.random.normal(ks[4], (INNER, DIM), dtype=jnp.float32) / np.sqrt(INNER)
        b_out = jnp.zeros((DIM,), jnp.float32)
        gate = jnp.array([0.5], jnp.float32)
        return {'x': x, 'context': context, 'ln_gamma': ln_gamma, 'ln_beta': ln_beta, 'w_q': w_q, 'w_kv': w_kv, 'w_out': w_out, 'b_out': b_out, 'gate': gate}
    _L1_xattn_all = _L1_xattn_setup()
    _L1_xattn_in = {k: v for k, v in _L1_xattn_all.items() if k in ('ln_gamma', 'ln_beta', 'w_q', 'w_kv', 'w_out', 'b_out', 'gate')}
    del _L1_xattn_all

    def _L1_ffn_setup():
        import jax, jax.numpy as jnp
        import numpy as np
        B, S, H = (2, 256, 128)
        E_ROUTED = 8
        TOP_K = 2
        I = 256
        key = jax.random.key(seed)
        ks = jax.random.split(key, 9)
        s = 0.02
        return {'x': jax.random.normal(ks[0], (B, S, H), dtype=jnp.float32), 'shared_gate': jax.random.normal(ks[1], (I, H), dtype=jnp.float32) * s, 'shared_up': jax.random.normal(ks[2], (I, H), dtype=jnp.float32) * s, 'shared_down': jax.random.normal(ks[3], (H, I), dtype=jnp.float32) * s, 'gate_w': jax.random.normal(ks[4], (E_ROUTED, H, I), dtype=jnp.float32) * s, 'up_w': jax.random.normal(ks[5], (E_ROUTED, H, I), dtype=jnp.float32) * s, 'down_w': jax.random.normal(ks[6], (E_ROUTED, I, H), dtype=jnp.float32) * s, 'router_w': jax.random.normal(ks[7], (E_ROUTED, H), dtype=jnp.float32) * s, 'routing_bias': jnp.zeros((E_ROUTED,), dtype=jnp.float32)}
    _L1_ffn_all = _L1_ffn_setup()
    _L1_ffn_in = {k: v for k, v in _L1_ffn_all.items() if k in ('shared_gate', 'shared_up', 'shared_down', 'gate_w', 'up_w', 'down_w', 'router_w', 'routing_bias')}
    del _L1_ffn_all
    return {'x': x, 'ctx_1024': ctx_1024, 'L0_attn_wq': _L0_attn_in['wq'], 'L0_attn_bq': _L0_attn_in['bq'], 'L0_attn_wk': _L0_attn_in['wk'], 'L0_attn_bk': _L0_attn_in['bk'], 'L0_attn_wv': _L0_attn_in['wv'], 'L0_attn_bv': _L0_attn_in['bv'], 'L0_attn_wo': _L0_attn_in['wo'], 'L0_attn_bo': _L0_attn_in['bo'], 'L0_xattn_Wk': _L0_xattn_in['Wk'], 'L0_xattn_Wv': _L0_xattn_in['Wv'], 'L0_xattn_bv': _L0_xattn_in['bv'], 'L0_xattn_Wq': _L0_xattn_in['Wq'], 'L0_xattn_bq': _L0_xattn_in['bq'], 'L0_xattn_Wo': _L0_xattn_in['Wo'], 'L0_xattn_bo': _L0_xattn_in['bo'], 'L0_ffn_w_up': _L0_ffn_in['w_up'], 'L0_ffn_w_down': _L0_ffn_in['w_down'], 'L0_ffn_b_up': _L0_ffn_in['b_up'], 'L0_ffn_b_down': _L0_ffn_in['b_down'], 'L0_ffn_w_router': _L0_ffn_in['w_router'], 'L1_attn_ln_g': _L1_attn_in['ln_g'], 'L1_attn_ln_b': _L1_attn_in['ln_b'], 'L1_attn_mix_w': _L1_attn_in['mix_w'], 'L1_attn_mix_b': _L1_attn_in['mix_b'], 'L1_attn_Wi': _L1_attn_in['Wi'], 'L1_attn_bi': _L1_attn_in['bi'], 'L1_attn_Wsin': _L1_attn_in['Wsin'], 'L1_attn_bsin': _L1_attn_in['bsin'], 'L1_attn_Wd': _L1_attn_in['Wd'], 'L1_attn_bd': _L1_attn_in['bd'], 'L1_attn_Wsel': _L1_attn_in['Wsel'], 'L1_attn_bsel': _L1_attn_in['bsel'], 'L1_attn_Wso': _L1_attn_in['Wso'], 'L1_attn_bso': _L1_attn_in['bso'], 'L1_attn_Wg': _L1_attn_in['Wg'], 'L1_attn_bg': _L1_attn_in['bg'], 'L1_attn_Wout': _L1_attn_in['Wout'], 'L1_attn_bout': _L1_attn_in['bout'], 'L1_xattn_ln_gamma': _L1_xattn_in['ln_gamma'], 'L1_xattn_ln_beta': _L1_xattn_in['ln_beta'], 'L1_xattn_w_q': _L1_xattn_in['w_q'], 'L1_xattn_w_kv': _L1_xattn_in['w_kv'], 'L1_xattn_w_out': _L1_xattn_in['w_out'], 'L1_xattn_b_out': _L1_xattn_in['b_out'], 'L1_xattn_gate': _L1_xattn_in['gate'], 'L1_ffn_shared_gate': _L1_ffn_in['shared_gate'], 'L1_ffn_shared_up': _L1_ffn_in['shared_up'], 'L1_ffn_shared_down': _L1_ffn_in['shared_down'], 'L1_ffn_gate_w': _L1_ffn_in['gate_w'], 'L1_ffn_up_w': _L1_ffn_in['up_w'], 'L1_ffn_down_w': _L1_ffn_in['down_w'], 'L1_ffn_router_w': _L1_ffn_in['router_w'], 'L1_ffn_routing_bias': _L1_ffn_in['routing_bias']}

def reference(x, ctx_1024, L0_attn_wq, L0_attn_bq, L0_attn_wk, L0_attn_bk, L0_attn_wv, L0_attn_bv, L0_attn_wo, L0_attn_bo, L0_xattn_Wk, L0_xattn_Wv, L0_xattn_bv, L0_xattn_Wq, L0_xattn_bq, L0_xattn_Wo, L0_xattn_bo, L0_ffn_w_up, L0_ffn_w_down, L0_ffn_b_up, L0_ffn_b_down, L0_ffn_w_router, L1_attn_ln_g, L1_attn_ln_b, L1_attn_mix_w, L1_attn_mix_b, L1_attn_Wi, L1_attn_bi, L1_attn_Wsin, L1_attn_bsin, L1_attn_Wd, L1_attn_bd, L1_attn_Wsel, L1_attn_bsel, L1_attn_Wso, L1_attn_bso, L1_attn_Wg, L1_attn_bg, L1_attn_Wout, L1_attn_bout, L1_xattn_ln_gamma, L1_xattn_ln_beta, L1_xattn_w_q, L1_xattn_w_kv, L1_xattn_w_out, L1_xattn_b_out, L1_xattn_gate, L1_ffn_shared_gate, L1_ffn_shared_up, L1_ffn_shared_down, L1_ffn_gate_w, L1_ffn_up_w, L1_ffn_down_w, L1_ffn_router_w, L1_ffn_routing_bias):
    import jax
    import jax.numpy as jnp

    def _L0_attn_ref(x, wq, bq, wk, bk, wv, bv, wo, bo):
        import jax, jax.numpy as jnp
        import numpy as np
        N_HEADS = 16
        WINDOW = 32

        def _sliding_window_bias(seq_len: int) -> jnp.ndarray:
            i = jnp.arange(seq_len)[:, None]
            j = jnp.arange(seq_len)[None, :]
            allowed = jnp.abs(i - j) <= WINDOW
            return jnp.where(allowed, 0.0, -jnp.inf).astype(jnp.float32)
        B, S, D = x.shape
        H = N_HEADS
        dh = D // H
        scale = dh ** (-0.5)
        q = (x @ wq.T + bq).reshape(B, S, H, dh).transpose(0, 2, 1, 3)
        k = (x @ wk.T + bk).reshape(B, S, H, dh).transpose(0, 2, 1, 3)
        v = (x @ wv.T + bv).reshape(B, S, H, dh).transpose(0, 2, 1, 3)
        scores = jnp.einsum('bhqd,bhkd->bhqk', q, k) * scale
        scores = scores + _sliding_window_bias(S)[None, None]
        attn = jax.nn.softmax(scores, axis=-1)
        out = jnp.einsum('bhqk,bhkd->bhqd', attn, v)
        out = out.transpose(0, 2, 1, 3).reshape(B, S, D)
        return out @ wo.T + bo

    def _L0_xattn_ref(k, v, q, Wk, Wv, bv, Wq, bq, Wo, bo):
        import jax, jax.numpy as jnp
        import numpy as np
        D_MODEL = 128
        B, S = (4, 256)
        kp = jnp.einsum('bsd,ed->bse', k, Wk)
        vp = jnp.einsum('bsd,ed->bse', v, Wv) + bv
        qp = jnp.einsum('bsd,ed->bse', q, Wq) + bq
        scale = 1.0 / jnp.sqrt(jnp.float32(kp.shape[-1]))
        scores = jnp.einsum('bqd,bkd->bqk', qp, kp) * scale
        probs = jax.nn.softmax(scores, axis=-1)
        ctx = jnp.einsum('bqk,bkd->bqd', probs, vp)
        return jnp.einsum('bqd,ed->bqe', ctx, Wo) + bo

    def _L0_ffn_ref(x, w_up, w_down, b_up, b_down, w_router):
        import jax, jax.numpy as jnp
        import numpy as np
        TOP_K = 2
        logits = jnp.einsum('bsd,ed->bse', x, w_router)
        top_vals, top_idx = jax.lax.top_k(logits, TOP_K)
        router_weights = jax.nn.softmax(top_vals, axis=-1)
        up = jnp.einsum('eud,bsd->bseu', w_up, x) + b_up
        h = jax.nn.gelu(up, approximate=False)
        down = jnp.einsum('edu,bseu->bsed', w_down, h) + b_down
        sel = jnp.take_along_axis(down, top_idx[..., None], axis=2)
        return jnp.einsum('bskd,bsk->bsd', sel, router_weights)

    def _L1_attn_ref(x, ln_g, ln_b, mix_w, mix_b, Wi, bi, Wsin, bsin, Wd, bd, Wsel, bsel, Wso, bso, Wg, bg, Wout, bout):
        import jax, jax.numpy as jnp
        import numpy as np
        B, S, DIM, SDIM = (4, 512, 128, 32)
        eps = 1e-05
        mu = jnp.mean(x, axis=-1, keepdims=True)
        var = jnp.mean(jnp.square(x - mu), axis=-1, keepdims=True)
        h = (x - mu) * jax.lax.rsqrt(var + eps) * ln_g + ln_b
        hc = jnp.transpose(h, (0, 2, 1))
        mixed = jax.lax.conv_general_dilated(hc, mix_w, window_strides=(1,), padding=[(1, 1)], dimension_numbers=('NCH', 'OIH', 'NCH'), feature_group_count=hc.shape[1])
        mixed = jnp.transpose(mixed + mix_b[None, :, None], (0, 2, 1))
        u = jnp.tanh(mixed @ Wi + bi)
        x_state = jnp.tanh(mixed @ Wsin + bsin)
        decay = jax.nn.sigmoid(mixed @ Wd + bd)
        select = jax.nn.sigmoid(mixed @ Wsel + bsel)

        def step(state, inp):
            dt, xt = inp
            state = dt * state + (1.0 - dt) * xt
            return (state, state)
        init = jnp.zeros((x.shape[0], x_state.shape[-1]), x.dtype)
        _, states = jax.lax.scan(step, init, (jnp.swapaxes(decay, 0, 1), jnp.swapaxes(x_state, 0, 1)))
        states = jnp.swapaxes(states, 0, 1)
        y = select * states @ Wso + bso
        g = jax.nn.sigmoid(mixed @ Wg + bg)
        out = (g * y + (1.0 - g) * u) @ Wout + bout
        return x + out

    def _L1_xattn_ref(x, context, ln_gamma, ln_beta, w_q, w_kv, w_out, b_out, gate):
        import jax, jax.numpy as jnp
        import numpy as np
        DIM = 128
        NUM_HEADS = 16
        DIM_HEAD = 64
        INNER = NUM_HEADS * DIM_HEAD
        SCALE = DIM_HEAD ** (-0.5)

        def _layernorm(x, gamma, beta, eps=1e-05):
            mu = jnp.mean(x, axis=-1, keepdims=True)
            var = jnp.mean(jnp.square(x - mu), axis=-1, keepdims=True)
            return (x - mu) * jax.lax.rsqrt(var + eps) * gamma + beta
        B, SQ, _ = x.shape
        SK = context.shape[1]
        xn = _layernorm(x, ln_gamma, ln_beta)
        q = (xn @ w_q).reshape(B, SQ, NUM_HEADS, DIM_HEAD)
        kv = context @ w_kv
        k, v = jnp.split(kv, 2, axis=-1)
        k = k.reshape(B, SK, NUM_HEADS, DIM_HEAD)
        v = v.reshape(B, SK, NUM_HEADS, DIM_HEAD)
        scores = jnp.einsum('bqhd,bkhd->bhqk', q * SCALE, k)
        attn = jax.nn.softmax(scores, axis=-1)
        out = jnp.einsum('bhqk,bkhd->bqhd', attn, v).reshape(B, SQ, INNER)
        out = out @ w_out + b_out
        return out * jnp.tanh(gate[0])

    def _L1_ffn_ref(x, shared_gate, shared_up, shared_down, gate_w, up_w, down_w, router_w, routing_bias):
        import jax, jax.numpy as jnp
        import numpy as np
        B, S, H = (2, 256, 128)
        E_ROUTED = 8
        TOP_K = 2
        I = 256
        b, s, h = x.shape
        shared = jnp.einsum('bsi,hi->bsh', jax.nn.silu(jnp.einsum('bsh,ih->bsi', x, shared_gate)) * jnp.einsum('bsh,ih->bsi', x, shared_up), shared_down)
        logits = jnp.einsum('bsh,eh->bse', x, router_w) + routing_bias
        probs = jax.nn.sigmoid(logits)
        scores, indices = jax.lax.top_k(probs, TOP_K)
        scores = scores / jnp.sum(scores, axis=-1, keepdims=True)
        t = b * s
        xf = x.reshape(t, h)
        idx = indices.reshape(t, TOP_K)
        sc = scores.reshape(t, TOP_K)
        w = jnp.zeros((t, E_ROUTED), dtype=x.dtype)
        w = w.at[jnp.arange(t)[:, None], idx].add(sc)
        g = jax.nn.silu(jnp.einsum('th,ehi->tei', xf, gate_w))
        u = jnp.einsum('th,ehi->tei', xf, up_w)
        combined = jnp.einsum('tei,eih,te->th', g * u, down_w, w)
        return shared + combined.reshape(b, s, h)
    x = _layernorm(x + _L0_attn_ref(x, L0_attn_wq, L0_attn_bq, L0_attn_wk, L0_attn_bk, L0_attn_wv, L0_attn_bv, L0_attn_wo, L0_attn_bo), axis=-1)
    x = _layernorm(x + _L0_xattn_ref(ctx_1024, ctx_1024, x, L0_xattn_Wk, L0_xattn_Wv, L0_xattn_bv, L0_xattn_Wq, L0_xattn_bq, L0_xattn_Wo, L0_xattn_bo), axis=-1)
    x = _layernorm(x + _L0_ffn_ref(x, L0_ffn_w_up, L0_ffn_w_down, L0_ffn_b_up, L0_ffn_b_down, L0_ffn_w_router), axis=-1)
    x = _layernorm(x + _L1_attn_ref(x, L1_attn_ln_g, L1_attn_ln_b, L1_attn_mix_w, L1_attn_mix_b, L1_attn_Wi, L1_attn_bi, L1_attn_Wsin, L1_attn_bsin, L1_attn_Wd, L1_attn_bd, L1_attn_Wsel, L1_attn_bsel, L1_attn_Wso, L1_attn_bso, L1_attn_Wg, L1_attn_bg, L1_attn_Wout, L1_attn_bout), axis=-1)
    x = _layernorm(x + _L1_xattn_ref(x, ctx_1024, L1_xattn_ln_gamma, L1_xattn_ln_beta, L1_xattn_w_q, L1_xattn_w_kv, L1_xattn_w_out, L1_xattn_b_out, L1_xattn_gate), axis=-1)
    x = _layernorm(x + _L1_ffn_ref(x, L1_ffn_shared_gate, L1_ffn_shared_up, L1_ffn_shared_down, L1_ffn_gate_w, L1_ffn_up_w, L1_ffn_down_w, L1_ffn_router_w, L1_ffn_routing_bias), axis=-1)
    return x

_drawn_inputs = setup_inputs


def setup_inputs(seed=0):
    import zlib

    import numpy as np

    out = dict(_drawn_inputs(seed))
    spreads = {'L0_attn_bq': (0.0, 0.8),
     'L0_attn_bk': (0.0, 0.8),
     'L0_attn_bv': (0.0, 0.1),
     'L0_attn_bo': (0.0, 0.1),
     'L0_xattn_bv': (0.0, 0.1),
     'L0_xattn_bq': (0.0, 0.1),
     'L0_xattn_bo': (0.0, 0.1),
     'L1_attn_ln_g': (1.0, 0.6),
     'L1_attn_ln_b': (0.0, 0.8),
     'L1_attn_mix_b': (0.0, 0.378),
     'L1_attn_bi': (0.0, 0.421),
     'L1_attn_bsin': (0.0, 0.732),
     'L1_attn_bd': (0.0, 0.8),
     'L1_attn_bsel': (0.0, 0.8),
     'L1_attn_bso': (0.0, 0.356),
     'L1_attn_bg': (0.0, 0.8),
     'L1_attn_bout': (0.0, 0.1),
     'L1_xattn_ln_gamma': (1.0, 0.6),
     'L1_xattn_ln_beta': (0.0, 0.776),
     'L1_xattn_b_out': (0.0, 0.1),
     'L1_ffn_routing_bias': (0.0, 0.8)}
    factors = {'L0_attn_wq': 8.0,
     'L0_attn_wk': 8.0,
     'L0_ffn_b_down': 8.0,
     'L1_attn_Wd': 6.286,
     'L1_attn_Wsel': 6.053,
     'L1_ffn_shared_gate': 6.848,
     'L1_ffn_shared_up': 6.826,
     'L1_ffn_shared_down': 6.787,
     'L1_ffn_gate_w': 8.0,
     'L1_ffn_up_w': 8.0,
     'L1_ffn_down_w': 8.0,
     'L1_ffn_router_w': 8.0}
    for name, (base, spread) in spreads.items():
        noise = np.random.default_rng([zlib.crc32(name.encode()), seed]).standard_normal(out[name].shape)
        drawn = base * np.exp(spread * noise) if base else spread * noise
        out[name] = jnp.asarray(drawn.astype(out[name].dtype))
    for name, factor in factors.items():
        out[name] = (out[name] * factor).astype(out[name].dtype)
    return out
```

```python
from contextlib import ExitStack

import numpy as np
import concourse.bass as bass
from concourse import mybir

fp32 = mybir.dt.float32
fp32r = mybir.dt.float32r
u32 = mybir.dt.uint32
ALU = mybir.AluOpType
ACT = mybir.ActivationFunctionType
AX = mybir.AxisListType

B, S, D = 32, 56, 128
SP = 64
PAIRS = B // 2
CK = 4
CHUNKS = PAIRS // CK
CB = 2 * CK
CT = CB * S
C, KT, KP = 1500, 12, 125
H0, DH0, WIN = 16, 8, 32
H1, DH1 = 16, 64
E, U0, I1 = 8, 512, 256
EPS = 1e-5
NEG = -1.0e30


def this(i, n=1, per=1):
    return i * per + (per + n)


def last(i, n=1, per=1):
    return i * per + n


class Core:

    def __init__(self, nc, ctx, dram):
        self.nc, self.ctx, self.dram = nc, ctx, dram
        self.used = []

    def sb(self, ctx, name, shape, dt=fp32):
        return ctx.enter_context(self.nc.sbuf_tensor(name, shape, dt))

    def sem(self, ctx, name):
        handle = ctx.enter_context(self.nc.semaphore(name))
        self.used.append(handle.num)
        return handle

    def clear_semaphores(self):
        nums, self.used = sorted(self.used), []
        with self.nc.Block() as block:
            @block.gpsimd
            def _(pool):
                start = nums[0]
                for a, b in zip(nums, nums[1:] + [None]):
                    if b != a + 1:
                        pool.sem_clear(range(start, a + 1))
                        start = b


def setup_phase(k):
    nc, d = k.nc, k.dram
    with ExitStack() as ctx:
        consts_built = k.sem(ctx, "consts_built")
        pads_zeroed = k.sem(ctx, "pads_zeroed")
        tanh_gate_ready = k.sem(ctx, "tanh_gate_ready")
        row_ready = k.sem(ctx, "row_ready")
        psum = ctx.enter_context(nc.psum_tensor("setup_psum", [128, 8, 512], fp32))
        fold_ready = k.sem(ctx, "fold_ready")
        fold_used = k.sem(ctx, "fold_used")
        wqT1 = k.sb(ctx, "wqT1", [DH1, H1, D])
        wkT1 = k.sb(ctx, "wkT1", [DH1, H1, D])
        wvT1 = k.sb(ctx, "wvT1", [DH1, H1, D])
        wo1 = k.sb(ctx, "wo1", [DH1, H1, D])
        block = ctx.enter_context(nc.Block())

        @block.sync
        def _(sp):
            for name, dst in k.loads:
                sp.dma_start(dst, d[name]).then_inc(k.weights_loaded, 16)
            for name, dst in (("L1_wqT", wqT1), ("L1_wkT", wkT1), ("L1_wvT", wvT1), ("L1_wo", wo1)):
                sp.dma_start(dst[:, :, :], d[name]).then_inc(k.fold_loaded, 16)
            for name, dst in k.late_loads:
                sp.dma_start(dst, d[name]).then_inc(k.late_weights_loaded, 16)

        @block.gpsimd
        def _(pool):
            n = 0

            def step(instruction):
                nonlocal n
                n += 1
                instruction.then_inc(consts_built, 1)

            step(pool.memset(k.ident[:, :], 0.0))
            step(pool.memset(k.window_mask[:, :], 0.0))
            step(pool.memset(k.head_mask[:, :], 1.0))
            step(pool.memset(k.value_mask[:, :, :, :], 1.0))
            step(pool.memset(k.minus_half[:, :], -0.5))
            step(pool.memset(k.eps[:, :], EPS))
            pool.wait_ge(consts_built, n)
            step(pool.affine_select(out=k.ident[:, :], in_=k.ident[:, :], compare_op=ALU.not_equal,
                                    fill=1.0, base=0, pattern=[[-1, 128]], channel_multiplier=1))
            for half in range(2):
                rows = k.window_mask[half * SP:(half + 1) * SP, :]
                pool.wait_ge(consts_built, n)
                step(pool.affine_select(out=rows, in_=rows, compare_op=ALU.is_ge, fill=NEG,
                                        base=WIN, pattern=[[-1, S]], channel_multiplier=1))
                pool.wait_ge(consts_built, n)
                step(pool.affine_select(out=rows, in_=rows, compare_op=ALU.is_ge, fill=NEG,
                                        base=WIN, pattern=[[1, S]], channel_multiplier=-1))
            pool.wait_ge(consts_built, n)
            step(pool.affine_select(out=k.head_mask[:, :], in_=k.head_mask[:, :], compare_op=ALU.is_ge,
                                    fill=0.0, base=0, pattern=[[-DH0, H0]], channel_multiplier=1))
            pool.wait_ge(consts_built, n)
            step(pool.affine_select(out=k.head_mask[:, :], in_=k.head_mask[:, :], compare_op=ALU.is_ge,
                                    fill=0.0, base=DH0 - 1, pattern=[[DH0, H0]], channel_multiplier=-1))
            pool.wait_ge(consts_built, n)
            even = k.value_mask[:, :, 0, :]
            step(pool.affine_select(out=even, in_=even, compare_op=ALU.is_ge, fill=0.0,
                                    base=S - 1, pattern=[[0, H0 // 2], [0, DH0]], channel_multiplier=-1))
            odd = k.value_mask[:, :, 1, :]
            step(pool.affine_select(out=odd, in_=odd, compare_op=ALU.is_ge, fill=0.0,
                                    base=-S, pattern=[[0, H0 // 2], [0, DH0]], channel_multiplier=1))
            step(pool.iota(k.expert_index_u[:, :], pattern=[[1, E]], base=0, channel_multiplier=0))
            pool.wait_ge(consts_built, n)
            step(pool.tensor_copy(k.expert_index[:, :], k.expert_index_u[:, :]))
            pool.wait_ge(consts_built, n)

        @block.vector
        def _(dve):
            dve.memset(k.x_tok[:, :, :], 0.0).then_inc(pads_zeroed, 1)
            for g in range(2 * H1 // 4):
                dst = k.key_query if g < 4 else k.value_out
                h = 4 * (g % 4)
                dve.wait_ge(fold_ready, g + 1)
                nc.vector.tensor_copy(dst[:, h:h + 4, :],
                                      psum[:, g, :].rearrange("p (h n) -> p h n", h=4)).then_inc(fold_used, 1)
            dve.wait_ge(row_ready, 1)
            nc.vector.tensor_tensor(k.cross_row[:, :], psum[:, 0, 0:D], k.bo_row0x[:, :], ALU.add)\
                .then_inc(fold_used, 1)
            dve.wait_ge(fold_used, 2 * H1 // 4 + 1)
            dve.wait_ge(tanh_gate_ready, 1)
            dve.wait_ge(pads_zeroed, 1)

        @block.tensor
        def _(pe):
            pe.wait_ge(k.fold_loaded, 4 * 16)
            for g in range(8):
                a, b = (wqT1, wkT1) if g < 4 else (wvT1, wo1)
                for j in range(4):
                    h = 4 * (g % 4) + j
                    done = nc.tensor.matmul(psum[:, g, j * D:(j + 1) * D], a[:, h, :], b[:, h, :],
                                            start=True, stop=True)
                done.then_inc(fold_ready, 1)
            pe.wait_ge(k.weights_loaded, 16 * len(k.loads))
            pe.wait_ge(fold_used, 1)
            nc.tensor.matmul(psum[:, 0, 0:D], k.bv0x[:, 0:1].to_broadcast([128, 128]), k.woT0x[:, :],
                             start=True, stop=True).then_inc(row_ready, 1)

        @block.scalar
        def _(act):
            act.wait_ge(k.weights_loaded, 16 * len(k.loads))
            nc.scalar.activation(k.gate_tanh[:, :], k.gate_in[:, :], ACT.Tanh).then_inc(tanh_gate_ready, 1)


def open_sems(engine, per, *sems):
    for s in sems:
        engine.sem_inc(s, per)


class Tail:

    def __init__(self, k, ctx, tag, inner=None, router=None, final=False):
        sem = lambda name: k.sem(ctx, f"{tag}_{name}")
        self.k, self.inner, self.router, self.final = k, inner, router, final
        self.per = CK
        self.r = k.sb(ctx, tag + "_r", [128, self.per, D])
        self.moments = k.sb(ctx, tag + "_moments", [128, self.per, 6])
        self.mean_var = k.sb(ctx, tag + "_mean_var", [128, self.per, 2])
        self.var_eps = k.sb(ctx, tag + "_var_eps", [128, self.per, 1])
        self.rstd = k.sb(ctx, tag + "_rstd", [128, self.per, 1])
        self.xn = k.sb(ctx, tag + "_xn", [128, self.per, D])
        self.r_ready = sem("r_ready")
        self.moments_ready = sem("moments_ready")
        self.mean_var_ready = sem("mean_var_ready")
        self.var_eps_ready = sem("var_eps_ready")
        self.aggregating = sem("aggregating")
        self.storing = sem("storing")
        self.rstd_ready = sem("rstd_ready")
        self.xn_ready = sem("xn_ready")
        self.xnT_ready = sem("xnT_ready")
        self.feat_stored = sem("feat_stored")
        self.tok_stored = sem("tok_stored")
        if inner:
            self.moments2 = k.sb(ctx, tag + "_moments2", [128, self.per, 6])
            self.mean_var2 = k.sb(ctx, tag + "_mean_var2", [128, self.per, 2])
            self.var_eps2 = k.sb(ctx, tag + "_var_eps2", [128, self.per, 1])
            self.rstd2 = k.sb(ctx, tag + "_rstd2", [128, self.per, 1])
            self.xn2 = k.sb(ctx, tag + "_xn2", [128, self.per, D])
            self.moments2_ready = sem("moments2_ready")
            self.mean_var2_ready = sem("mean_var2_ready")
            self.var_eps2_ready = sem("var_eps2_ready")
            self.rstd2_ready = sem("rstd2_ready")
            self.xn2_ready = sem("xn2_ready")
        if router is not None:
            self.xnT = k.sb(ctx, tag + "_xnT", [128, 128])
            self.xnT_kept = sem("xnT_kept")
            self.logits_ready = sem("logits_ready")
            self.logits_kept = sem("logits_kept")
        self.out = self.xn2 if inner else self.xn
        self.out_ready = self.xn2_ready if inner else self.xn_ready

    def open_vector(self, dve):
        open_sems(dve, self.per, self.r_ready, self.moments_ready, self.mean_var_ready, self.xn_ready)
        if self.inner:
            open_sems(dve, self.per, self.moments2_ready, self.mean_var2_ready, self.xn2_ready)

        if self.router is not None:
            open_sems(dve, self.per, self.logits_kept)

    def open_pool(self, pool):
        open_sems(pool, self.per, self.var_eps_ready, self.rstd_ready, self.tok_stored)
        if self.inner:
            open_sems(pool, self.per, self.var_eps2_ready, self.rstd2_ready)

    def open_tensor(self, pe):
        open_sems(pe, self.per, self.xnT_ready)
        if self.router is not None:
            open_sems(pe, self.per, self.logits_ready)

    def open_scalar(self, act):
        open_sems(act, self.per, self.feat_stored)
        if self.router is not None:
            open_sems(act, self.per, self.xnT_kept)

    def vector_moments(self, dve, i, p):
        nc = self.k.nc
        dve.wait_ge(self.r_ready, this(i, p + 1, self.per))
        nc.vector.bn_stats(self.moments[:, p, :], self.r[:, p, :]).then_inc(self.moments_ready, 1)
        dve.wait_ge(self.moments_ready, this(i, p + 1, self.per))
        dve.sem_inc(self.aggregating, 1)
        nc.vector.bn_aggr(self.mean_var[:, p, :], self.moments[:, p, :]).then_inc(self.mean_var_ready, 1)

    def pool_rstd(self, pool, i, p):
        pool.wait_ge(self.mean_var_ready, this(i, p + 1, self.per))
        pool.tensor_tensor(self.var_eps[:, p, :], self.mean_var[:, p, 1:2], self.k.eps[:, :], ALU.add)\
            .then_inc(self.var_eps_ready, 1)
        pool.wait_ge(self.var_eps_ready, this(i, p + 1, self.per))
        pool.wait_ge(self.xn_ready, last(i, p + 1, self.per))
        pool.tensor_tensor(self.rstd[:, p, :], self.var_eps[:, p, :], self.k.minus_half[:, :], ALU.pow)\
            .then_inc(self.rstd_ready, 1)

    def vector_normalise(self, dve, i, p):
        nc = self.k.nc
        dve.wait_ge(self.rstd_ready, this(i, p + 1, self.per))
        if self.final:
            nc.vector.tensor_scalar(self.k.x_tok[:, bass.ds(i * self.per + p, 1), :], self.r[:, p:p + 1, :],
                                    self.mean_var[:, p, 0:1], self.rstd[:, p, :], ALU.subtract, ALU.mult)\
                .then_inc(self.xn_ready, 1)
            return
        if not self.inner:
            dve.wait_ge(self.xnT_ready, last(i, p + 1, self.per))
        dve.wait_ge(self.tok_stored, last(i, p + 1, self.per))
        nc.vector.tensor_scalar(self.xn[:, p, :], self.r[:, p, :], self.mean_var[:, p, 0:1],
                                self.rstd[:, p, :], ALU.subtract, ALU.mult).then_inc(self.xn_ready, 1)

    def vector_inner_moments(self, dve, i, p):
        nc = self.k.nc
        dve.wait_ge(self.xn_ready, this(i, p + 1, self.per))
        nc.vector.bn_stats(self.moments2[:, p, :], self.xn[:, p, :]).then_inc(self.moments2_ready, 1)
        dve.wait_ge(self.moments2_ready, this(i, p + 1, self.per))
        dve.sem_inc(self.aggregating, 1)
        nc.vector.bn_aggr(self.mean_var2[:, p, :], self.moments2[:, p, :]).then_inc(self.mean_var2_ready, 1)

    def pool_inner_rstd(self, pool, i, p):
        pool.wait_ge(self.mean_var2_ready, this(i, p + 1, self.per))
        pool.tensor_tensor(self.var_eps2[:, p, :], self.mean_var2[:, p, 1:2], self.k.eps[:, :], ALU.add)\
            .then_inc(self.var_eps2_ready, 1)
        pool.wait_ge(self.var_eps2_ready, this(i, p + 1, self.per))
        pool.wait_ge(self.xn2_ready, last(i, p + 1, self.per))
        pool.tensor_tensor(self.rstd2[:, p, :], self.var_eps2[:, p, :], self.k.minus_half[:, :], ALU.pow)\
            .then_inc(self.rstd2_ready, 1)

    def vector_inner_normalise(self, dve, i, p):
        nc = self.k.nc
        dve.wait_ge(self.rstd2_ready, this(i, p + 1, self.per))
        dve.wait_ge(self.xnT_ready, last(i, p + 1, self.per))
        nc.vector.tensor_scalar(self.xn2[:, p, :], self.xn[:, p, :], self.mean_var2[:, p, 0:1],
                                self.rstd2[:, p, :], ALU.subtract, ALU.mult).then_inc(self.xn2_ready, 1)

    def pool_store(self, pool, i, p):
        pool.wait_ge(self.xn_ready, this(i, p + 1, self.per))
        pool.sem_inc(self.storing, 1)
        pool.tensor_copy(self.k.x_tok[:, bass.ds(i * self.per + p, 1), :], self.xn[:, p:p + 1, :])\
            .then_inc(self.tok_stored, 1)

    def tensor_transpose(self, pe, i, p, bank):
        pe.wait_ge(self.out_ready, this(i, p + 1, self.per))
        pe.transpose(bank, self.out[:, p, :], self.k.ident[:, :]).then_inc(self.xnT_ready, 1)

    def scalar_store(self, act, i, p, bank):
        k = self.k
        act.wait_ge(self.xnT_ready, this(i, p + 1, self.per))
        if self.router is not None:
            act.wait_ge(self.logits_ready, last(i, self.per, self.per) if p == 0 else this(i, p, self.per))
            k.nc.scalar.activation(self.xnT[:, :], bank, ACT.Copy).then_inc(self.xnT_kept, 1)
        src = bank.rearrange("p (b s) -> p b s", b=2)[:, :, 0:S]
        dst = k.x_feat[:, bass.ds(2 * (i * self.per + p), 2), :]
        if self.inner:
            gain, bias = self.inner
            k.nc.scalar.activation(dst, src, ACT.Identity, bias=bias, scale=gain)\
                .then_inc(self.feat_stored, 1)
        else:
            k.nc.scalar.activation(dst, src, ACT.Copy).then_inc(self.feat_stored, 1)


    def tensor_logits(self, pe, i, p, bank):
        pe.wait_ge(self.xnT_kept, this(i, p + 1, self.per))
        pe.matmul(bank, self.xnT[:, :], self.router[:, :], start=True, stop=True).then_inc(self.logits_ready, 1)

    def vector_logits(self, dve, i, p, bank):
        dve.wait_ge(self.logits_ready, this(i, p + 1, self.per))
        self.k.nc.vector.tensor_copy(self.k.logits[:, bass.ds(i * self.per + p, 1), :],
                                     bank.unsqueeze(1)).then_inc(self.logits_kept, 1)


def self_attention_phase(k):
    nc = k.nc
    HP = H0 // 2
    with ExitStack() as ctx:
        t = Tail(k, ctx, "sa")
        sem = lambda name: k.sem(ctx, "sa_" + name)
        xdup = k.sb(ctx, "sa_xdup", [128, CB, 2, S])
        xres = k.sb(ctx, "sa_xres", [128, CK, D])
        xbo = k.sb(ctx, "sa_xbo", [128, CK, D])
        qs = k.sb(ctx, "sa_qs", [128, CB, SP])
        kf = k.sb(ctx, "sa_kf", [128, CB, S])
        kexp = k.sb(ctx, "sa_kexp", [128, 4, H0, S])
        vexp = k.sb(ctx, "sa_vexp", [2 * S, CB, D])
        sm = k.sb(ctx, "sa_sm", [128, 2, H0, S])
        pr = k.sb(ctx, "sa_pr", [128, 2, H0, S])
        mx = k.sb(ctx, "sa_mx", [128, 2, H0])
        rs = k.sb(ctx, "sa_rs", [128, 2, H0])
        rinv = k.sb(ctx, "sa_rinv", [128, 2, H0])
        prT = k.sb(ctx, "sa_prT", [2 * S, 2, HP, 128])
        on = k.sb(ctx, "sa_on", [128, D])
        oT = k.sb(ctx, "sa_oT", [128, 128])
        psum = ctx.enter_context(nc.psum_tensor("sa_psum", [128, 8, 512], fp32))
        x_loaded, xres_zeroed, qs_zeroed = sem("x_loaded"), sem("xres_zeroed"), sem("qs_zeroed")
        qT_ready, kT_ready, v_ready = sem("qT_ready"), sem("kT_ready"), sem("v_ready")
        q_kept, k_kept, v_kept = sem("q_kept"), sem("k_kept"), sem("v_kept")
        xbo_ready, keys_ready, scores_ready = sem("xbo_ready"), sem("keys_ready"), sem("scores_ready")
        masked, max_ready, shifted = sem("masked"), sem("max_ready"), sem("shifted")
        exp_ready, sum_ready, rinv_ready = sem("exp_ready"), sem("sum_ready"), sem("rinv_ready")
        prT_ready, prT_kept = sem("prT_ready"), sem("prT_kept")
        o_ready, o_kept, oT_ready, oT_kept, y_ready = sem("o_ready"), sem("o_kept"), sem("oT_ready"), sem("oT_kept"), sem("y_ready")
        block = ctx.enter_context(nc.Block())
        n = lambda i, p: this(i, p + 1, CK)
        b = lambda i, p: last(i, p + 1, CK)

        @block.sync
        def _(sp):
            sp.wait_ge(xres_zeroed, 1)
            with sp.Fori(0, CHUNKS) as i:
                sp.wait_ge(q_kept, last(i))
                sp.wait_ge(k_kept, last(i))
                sp.wait_ge(v_kept, last(i, 2, 2))
                sp.wait_ge(xbo_ready, b(i, CK - 1))
                for c in range(2):
                    sp.dma_start(xdup[:, :, c, :], k.dram["xT"][:, bass.ds(i * CB, CB), :]).then_inc(x_loaded, 16)
                for h in range(2):
                    sp.dma_start(xres[h * SP:h * SP + S, :, :], k.dram["x_pairs"][h, :, bass.ds(i * CK, CK), :])\
                        .then_inc(x_loaded, 16)
            sp.wait_ge(k.late_weights_loaded, 16 * len(k.late_loads))

        @block.gpsimd
        def _(pool):
            open_sems(pool, CK, xbo_ready)
            open_sems(pool, CB, keys_ready)
            t.open_pool(pool)
            pool.memset(xres[:, :, :], 0.0).then_inc(xres_zeroed, 1)
            with pool.Fori(0, CHUNKS) as i:
                def expand(b_):
                    if b_ == 0:
                        pool.wait_ge(k_kept, this(i))
                    if b_ % 2 == 0:
                        pool.wait_ge(scores_ready, b(i, b_ // 2 + 2) if b_ < 4 else n(i, b_ // 2 - 2))
                    pool.tensor_tensor(kexp[:, b_ % 4, :, :],
                                       kf[:, b_, :].unsqueeze(1).to_broadcast([128, H0, S]),
                                       k.head_mask[:, :].unsqueeze(2).to_broadcast([128, H0, S]),
                                       ALU.mult).then_inc(keys_ready, 1)

                expand(0)
                expand(1)
                pool.wait_ge(x_loaded, (i + 1) * 64)
                for p in range(CK):
                    pool.wait_ge(t.r_ready, b(i, p))
                    pool.tensor_tensor(xbo[:, p, :], xres[:, p, :], k.bo_row0[:, :], ALU.add).then_inc(xbo_ready, 1)
                for step in range(1, CK + 5):
                    if step < CK:
                        expand(2 * step)
                        expand(2 * step + 1)
                    if 0 <= step - 4 < CK:
                        t.pool_rstd(pool, i, step - 4)
                    if 0 <= step - 5 < CK:
                        t.pool_store(pool, i, step - 5)

        @block.tensor
        def _(pe):
            open_sems(pe, CK, scores_ready, prT_ready, o_ready, oT_ready, y_ready)
            open_sems(pe, 1, qT_ready, kT_ready)
            open_sems(pe, 2, v_ready)
            t.open_tensor(pe)
            with pe.Fori(0, CHUNKS) as i:
                pe.wait_ge(x_loaded, (i + 1) * 64)
                xc = xdup[:, :, 0, :]
                pe.wait_ge(prT_kept, b(i, CK - 1))
                nc.tensor.matmul(psum[:, 4, 0:CT], k.wqT0[:, :], xc, start=True, stop=True).then_inc(qT_ready, 1)
                nc.tensor.matmul(psum[:, 5, 0:CT], k.wkT0[:, :], xc, start=True, stop=True).then_inc(kT_ready, 1)
                pe.wait_ge(o_kept, b(i, CK - 1))
                pe.wait_ge(t.feat_stored, b(i, CK - 1))
                for g in range(2):
                    for j in range(4):
                        done = nc.tensor.matmul(psum[0:2 * S, 6 + g, j * D:(j + 1) * D],
                                                xdup[:, 4 * g + j, :, :], k.wvT0[:, :], start=True, stop=True)
                    done.then_inc(v_ready, 1)
                for step in range(CK + 5):
                    p = step
                    if p < CK:
                        if p == 0:
                            pe.wait_ge(q_kept, this(i))
                        pe.wait_ge(keys_ready, this(i, 2 * p + 2, CB))
                        pe.wait_ge(masked, b(i, p + 2) if p < 2 else n(i, p - 2))
                        for half in range(2):
                            for hh in range(2):
                                done = nc.tensor.matmul(psum[half * SP:(half + 1) * SP, 2 * (p % 2) + hh, 0:CT],
                                                        qs[:, 2 * p + half, :],
                                                        kexp[:, (2 * p + half) % 4, hh * 8:(hh + 1) * 8, :],
                                                        start=True, stop=True)
                        done.then_inc(scores_ready, 1)
                    p = step - 1
                    if 0 <= p < CK:
                        pe.wait_ge(exp_ready, n(i, p))
                        if p == 0:
                            pe.wait_ge(k_kept, this(i))
                        else:
                            pe.wait_ge(prT_kept, n(i, p - 1))
                        for hp in range(HP):
                            done = nc.tensor.transpose(psum[0:2 * S, 4 + hp // 4, (hp % 4) * 128:(hp % 4 + 1) * 128],
                                                       pr[:, p % 2, 2 * hp:2 * hp + 2, :], k.ident[:, :])
                        done.then_inc(prT_ready, 1)
                    p = step - 2
                    if 0 <= p < CK:
                        pe.wait_ge(prT_kept, n(i, p))
                        if p == 0:
                            pe.wait_ge(v_kept, this(i, 2, 2))
                        else:
                            pe.wait_ge(o_kept, n(i, p - 1))
                        for half in range(2):
                            for hp in range(HP):
                                done = nc.tensor.matmul(psum[half * SP:(half + 1) * SP, 6, hp * 16:(hp + 1) * 16],
                                                        prT[:, p % 2, hp, half * SP:(half + 1) * SP],
                                                        vexp[:, 2 * p + half, hp * 16:(hp + 1) * 16],
                                                        start=True, stop=True)
                        done.then_inc(o_ready, 1)
                    p = step - 5
                    if 0 <= p < CK:
                        pe.wait_ge(t.r_ready, n(i, min(p + 1, CK - 1)))
                        if p == CK - 1:
                            pe.wait_ge(t.feat_stored, n(i, p - 1))
                        t.tensor_transpose(pe, i, p, psum[:, 7, 256:384])
                    p = step - 3
                    if 0 <= p < CK:
                        pe.wait_ge(o_kept, n(i, p))
                        if p >= 2:
                            pe.wait_ge(t.feat_stored, n(i, p - 2))
                        elif p == 1:
                            pe.wait_ge(t.r_ready, n(i, 0))
                        nc.tensor.transpose(psum[:, 7, 0:128], on[:, :], k.ident[:, :]).then_inc(oT_ready, 1)
                        pe.wait_ge(oT_kept, n(i, p))
                        nc.tensor.matmul(psum[:, 7, 128:256], oT[:, :], k.woT0[:, :], start=True, stop=True)\
                            .then_inc(y_ready, 1)

        @block.vector
        def _(dve):
            open_sems(dve, CK, masked, max_ready, shifted, sum_ready, rinv_ready, o_kept)
            open_sems(dve, 1, q_kept)
            open_sems(dve, 2, v_kept)
            t.open_vector(dve)
            dve.memset(qs[:, :, :], 0.0).then_inc(qs_zeroed, 1)
            dve.wait_ge(qs_zeroed, 1)
            with dve.Fori(0, CHUNKS) as i:
                dve.wait_ge(qT_ready, this(i))
                nc.vector.tensor_scalar(qs[:, :, 0:S], psum[:, 4, 0:CT].rearrange("p (b s) -> p b s", b=CB),
                                        k.bq0[:, :], DH0 ** -0.5, ALU.add, ALU.mult).then_inc(q_kept, 1)
                for g in range(2):
                    dve.wait_ge(v_ready, this(i, g + 1, 2))
                    if g == 0:
                        dve.wait_ge(o_ready, b(i, CK - 1))
                    nc.vector.tensor_tensor(vexp[:, 4 * g:4 * g + 4, :],
                                            psum[0:2 * S, 6 + g, :].rearrange("p (b d) -> p b d", b=4),
                                            k.value_mask[0:2 * S, :, :, :].rearrange("p a c j -> p (a c j)")
                                            .unsqueeze(1).to_broadcast([2 * S, 4, D]),
                                            ALU.mult).then_inc(v_kept, 1)
                for step in range(CK + 5):
                    p = step - 5
                    if 0 <= p < CK:
                        t.vector_normalise(dve, i, p)
                    p = step
                    if p < CK:
                        dve.wait_ge(scores_ready, n(i, p))
                        dve.wait_ge(exp_ready, b(i, p + 2) if p < 2 else n(i, p - 2))
                        nc.vector.tensor_tensor(sm[:, p % 2, :, :].rearrange("p (a h) s -> p a h s", a=2),
                                                psum[:, 2 * (p % 2):2 * (p % 2) + 2, 0:CT]
                                                .rearrange("p a (h s) -> p a h s", h=8),
                                                k.window_mask[:, :].unsqueeze(1).unsqueeze(1)
                                                .to_broadcast([128, 2, 8, S]), ALU.add).then_inc(masked, 1)
                        dve.wait_ge(masked, n(i, p))
                        nc.vector.reduce_max(mx[:, p % 2, :], sm[:, p % 2, :, :], AX.X).then_inc(max_ready, 1)
                        dve.wait_ge(max_ready, n(i, p))
                        nc.vector.tensor_tensor(sm[:, p % 2, :, :], sm[:, p % 2, :, :],
                                                mx[:, p % 2, :].unsqueeze(2).to_broadcast([128, H0, S]),
                                                ALU.subtract).then_inc(shifted, 1)
                    p = step - 1
                    if 0 <= p < CK:
                        dve.wait_ge(exp_ready, n(i, p))
                        nc.vector.reduce_sum(rs[:, p % 2, :], pr[:, p % 2, :, :], AX.X).then_inc(sum_ready, 1)
                        dve.wait_ge(sum_ready, n(i, p))
                        nc.vector.reciprocal(rinv[:, p % 2, :], rs[:, p % 2, :]).then_inc(rinv_ready, 1)
                    p = step - 2
                    if 0 <= p < CK:
                        dve.wait_ge(rinv_ready, n(i, p))
                        dve.wait_ge(o_ready, n(i, p))
                        dve.wait_ge(oT_ready, b(i, CK - 1) if p == 0 else n(i, p - 1))
                        nc.vector.tensor_tensor(on[:, :].rearrange("p (h d) -> p h d", h=H0),
                                                psum[:, 6, 0:128].rearrange("p (h d) -> p h d", h=H0),
                                                rinv[:, p % 2, :].unsqueeze(2).to_broadcast([128, H0, DH0]),
                                                ALU.mult).then_inc(o_kept, 1)
                    p = step - 3
                    if 0 <= p < CK:
                        dve.wait_ge(y_ready, n(i, p))
                        dve.wait_ge(xbo_ready, n(i, p))
                        nc.vector.tensor_tensor(t.r[:, p, :], psum[:, 7, 128:256], xbo[:, p, :], ALU.add)\
                            .then_inc(t.r_ready, 1)
                        t.vector_moments(dve, i, p)

        @block.scalar
        def _(act):
            open_sems(act, CK, exp_ready, prT_kept, oT_kept)
            open_sems(act, 1, k_kept)
            t.open_scalar(act)
            with act.Fori(0, CHUNKS) as i:
                act.wait_ge(kT_ready, this(i))
                act.wait_ge(keys_ready, last(i, CB, CB))
                nc.scalar.activation(kf[:, :, :], psum[:, 5, 0:CT].rearrange("p (b s) -> p b s", b=CB),
                                     ACT.Identity, bias=k.bk0[:, :]).then_inc(k_kept, 1)
                for step in range(CK + 5):
                    p = step
                    if p < CK:
                        act.wait_ge(shifted, n(i, p))
                        act.wait_ge(prT_ready, b(i, p + 2) if p < 2 else n(i, p - 2))
                        act.wait_ge(sum_ready, b(i, p + 2) if p < 2 else n(i, p - 2))
                        nc.scalar.activation(pr[:, p % 2, :, :], sm[:, p % 2, :, :], ACT.Exp).then_inc(exp_ready, 1)
                    p = step - 1
                    if 0 <= p < CK:
                        act.wait_ge(prT_ready, n(i, p))
                        act.wait_ge(o_ready, b(i, p + 2) if p < 2 else n(i, p - 2))
                        nc.scalar.activation(prT[:, p % 2, :, :].rearrange("p (a h) s -> p a (h s)", a=2),
                                             psum[0:2 * S, 4:6, :], ACT.Copy).then_inc(prT_kept, 1)
                    p = step - 5
                    if 0 <= p < CK:
                        t.scalar_store(act, i, p, psum[:, 7, 256:384])
                    p = step - 3
                    if 0 <= p < CK:
                        act.wait_ge(oT_ready, n(i, p))
                        act.wait_ge(y_ready, b(i, CK - 1) if p == 0 else n(i, p - 1))
                        nc.scalar.activation(oT[:, :], psum[:, 7, 0:128], ACT.Identity, bias=k.bv0[:, :])\
                            .then_inc(oT_kept, 1)


def context_attention_phase(k):
    nc = k.nc
    Q4 = C // 4
    with ExitStack() as ctx:
        t = Tail(k, ctx, "ca", router=k.router0)
        sem = lambda name: k.sem(ctx, "ca_" + name)
        qp = k.sb(ctx, "ca_qp", [128, CT])
        qk = k.sb(ctx, "ca_qk", [128, CB, SP])
        ctxT = k.sb(ctx, "ca_ctxT", [128, 2, 2, C])
        ctxN = k.sb(ctx, "ca_ctxN", [KP, 2, 2, KT * D])
        pr = k.sb(ctx, "ca_pr", [128, 2, C])
        prT = k.sb(ctx, "ca_prT", [KP, 2, KT, 128])
        negmax = k.sb(ctx, "ca_negmax", [128, 2, 1])
        rs = k.sb(ctx, "ca_rs", [128, 2, 1])
        rinv = k.sb(ctx, "ca_rinv", [128, CK, 1])
        xb = k.sb(ctx, "ca_xb", [128, CK, D])
        oT = k.sb(ctx, "ca_oT", [128, 2, 128])
        vT = k.sb(ctx, "ca_vT", [128, 2, 128])
        psum = ctx.enter_context(nc.psum_tensor("ca_psum", [128, 8, 512], fp32))
        ctxT_loaded = [sem("ctxT_loaded0"), sem("ctxT_loaded1")]
        ctxN_loaded = [sem("ctxN_loaded0"), sem("ctxN_loaded1")]
        qk_zeroed, qp_ready, qp_kept, qk_ready, qk_kept = sem("qk_zeroed"), sem("qp_ready"), sem("qp_kept"), sem("qk_ready"), sem("qk_kept")
        scores_ready, max_ready, exp_ready, rinv_ready = sem("scores_ready"), sem("max_ready"), sem("exp_ready"), sem("rinv_ready")
        prT_ready, even_kept, odd_kept = sem("prT_ready"), sem("even_kept"), sem("odd_kept")
        pv_ready, oT_kept, vT_ready, vT_kept, y_ready, xb_ready = (
            sem("pv_ready"), sem("oT_kept"), sem("vT_ready"), sem("vT_kept"), sem("y_ready"), sem("xb_ready"))
        block = ctx.enter_context(nc.Block())
        n = lambda i, p: this(i, p + 1, CK)
        b = lambda i, p: last(i, p + 1, CK)
        before = lambda i, p, back: n(i, p - back) if p >= back else b(i, p + CK - back)
        STEPS = CK + 4

        @block.sync
        def _(sp):
            with sp.Fori(0, CHUNKS) as i:
                for p in range(CK):
                    sp.wait_ge(scores_ready, before(i, p, 2))
                    sp.dma_start(ctxT[:, p % 2, :, :],
                                 k.dram["ctxT"][bass.ds(i * CB + 2 * p, 2), :, :].rearrange("b d c -> d b c"))\
                        .then_inc(ctxT_loaded[p % 2], 16)
                    sp.wait_ge(pv_ready, before(i, p, 2))
                    sp.dma_start(ctxN[:, p % 2, :, :],
                                 k.dram["ctxN"][bass.ds(i * CB + 2 * p, 2), :, :, :].rearrange("b q t d -> q b (t d)"))\
                        .then_inc(ctxN_loaded[p % 2], 16)

        @block.gpsimd
        def _(pool):
            open_sems(pool, CK, xb_ready)
            t.open_pool(pool)
            with pool.Fori(0, CHUNKS) as i:
                for step in range(STEPS + 1):
                    if step < CK:
                        pool.wait_ge(t.r_ready, b(i, step))
                        pool.tensor_tensor(xb[:, step:step + 1, :], k.x_tok[:, bass.ds(i * CK + step, 1), :],
                                           k.cross_row[:, :].unsqueeze(1), ALU.add).then_inc(xb_ready, 1)
                    if 0 <= step - 3 < CK:
                        t.pool_rstd(pool, i, step - 3)
                    if 0 <= step - 4 < CK:
                        t.pool_store(pool, i, step - 4)

        @block.tensor
        def _(pe):
            open_sems(pe, 1, qp_ready, qk_ready)
            open_sems(pe, CK, scores_ready, pv_ready, vT_ready, y_ready)
            open_sems(pe, 3 * CK, prT_ready)
            t.open_tensor(pe)
            with pe.Fori(0, CHUNKS) as i:
                pe.wait_ge(t.logits_kept, b(i, CK - 1))
                pe.wait_ge(t.feat_stored, b(i, CK - 1))
                nc.tensor.matmul(psum[:, 7, 0:CT], k.wqT0x[:, :], k.x_feat[:, bass.ds(i * CB, CB), :],
                                 start=True, stop=True).then_inc(qp_ready, 1)
                pe.wait_ge(qp_kept, this(i))
                pe.wait_ge(oT_kept, b(i, CK - 1))
                nc.tensor.matmul(psum[:, 6, 0:CT], k.wk0x[:, :], qp[:, :], start=True, stop=True).then_inc(qk_ready, 1)

                def transposes(p, r):
                    for j in range(4):
                        kt = 4 * r + j
                        done = nc.tensor.transpose(psum[0:KP, 4 + r % 2, j * 128:(j + 1) * 128],
                                                   pr[:, p % 2, kt * KP:(kt + 1) * KP], k.ident[:, :])
                    done.then_inc(prT_ready, 1)

                for step in range(STEPS + 1):
                    p = step - 3
                    if 0 <= p < CK:
                        pe.wait_ge(oT_kept, n(i, p))
                        if p >= 2:
                            pe.wait_ge(t.logits_kept, n(i, p - 2))
                        elif p == 1:
                            pe.wait_ge(t.r_ready, n(i, 0))
                        nc.tensor.matmul(psum[:, 7, 0:128], k.wvT0x[:, :], oT[:, p % 2, :], start=True, stop=True)\
                            .then_inc(vT_ready, 1)
                    p = step
                    if p < CK:
                        if p == 0:
                            pe.wait_ge(qk_kept, this(i))
                        pe.wait_ge(ctxT_loaded[p % 2], (i * 2 + p // 2 + 1) * 16)
                        pe.wait_ge(exp_ready, before(i, p, 1))
                        for half in range(2):
                            for j in range(4):
                                done = nc.tensor.matmul(psum[half * SP:(half + 1) * SP, j, 0:Q4], qk[:, 2 * p + half, :],
                                                        ctxT[:, p % 2, half, j * Q4:(j + 1) * Q4], start=True, stop=True)
                        done.then_inc(scores_ready, 1)
                    p = step - 4
                    if 0 <= p < CK:
                        if p + 1 < CK:
                            pe.wait_ge(vT_kept, n(i, p + 1))
                        else:
                            pe.wait_ge(t.logits_kept, n(i, p - 1))
                        t.tensor_transpose(pe, i, p, psum[:, 7, 256:384])
                    p = step - 1
                    if 0 <= p < CK:
                        pe.wait_ge(exp_ready, n(i, p))
                        pe.wait_ge(even_kept, this(i, 2 * p, 2 * CK) if p else last(i, 2 * CK, 2 * CK))
                        transposes(p, 0)
                        pe.wait_ge(odd_kept, before(i, p, 1))
                        transposes(p, 1)
                    p = step - 3
                    if 0 <= p < CK:
                        pe.wait_ge(vT_kept, n(i, p))
                        if p >= 1:
                            pe.wait_ge(t.feat_stored, n(i, p - 1))
                        nc.tensor.matmul(psum[:, 7, 128:256], vT[:, p % 2, :], k.woT0x[:, :], start=True, stop=True)\
                            .then_inc(y_ready, 1)
                    p = step - 2
                    if 0 <= p < CK:
                        pe.wait_ge(ctxN_loaded[p % 2], (i * 2 + p // 2 + 1) * 16)
                        pe.wait_ge(even_kept, this(i, 2 * p + 2, 2 * CK))
                        pe.wait_ge(odd_kept, n(i, p))
                        if p:
                            pe.wait_ge(oT_kept, n(i, p - 1))
                        for half in range(2):
                            for kt in range(KT):
                                done = nc.tensor.matmul(psum[:, 6, half * SP:(half + 1) * SP],
                                                        ctxN[:, p % 2, half, kt * D:(kt + 1) * D],
                                                        prT[:, p % 2, kt, half * SP:(half + 1) * SP],
                                                        start=(kt == 0), stop=(kt == KT - 1))
                        done.then_inc(pv_ready, 1)
                    p = step - 4
                    if 0 <= p < CK:
                        if p + 1 < CK:
                            pe.wait_ge(t.r_ready, n(i, p + 1))
                        pe.wait_ge(t.feat_stored, n(i, p))
                        t.tensor_logits(pe, i, p, psum[:, 7, 384:384 + E])
                    p = step - 1
                    if 0 <= p < CK:
                        pe.wait_ge(even_kept, this(i, 2 * p + 1, 2 * CK))
                        transposes(p, 2)

        @block.vector
        def _(dve):
            open_sems(dve, CK, max_ready, rinv_ready, vT_kept)
            open_sems(dve, 2 * CK, even_kept)
            open_sems(dve, 1, qp_kept, qk_kept)
            t.open_vector(dve)
            dve.memset(qk[:, :, :], 0.0).then_inc(qk_zeroed, 1)
            dve.wait_ge(qk_zeroed, 1)
            with dve.Fori(0, CHUNKS) as i:
                dve.wait_ge(qp_ready, this(i))
                nc.vector.tensor_scalar(qp[:, :], psum[:, 7, 0:CT], k.bq0x[:, :], D ** -0.5, ALU.add, ALU.mult)\
                    .then_inc(qp_kept, 1)
                dve.wait_ge(qk_ready, this(i))
                nc.vector.tensor_copy(qk[:, :, 0:S], psum[:, 6, 0:CT].rearrange("p (b s) -> p b s", b=CB))\
                    .then_inc(qk_kept, 1)
                for step in range(STEPS + 1):
                    p = step - 3
                    if 0 <= p < CK:
                        dve.wait_ge(vT_ready, n(i, p))
                        dve.wait_ge(y_ready, before(i, p, 2))
                        nc.vector.tensor_copy(vT[:, p % 2, :], psum[:, 7, 0:128]).then_inc(vT_kept, 1)
                    p = step - 4
                    if 0 <= p < CK:
                        t.vector_normalise(dve, i, p)
                    p = step
                    if p < CK:
                        dve.wait_ge(scores_ready, n(i, p))
                        nc.vector.tensor_reduce(negmax[:, p % 2, :], psum[:, 0:4, 0:Q4], AX.XY, ALU.max, negate=True)\
                            .then_inc(max_ready, 1)
                    p = step - 1
                    if 0 <= p < CK:
                        dve.wait_ge(exp_ready, n(i, p))
                        nc.vector.reciprocal(rinv[:, p, :], rs[:, p % 2, :]).then_inc(rinv_ready, 1)
                        dve.wait_ge(prT_ready, this(i, 3 * p + 1, 3 * CK))
                        dve.wait_ge(pv_ready, before(i, p, 2))
                        nc.vector.tensor_copy(prT[:, p % 2, 0:4, :].rearrange("p a b -> p (a b)"), psum[0:KP, 4, :])\
                            .then_inc(even_kept, 1)
                    p = step - 3
                    if 0 <= p < CK:
                        dve.wait_ge(y_ready, n(i, p))
                        dve.wait_ge(xb_ready, n(i, p))
                        nc.vector.scalar_tensor_tensor(t.r[:, p, :], psum[:, 7, 128:256], rinv[:, p, :], xb[:, p, :],
                                                       ALU.mult, ALU.add).then_inc(t.r_ready, 1)
                        t.vector_moments(dve, i, p)
                    p = step - 4
                    if 0 <= p < CK:
                        t.vector_logits(dve, i, p, psum[:, 7, 384:384 + E])
                    p = step - 1
                    if 0 <= p < CK:
                        dve.wait_ge(prT_ready, this(i, 3 * p + 3, 3 * CK))
                        nc.vector.tensor_copy(prT[:, p % 2, 8:12, :].rearrange("p a b -> p (a b)"), psum[0:KP, 4, :])\
                            .then_inc(even_kept, 1)

        @block.scalar
        def _(act):
            open_sems(act, CK, exp_ready, odd_kept, oT_kept)
            t.open_scalar(act)
            with act.Fori(0, CHUNKS) as i:
                for step in range(STEPS + 1):
                    p = step - 4
                    if 0 <= p < CK:
                        t.scalar_store(act, i, p, psum[:, 7, 256:384])
                    p = step
                    if p < CK:
                        act.wait_ge(max_ready, n(i, p))
                        act.wait_ge(prT_ready, this(i, 3 * (p - 1), 3 * CK) if p >= 2 else last(i, 3 * (p + 3), 3 * CK))
                        act.wait_ge(rinv_ready, before(i, p, 2))
                        nc.scalar.activation(pr[:, p % 2, :].rearrange("p (a c) -> p a c", a=4), psum[:, 0:4, 0:Q4],
                                             ACT.Exp, bias=negmax[:, p % 2, :], accum_out=rs[:, p % 2, :])\
                            .then_inc(exp_ready, 1)
                    p = step - 1
                    if 0 <= p < CK:
                        act.wait_ge(prT_ready, this(i, 3 * p + 2, 3 * CK))
                        act.wait_ge(pv_ready, before(i, p, 2))
                        nc.scalar.activation(prT[:, p % 2, 4:8, :].rearrange("p a b -> p (a b)"), psum[0:KP, 5, :],
                                             ACT.Copy).then_inc(odd_kept, 1)
                    p = step - 2
                    if 0 <= p < CK:
                        act.wait_ge(pv_ready, n(i, p))
                        act.wait_ge(vT_ready, before(i, p, 2))
                        nc.scalar.activation(oT[:, p % 2, :], psum[:, 6, 0:128], ACT.Copy).then_inc(oT_kept, 1)


def routing_phase(k, layer):
    nc = k.nc
    with ExitStack() as ctx:
        sem = lambda name: k.sem(ctx, f"route{layer}_{name}")
        sb = lambda name, shape, dt=fp32: k.sb(ctx, f"route{layer}_{name}", shape, dt)
        best = sb("best", [128, PAIRS, 8])
        index_u = sb("index_u", [128, PAIRS, 8], u32)
        index = sb("index", [128, PAIRS, 2])
        gap, e2, total, inv, w2 = (sb(x, [128, PAIRS, 1]) for x in ("gap", "e2", "total", "inv", "w2"))
        hot = sb("hot", [128, PAIRS, E])
        first = sb("first", [128, PAIRS, E])
        biased = sb("biased", [128, PAIRS, E])
        step_done, exp_ready, biased_ready, gap_ready = sem("step_done"), sem("exp_ready"), sem("biased_ready"), sem("gap_ready")
        block = ctx.enter_context(nc.Block())
        wide = lambda v: v.to_broadcast([128, PAIRS, E])
        experts = k.expert_index[:, :].unsqueeze(1).to_broadcast([128, PAIRS, E])

        @block.vector
        def _(dve):
            n = 0

            def step(instruction):
                nonlocal n
                n += 1
                instruction.then_inc(step_done, 1)
                dve.wait_ge(step_done, n)

            values = k.logits
            if layer == 1:
                nc.vector.tensor_tensor(biased[:, :, :], k.logits[:, :, :],
                                        k.router_bias_row1[:, :].unsqueeze(1).to_broadcast([128, PAIRS, E]),
                                        ALU.add).then_inc(biased_ready, 1)
                dve.wait_ge(exp_ready, 1)
                values = first
            for g in range(PAIRS):
                last_max = nc.vector.max(best[:, g, :], values[:, g, :])
            step(last_max)
            for g in range(PAIRS):
                last_index = nc.vector.max_index(index_u[:, g, :], best[:, g, :], values[:, g, :])
            step(last_index)
            step(nc.vector.tensor_copy(index[:, :, :], index_u[:, :, 0:2]))
            if layer == 0:
                nc.vector.tensor_tensor(gap[:, :, :], best[:, :, 1:2], best[:, :, 0:1], ALU.subtract).then_inc(gap_ready, 1)
                dve.wait_ge(exp_ready, 1)
                step(nc.vector.tensor_scalar(total[:, :, :], e2[:, :, :], 1.0, None, ALU.add))
                step(nc.vector.reciprocal(inv[:, :, :], total[:, :, :]))
                w1 = inv
                step(nc.vector.tensor_tensor(w2[:, :, :], e2[:, :, :], inv[:, :, :], ALU.mult))
            else:
                step(nc.vector.tensor_tensor(total[:, :, :], best[:, :, 1:2], best[:, :, 0:1], ALU.add))
                step(nc.vector.reciprocal(inv[:, :, :], total[:, :, :]))
                w1 = gap
                step(nc.vector.tensor_tensor(gap[:, :, :], best[:, :, 0:1], inv[:, :, :], ALU.mult))
                step(nc.vector.tensor_tensor(w2[:, :, :], best[:, :, 1:2], inv[:, :, :], ALU.mult))
            step(nc.vector.tensor_tensor(hot[:, :, :], experts, wide(index[:, :, 0:1]), ALU.is_equal))
            step(nc.vector.tensor_tensor(biased[:, :, :], hot[:, :, :], wide(w1[:, :, :]), ALU.mult))
            step(nc.vector.tensor_tensor(hot[:, :, :], experts, wide(index[:, :, 1:2]), ALU.is_equal))
            step(nc.vector.tensor_tensor(first[:, :, :], hot[:, :, :], wide(w2[:, :, :]), ALU.mult))
            step(nc.vector.tensor_tensor(k.expert_weights[:, :, :], biased[:, :, :], first[:, :, :], ALU.add))

        @block.scalar
        def _(act):
            if layer == 1:
                act.wait_ge(biased_ready, 1)
                nc.scalar.activation(first[:, :, :], biased[:, :, :], ACT.Sigmoid).then_inc(exp_ready, 1)
            else:
                act.wait_ge(gap_ready, 1)
                nc.scalar.activation(e2[:, :, :], gap[:, :, :], ACT.Exp).then_inc(exp_ready, 1)


def expert_phase(k, layer):
    nc = k.nc
    HT = (U0 if layer == 0 else I1) // 128
    NE = E if layer == 0 else E + 1
    down = k.down0 if layer == 0 else k.down1
    with ExitStack() as ctx:
        tag = f"moe{layer}"
        inner = (k.ln_g1[:, :], k.ln_b1[:, :]) if layer == 0 else None
        final = layer == 1
        t = Tail(k, ctx, tag, inner=inner, final=final)
        sem = lambda name: k.sem(ctx, f"{tag}_{name}")
        sb = lambda name, shape, dt=fp32: k.sb(ctx, f"{tag}_{name}", shape, dt)
        xc = sb("xc", [128, CT])
        wc = sb("wc", [128, CK, E])
        spread = sb("spread", [128, E, CT])
        hid = sb("hid", [128, 2, HT, CT])
        act_out = sb("act_out", [128, 2, CT])
        part = sb("part", [128, 2, CT])
        acc = sb("acc", [128, CB, SP])
        psum = ctx.enter_context(nc.psum_tensor(f"{tag}_psum", [128, 8, 512], fp32))
        acc_zeroed, xc_ready, wc_ready, spread_ready, spread_kept = (
            sem("acc_zeroed"), sem("xc_ready"), sem("wc_ready"), sem("spread_ready"), sem("spread_kept"))
        up_ready, hid_ready, silu_ready, down_ready, part_ready, acc_ready, y_ready = (
            sem("up_ready"), sem("hid_ready"), sem("silu_ready"), sem("down_ready"), sem("part_ready"),
            sem("acc_ready"), sem("y_ready"))
        out_stored = sem("out_stored")
        block = ctx.enter_context(nc.Block())
        n = lambda i, p: this(i, p + 1, CK)
        b = lambda i, p: last(i, p + 1, CK)
        NT = NE * HT

        def slot(i, e):
            if e >= 2:
                return this(i, e - 1, NE)
            return last(i, NE if (NE - 1) % 2 == e else NE - 1, NE)

        def hid_tile(i, j, back=0):
            return this(i, j + 1 - back, NT) if j >= back else last(i, NT + j + 1 - back, NT)

        @block.gpsimd
        def _(pool):
            open_sems(pool, 1, xc_ready, wc_ready)
            open_sems(pool, NE - 1, acc_ready)
            t.open_pool(pool)
            pool.memset(acc[:, :, :], 0.0).then_inc(acc_zeroed, 1)
            with pool.Fori(0, CHUNKS) as i:
                pool.wait_ge(up_ready, last(i, NT, NT))
                pool.tensor_copy(xc[:, :].rearrange("p (b s) -> p b s", b=CB), k.x_feat[:, bass.ds(i * CB, CB), :])\
                    .then_inc(xc_ready, 1)
                pool.wait_ge(spread_ready, last(i, E, E))
                pool.tensor_copy(wc[:, :, :], k.expert_weights[:, bass.ds(i * CK, CK), :]).then_inc(wc_ready, 1)
                total = acc[:, :, 0:S]
                for e in range(1, NE):
                    pool.wait_ge(part_ready, this(i, e + 1, NE))
                    if e > 1:
                        pool.wait_ge(acc_ready, this(i, e - 1, NE - 1))
                    pool.tensor_tensor(total, total, part[:, e % 2, :].rearrange("p (b s) -> p b s", b=CB), ALU.add)\
                        .then_inc(acc_ready, 1)
                for p in range(CK):
                    t.pool_rstd(pool, i, p)
                if inner:
                    for p in range(CK):
                        t.pool_inner_rstd(pool, i, p)
                if not final:
                    for p in range(CK):
                        t.pool_store(pool, i, p)

        @block.sync
        def _(sp):
            if not final:
                return
            with sp.Fori(0, CHUNKS) as i:
                sp.wait_ge(t.xn_ready, n(i, CK - 1))
                for h in range(2):
                    sp.dma_start(k.out[bass.ds(i * CB, CB), :, :].rearrange("(g h) s d -> h s g d", h=2)[h],
                                 k.x_tok[h * SP:h * SP + S, bass.ds(i * CK, CK), :]).then_inc(out_stored, 16)
            sp.wait_ge(out_stored, CHUNKS * 2 * 16)

        @block.tensor
        def _(pe):
            open_sems(pe, E, spread_ready)
            open_sems(pe, NT * (1 if layer == 0 else 2), up_ready)
            open_sems(pe, NE, down_ready)
            open_sems(pe, CK, y_ready)
            t.open_tensor(pe)
            with pe.Fori(0, CHUNKS) as i:
                def spread_weights(e):
                    if e >= 2:
                        pe.wait_ge(spread_kept, this(i, e - 1, E))
                    for p in range(CK):
                        done = nc.tensor.transpose(psum[:, 6 + e % 2, p * 128:(p + 1) * 128],
                                                   wc[:, p, e:e + 1].to_broadcast([128, 128]), k.ident[:, :])
                    done.then_inc(spread_ready, 1)

                def hidden(e):
                    for j in range(HT):
                        u = e * HT + j
                        if layer == 0:
                            pe.wait_ge(hid_ready, hid_tile(i, u, 4))
                            nc.tensor.matmul(psum[:, u % 4, 0:CT], k.up0[:, e, j * 128:(j + 1) * 128], xc[:, :],
                                             start=True, stop=True).then_inc(up_ready, 1)
                        else:
                            pe.wait_ge(hid_ready, hid_tile(i, u, 2))
                            for c, w in enumerate((k.gate1, k.up1)):
                                nc.tensor.matmul(psum[:, 2 * c + u % 2, 0:CT], w[:, e, j * 128:(j + 1) * 128], xc[:, :],
                                                 start=True, stop=True).then_inc(up_ready, 1)

                def project(e):
                    pe.wait_ge(part_ready, slot(i, e))
                    for j in range(HT):
                        pe.wait_ge(hid_ready, this(i, e * HT + j + 1, NT))
                        done = nc.tensor.matmul(psum[:, 4 + e % 2, 0:CT], down[:, e, j, :],
                                                hid[:, e % 2, j, :], start=(j == 0), stop=(j == HT - 1))
                    done.then_inc(down_ready, 1)

                pe.wait_ge(xc_ready, this(i))
                hidden(0)
                pe.wait_ge(wc_ready, this(i))
                if not final:
                    pe.wait_ge(t.feat_stored, b(i, CK - 1))
                pe.wait_ge(t.r_ready, b(i, CK - 1))
                spread_weights(0)
                spread_weights(1)
                for e in range(1, NE):
                    hidden(e)
                    if e + 1 < E:
                        spread_weights(e + 1)
                    project(e - 1)
                project(NE - 1)
                for p in range(CK):
                    if p == 0:
                        pe.wait_ge(acc_ready, this(i, NE - 1, NE - 1))
                        pe.wait_ge(spread_kept, this(i, E, E))
                    else:
                        pe.wait_ge(t.r_ready, n(i, p - 1))
                    nc.tensor.transpose(psum[:, 6, 0:128], acc[:, 2 * p:2 * p + 2, :], k.ident[:, :]).then_inc(y_ready, 1)
                for p in range(0 if final else CK):
                    if p:
                        pe.wait_ge(t.feat_stored, n(i, p - 1))
                    t.tensor_transpose(pe, i, p, psum[:, 7, 0:128])

        @block.vector
        def _(dve):
            open_sems(dve, NE, part_ready)
            if layer == 0:
                open_sems(dve, E, spread_kept)
            else:
                open_sems(dve, E, spread_kept)
                open_sems(dve, NT, hid_ready)
            t.open_vector(dve)
            with dve.Fori(0, CHUNKS) as i:
                def keep_spread(e):
                    dve.wait_ge(spread_ready, this(i, e + 1, E))
                    nc.vector.tensor_copy(spread[:, e, :].rearrange("p (b s) -> p b s", b=CB),
                                          psum[:, 6 + e % 2, :].rearrange("p (b s) -> p b s", b=CB)[:, :, 0:S])\
                        .then_inc(spread_kept, 1)

                def gated(e):
                    for j in range(HT):
                        u = e * HT + j
                        dve.wait_ge(silu_ready, this(i, u + 1, NT))
                        dve.wait_ge(up_ready, this(i, 2 * u + 2, 2 * NT))
                        if j == 0:
                            dve.wait_ge(down_ready, slot(i, e))
                        nc.vector.tensor_tensor(hid[:, e % 2, j, :], act_out[:, u % 2, :], psum[:, 2 + u % 2, 0:CT],
                                                ALU.mult).then_inc(hid_ready, 1)

                def weigh(e):
                    dve.wait_ge(down_ready, this(i, e + 1, NE))
                    src = psum[:, 4 + e % 2, 0:CT]
                    if e == 0:
                        dve.wait_ge(y_ready, b(i, CK - 1))
                        dve.wait_ge(spread_kept, this(i, 1, E))
                        split = lambda v: v.rearrange("p (b s) -> p b s", b=CB)
                        if layer == 0:
                            nc.vector.scalar_tensor_tensor(acc[:, :, 0:S], split(src), k.down_bias0[:, 0:1],
                                                           split(spread[:, 0, :]), ALU.add, ALU.mult)\
                                .then_inc(part_ready, 1)
                        else:
                            nc.vector.tensor_tensor(acc[:, :, 0:S], split(src), split(spread[:, 0, :]), ALU.mult)\
                                .then_inc(part_ready, 1)
                        return
                    dve.wait_ge(acc_ready, this(i, e - 2, NE - 1) if e > 2 else last(i, NE - 1, NE - 1))
                    if layer == 0:
                        dve.wait_ge(spread_kept, this(i, e + 1, E))
                        nc.vector.scalar_tensor_tensor(part[:, e % 2, :], src, k.down_bias0[:, e:e + 1],
                                                       spread[:, e, :], ALU.add, ALU.mult).then_inc(part_ready, 1)
                    elif e < E:
                        dve.wait_ge(spread_kept, this(i, e + 1, E))
                        nc.vector.tensor_tensor(part[:, e % 2, :], src, spread[:, e, :], ALU.mult).then_inc(part_ready, 1)
                    else:
                        nc.vector.tensor_copy(part[:, e % 2, :], src).then_inc(part_ready, 1)

                if layer == 1:
                    gated(0)
                keep_spread(0)
                keep_spread(1)
                for e in range(1, NE):
                    if layer == 1:
                        gated(e)
                    if e + 1 < E:
                        keep_spread(e + 1)
                    weigh(e - 1)
                weigh(NE - 1)
                for p in range(CK):
                    dve.wait_ge(y_ready, n(i, p))
                    nc.vector.tensor_tensor(t.r[:, p:p + 1, :], psum[:, 6, 0:128].unsqueeze(1),
                                            k.x_tok[:, bass.ds(i * CK + p, 1), :], ALU.add).then_inc(t.r_ready, 1)
                    t.vector_moments(dve, i, p)
                for p in range(CK):
                    t.vector_normalise(dve, i, p)
                if inner:
                    for p in range(CK):
                        t.vector_inner_moments(dve, i, p)
                    for p in range(CK):
                        t.vector_inner_normalise(dve, i, p)

        @block.scalar
        def _(act):
            if layer == 0:
                open_sems(act, NT, hid_ready)
            else:
                open_sems(act, NT, silu_ready)
            t.open_scalar(act)
            with act.Fori(0, CHUNKS) as i:
                for e in range(NE):
                    for j in range(HT):
                        u = e * HT + j
                        if layer == 0:
                            act.wait_ge(up_ready, this(i, u + 1, NT))
                            if j == 0:
                                act.wait_ge(down_ready, slot(i, e))
                            nc.scalar.activation(hid[:, e % 2, j, :], psum[:, u % 4, 0:CT], ACT.Gelu,
                                                 bias=k.up_bias0[:, e, j:j + 1]).then_inc(hid_ready, 1)
                        else:
                            act.wait_ge(up_ready, this(i, 2 * u + 1, 2 * NT))
                            act.wait_ge(hid_ready, hid_tile(i, u, 2))
                            nc.scalar.activation(act_out[:, u % 2, :], psum[:, u % 2, 0:CT], ACT.Silu)\
                                .then_inc(silu_ready, 1)
                for p in range(0 if final else CK):
                    t.scalar_store(act, i, p, psum[:, 7, 0:128])


def expert_phase0(k):
    routing_phase(k, 0)
    k.clear_semaphores()
    expert_phase(k, 0)


def expert_phase1(k):
    routing_phase(k, 1)
    k.clear_semaphores()
    expert_phase(k, 1)


def state_space_phase(k):
    nc = k.nc
    N1 = 32
    with ExitStack() as ctx:
        t = Tail(k, ctx, "ss", inner=(k.gamma1[:, :], k.beta1[:, :]))
        sem = lambda name: k.sem(ctx, "ss_" + name)
        sb = lambda name, shape: k.sb(ctx, "ss_" + name, shape)
        hp = sb("hp", [128, CB, S + 2])
        tap0, tap1, mixed = sb("tap0", [128, CT]), sb("tap1", [128, CT]), sb("mixed", [128, CT])
        u, g = sb("u", [128, CT]), sb("g", [128, CT])
        xs, decay, sel = sb("xs", [N1, CT]), sb("decay", [N1, CT]), sb("sel", [N1, CT])
        keep, drive, states, chosen = sb("keep", [N1, CT]), sb("drive", [N1, CT]), sb("states", [N1, CT]), sb("chosen", [N1, CT])
        diff, gdiff = sb("diff", [128, CT]), sb("gdiff", [128, CT])
        z = sb("z", [128, CB, SP])
        xb, xb2 = sb("xb", [128, CK, D]), sb("xb2", [128, CK, D])
        psum = ctx.enter_context(nc.psum_tensor("ss_psum", [128, 8, 512], fp32))
        zeroed, h_ready, xb_ready, xb2_ready = sem("zeroed"), sem("h_ready"), sem("xb_ready"), sem("xb2_ready")
        step_done, proj_ready, act_ready = sem("step_done"), sem("proj_ready"), sem("act_ready")
        state_out_ready, out_ready = sem("state_out_ready"), sem("out_ready")
        block = ctx.enter_context(nc.Block())
        n = lambda i, p: this(i, p + 1, CK)
        b = lambda i, p: last(i, p + 1, CK)
        TAP0, TAP1, MIXED, ONE_MINUS, DRIVE, RESET, STATES, CHOSEN, DIFF, GDIFF, Z = range(1, 12)
        NV = Z
        XS, DECAY, SEL, U, G = range(5)

        @block.gpsimd
        def _(pool):
            open_sems(pool, 1, h_ready)
            open_sems(pool, CK, xb_ready, xb2_ready)
            t.open_pool(pool)
            pool.memset(hp[:, :, :], 0.0).then_inc(zeroed, 1)
            pool.memset(z[:, :, :], 0.0).then_inc(zeroed, 1)
            pool.wait_ge(zeroed, 2)
            with pool.Fori(0, CHUNKS) as i:
                pool.wait_ge(step_done, last(i, MIXED, NV))
                pool.tensor_copy(hp[:, :, 1:S + 1], k.x_feat[:, bass.ds(i * CB, CB), :]).then_inc(h_ready, 1)
                for p in range(CK):
                    pool.tensor_tensor(xb[:, p:p + 1, :], k.x_tok[:, bass.ds(i * CK + p, 1), :],
                                       k.bout_row1[:, :].unsqueeze(1), ALU.add).then_inc(xb_ready, 1)
                for p in range(CK):
                    pool.wait_ge(xb_ready, n(i, p))
                    pool.wait_ge(t.r_ready, b(i, p))
                    pool.sem_inc(t.storing, 1)
                    pool.tensor_tensor(xb2[:, p:p + 1, :], xb[:, p:p + 1, :], k.x_tok[:, bass.ds(i * CK + p, 1), :],
                                       ALU.add).then_inc(xb2_ready, 1)
                for p in range(CK):
                    t.pool_rstd(pool, i, p)
                for p in range(CK):
                    t.pool_inner_rstd(pool, i, p)
                for p in range(CK):
                    t.pool_store(pool, i, p)

        @block.tensor
        def _(pe):
            open_sems(pe, 5, proj_ready)
            open_sems(pe, 1, state_out_ready)
            open_sems(pe, CK, out_ready)
            t.open_tensor(pe)
            with pe.Fori(0, CHUNKS) as i:
                pe.wait_ge(step_done, this(i, MIXED, NV))
                pe.wait_ge(act_ready, last(i, 5, 5))
                for bank, w, rows in ((XS, k.wsin1, N1), (DECAY, k.wd1, N1), (SEL, k.wsel1, N1), (U, k.wi1, D), (G, k.wg1, D)):
                    nc.tensor.matmul(psum[0:rows, bank, 0:CT], w[:, :], mixed[:, :], start=True, stop=True)\
                        .then_inc(proj_ready, 1)
                pe.wait_ge(step_done, this(i, CHOSEN, NV))
                nc.tensor.matmul(psum[:, 5, 0:CT], k.wso1[:, :], chosen[:, :], start=True, stop=True)\
                    .then_inc(state_out_ready, 1)
                pe.wait_ge(step_done, this(i, Z, NV))
                for p in range(CK):
                    pe.wait_ge(t.r_ready, n(i, p - 1) if p else b(i, CK - 1))
                    nc.tensor.matmul(psum[:, 6, 0:D], z[:, 2 * p:2 * p + 2, :], k.wout1[:, :], start=True, stop=True)\
                        .then_inc(out_ready, 1)
                for p in range(CK):
                    pe.wait_ge(t.feat_stored, n(i, p - 1) if p else b(i, CK - 1))
                    t.tensor_transpose(pe, i, p, psum[:, 7, 0:128])

        @block.vector
        def _(dve):
            open_sems(dve, NV, step_done)
            t.open_vector(dve)
            dve.wait_ge(zeroed, 2)
            with dve.Fori(0, CHUNKS) as i:
                def follows(step):
                    dve.wait_ge(step_done, this(i, step, NV))

                dve.wait_ge(h_ready, this(i))
                nc.vector.tensor_scalar(tap0[:, :], hp[:, :, 0:S], k.mix_w1[:, 0:1], k.mix_b1[:, :], ALU.mult, ALU.add)\
                    .then_inc(step_done, 1)
                follows(TAP0)
                nc.vector.scalar_tensor_tensor(tap1[:, :].rearrange("p (b s) -> p b s", b=CB), hp[:, :, 1:S + 1],
                                               k.mix_w1[:, 1:2], tap0[:, :].rearrange("p (b s) -> p b s", b=CB),
                                               ALU.mult, ALU.add).then_inc(step_done, 1)
                follows(TAP1)
                dve.wait_ge(proj_ready, last(i, 5, 5))
                nc.vector.scalar_tensor_tensor(mixed[:, :].rearrange("p (b s) -> p b s", b=CB), hp[:, :, 2:S + 2],
                                               k.mix_w1[:, 2:3], tap1[:, :].rearrange("p (b s) -> p b s", b=CB),
                                               ALU.mult, ALU.add).then_inc(step_done, 1)
                dve.wait_ge(act_ready, this(i, DECAY + 1, 5))
                nc.vector.tensor_scalar(keep[:, :], decay[:, :], -1.0, 1.0, ALU.mult, ALU.add).then_inc(step_done, 1)
                follows(ONE_MINUS)
                nc.vector.tensor_tensor(drive[:, :], keep[:, :], xs[:, :], ALU.mult).then_inc(step_done, 1)
                nc.vector.memset(decay[:, :].rearrange("p (b s) -> p b s", b=CB)[:, :, 0:1], 0.0).then_inc(step_done, 1)
                follows(RESET)
                nc.vector.tensor_tensor_scan(states[:, :], decay[:, :], drive[:, :], 0.0, ALU.mult, ALU.add)\
                    .then_inc(step_done, 1)
                follows(STATES)
                dve.wait_ge(act_ready, this(i, SEL + 1, 5))
                dve.wait_ge(state_out_ready, last(i))
                nc.vector.tensor_tensor(chosen[:, :], states[:, :], sel[:, :], ALU.mult).then_inc(step_done, 1)
                dve.wait_ge(state_out_ready, this(i))
                dve.wait_ge(act_ready, this(i, 5, 5))
                nc.vector.scalar_tensor_tensor(diff[:, :], psum[:, 5, 0:CT], k.bso1[:, :], u[:, :],
                                               ALU.add, ALU.subtract).then_inc(step_done, 1)
                follows(DIFF)
                nc.vector.tensor_tensor(gdiff[:, :], diff[:, :], g[:, :], ALU.mult).then_inc(step_done, 1)
                follows(GDIFF)
                dve.wait_ge(out_ready, b(i, CK - 1))
                nc.vector.tensor_tensor(z[:, :, 0:S], gdiff[:, :].rearrange("p (b s) -> p b s", b=CB),
                                        u[:, :].rearrange("p (b s) -> p b s", b=CB), ALU.add).then_inc(step_done, 1)
                for p in range(CK):
                    dve.wait_ge(out_ready, n(i, p))
                    dve.wait_ge(xb2_ready, n(i, p))
                    nc.vector.tensor_tensor(t.r[:, p, :], psum[:, 6, 0:D], xb2[:, p, :], ALU.add).then_inc(t.r_ready, 1)
                    t.vector_moments(dve, i, p)
                for p in range(CK):
                    t.vector_normalise(dve, i, p)
                for p in range(CK):
                    t.vector_inner_moments(dve, i, p)
                for p in range(CK):
                    t.vector_inner_normalise(dve, i, p)

        @block.scalar
        def _(act):
            open_sems(act, 5, act_ready)
            t.open_scalar(act)
            with act.Fori(0, CHUNKS) as i:
                act.wait_ge(step_done, last(i, Z, NV))
                for bank, dst, f, bias in ((XS, xs, ACT.Tanh, k.bsin1), (DECAY, decay, ACT.Sigmoid, k.bd1),
                                           (SEL, sel, ACT.Sigmoid, k.bsel1), (U, u, ACT.Tanh, k.bi1),
                                           (G, g, ACT.Sigmoid, k.bg1)):
                    act.wait_ge(proj_ready, this(i, bank + 1, 5))
                    rows = D if bank >= U else N1
                    nc.scalar.activation(dst[:, :], psum[0:rows, bank, 0:CT], f, bias=bias[:, :]).then_inc(act_ready, 1)
                for p in range(CK):
                    t.scalar_store(act, i, p, psum[:, 7, 0:128])


def cross_attention_phase(k):
    nc = k.nc
    WIDTH = (2 * (C // 8) + 2, C // 2 - 2 * (C // 8) - 2)
    FIRST = (0, 2 * WIDTH[0])
    UQ = 128 // H1
    UPS = S // UQ
    NU = 2 * UPS
    HB = 4
    NB = H1 // HB
    SCALE = DH1 ** -0.5
    with ExitStack() as ctx:
        sem = lambda name: k.sem(ctx, "xa_" + name)
        sb = lambda name, shape, dt=fp32: k.sb(ctx, "xa_" + name, shape, dt)
        xq = sb("xq", [128, 2, S])
        q_hi, q_lo = sb("q_hi", [128, 2, S, H1], fp32r), sb("q_lo", [128, 2, S, H1], fp32r)
        ctxT = sb("ctxT", [128, 2, C])
        c_hi, c_lo = sb("c_hi", [128, 2, C], fp32r), sb("c_lo", [128, 2, C], fp32r)
        ctxN = sb("ctxN", [KP, 2, KT * D])
        pr = sb("pr", [128, 2, C])
        prT = sb("prT", [KP, 2, KT, 128])
        halfmax = sb("halfmax", [128, 2, 2])
        negmax = sb("negmax", [128, 2, 1])
        rs = sb("rs", [128, 2, 2])
        total = sb("total", [128, 2, 1])
        rinv = sb("rinv", [128, 2, 1])
        rb = sb("rb", [128, 2, 128])
        on = sb("on", [128, H1, 2, SP])
        ybo = sb("ybo", [128, D])
        psum = ctx.enter_context(nc.psum_tensor("xa_psum", [128, 8, 512], fp32))
        ctxT_loaded = [sem("ctxT_loaded0"), sem("ctxT_loaded1")]
        ctxN_loaded = [sem("ctxN_loaded0"), sem("ctxN_loaded1")]
        xq_ready, q_ready, q_hi_kept, q_lo_kept = sem("xq_ready"), sem("q_ready"), sem("q_hi_kept"), sem("q_lo_kept")
        c_hi_ready, c_lo_ready, splitting = sem("c_hi_ready"), sem("c_lo_ready"), sem("splitting")
        scores_ready, halfmax_ready, max_ready, exp_ready = sem("scores_ready"), sem("halfmax_ready"), sem("max_ready"), sem("exp_ready")
        total_ready, rinv_ready, rb_ready, rb_kept = sem("total_ready"), sem("rinv_ready"), sem("rb_ready"), sem("rb_kept")
        prT_ready, even_kept, odd_kept, pv_ready, on_kept = sem("prT_ready"), sem("even_kept"), sem("odd_kept"), sem("pv_ready"), sem("on_kept")
        on_zeroed, y_ready, ybo_ready, r_kept = sem("on_zeroed"), sem("y_ready"), sem("ybo_ready"), sem("r_kept")
        block = ctx.enter_context(nc.Block())
        n = lambda i, u: this(i, u + 1, NU)
        before = lambda i, u, back: n(i, u - back) if u >= back else last(i, u + 1 + NU - back, NU)

        @block.sync
        def _(sp):
            with sp.Fori(0, PAIRS) as i:
                for h in range(2):
                    sp.wait_ge(c_lo_ready, last(i, h + 1, 2))
                    sp.dma_start(ctxT[:, h:h + 1, :],
                                 k.dram["ctxT"][bass.ds(2 * i + h, 1), :, :].rearrange("b d c -> d b c"))\
                        .then_inc(ctxT_loaded[h], 16)
                    sp.wait_ge(pv_ready, last(i, (h + 1) * UPS, NU))
                    sp.dma_start(ctxN[:, h:h + 1, :],
                                 k.dram["ctxN"][bass.ds(2 * i + h, 1), :, :, :].rearrange("b q t d -> q b (t d)"))\
                        .then_inc(ctxN_loaded[h], 16)

        @block.gpsimd
        def _(pool):
            open_sems(pool, 1, xq_ready)
            open_sems(pool, 2, c_hi_ready, c_lo_ready)
            pool.memset(on[:, :, :, :], 0.0).then_inc(on_zeroed, 1)
            with pool.Fori(0, PAIRS) as i:
                pool.wait_ge(q_ready, last(i, NB, NB))
                pool.tensor_copy(xq[:, :, :], k.x_feat[:, bass.ds(2 * i, 2), :]).then_inc(xq_ready, 1)
                for h in range(2):
                    pool.wait_ge(ctxT_loaded[h], (i + 1) * 16)
                    pool.wait_ge(scores_ready, last(i, 2 * (h + 1) * UPS, 2 * NU))
                    pool.sem_inc(splitting, 1)
                    pool.tensor_copy(c_hi[:, h, :], ctxT[:, h, :]).then_inc(c_hi_ready, 1)
                    pool.wait_ge(c_hi_ready, this(i, h + 1, 2))
                    pool.tensor_tensor(c_lo[:, h, :], ctxT[:, h, :], c_hi[:, h, :].bitcast(fp32), ALU.subtract)\
                        .then_inc(c_lo_ready, 1)

        @block.tensor
        def _(pe):
            open_sems(pe, NB, q_ready)
            open_sems(pe, 2 * NU, scores_ready)
            open_sems(pe, 3 * NU, prT_ready)
            open_sems(pe, NU, pv_ready, rb_ready)
            open_sems(pe, 1, y_ready)
            with pe.Fori(0, PAIRS) as i:
                pe.wait_ge(xq_ready, this(i))
                for c in range(NB):
                    if c == 0:
                        pe.wait_ge(on_kept, last(i, NU, NU))
                    elif c == 1:
                        pe.wait_ge(ybo_ready, last(i))
                    else:
                        pe.wait_ge(q_lo_kept, this(i, c - 1, NB))
                    for j in range(HB):
                        done = nc.tensor.matmul(psum[:, 6 + c % 2, j * 2 * S:(j + 1) * 2 * S],
                                                k.key_query[:, c * HB + j, :], xq[:, :, :], start=True, stop=True)
                    done.then_inc(q_ready, 1)

                def transposes(u, r):
                    for j in range(4):
                        kt = 4 * r + j
                        done = nc.tensor.transpose(psum[0:KP, 4 + r % 2, j * 128:(j + 1) * 128],
                                                   pr[:, u % 2, kt * KP:(kt + 1) * KP], k.ident[:, :])
                    done.then_inc(prT_ready, 1)

                for step in range(NU + 2):
                    u = step
                    if u < NU:
                        h, p0 = u // UPS, (u % UPS) * UQ
                        if u == 0:
                            pe.wait_ge(q_lo_kept, this(i, NB, NB))
                        if u % UPS == 0:
                            pe.wait_ge(c_lo_ready, this(i, h + 1, 2))
                        for half in range(2):
                            pe.wait_ge(exp_ready, this(i, 2 * (u - 1) + half + 1, 2 * NU) if u
                                       else last(i, 2 * (NU - 1) + half + 1, 2 * NU))
                            for j in range(2 * half, 2 * half + 2):
                                w = WIDTH[half]
                                keys = slice(FIRST[half] + (j % 2) * w, FIRST[half] + (j % 2 + 1) * w)
                                qh = q_hi[:, h, p0:p0 + UQ, :].rearrange("p a b -> p (a b)")
                                ql = q_lo[:, h, p0:p0 + UQ, :].rearrange("p a b -> p (a b)")
                                nc.tensor.matmul(psum[:, j, 0:w], qh, c_hi[:, h, keys], start=True, stop=False)
                                nc.tensor.matmul(psum[:, j, 0:w], qh, c_lo[:, h, keys], start=False, stop=False)
                                done = nc.tensor.matmul(psum[:, j, 0:w], ql, c_hi[:, h, keys], start=False, stop=True)
                            done.then_inc(scores_ready, 1)
                    u = step - 1
                    if 0 <= u < NU:
                        pe.wait_ge(exp_ready, this(i, 2 * u + 2, 2 * NU))
                        pe.wait_ge(even_kept, this(i, 2 * u, 2 * NU) if u else last(i, 2 * NU, 2 * NU))
                        transposes(u, 0)
                        pe.wait_ge(odd_kept, before(i, u, 1))
                        transposes(u, 1)
                    u = step - 2
                    if 0 <= u < NU:
                        pe.wait_ge(rinv_ready, n(i, u))
                        if u:
                            pe.wait_ge(rb_kept, n(i, u - 1))
                        nc.tensor.transpose(psum[:, 7, 128:256], rinv[:, u % 2, :].to_broadcast([128, 128]), k.ident[:, :])\
                            .then_inc(rb_ready, 1)
                        if u % UPS == 0:
                            pe.wait_ge(ctxN_loaded[u // UPS], (i + 1) * 16)
                        pe.wait_ge(even_kept, this(i, 2 * u + 2, 2 * NU))
                        pe.wait_ge(odd_kept, n(i, u))
                        if u:
                            pe.wait_ge(on_kept, n(i, u - 1))
                        for kt in range(KT):
                            done = nc.tensor.matmul(psum[:, 6, 0:128], ctxN[:, u // UPS, kt * D:(kt + 1) * D],
                                                    prT[:, u % 2, kt, :], start=(kt == 0), stop=(kt == KT - 1))
                        done.then_inc(pv_ready, 1)
                    u = step - 1
                    if 0 <= u < NU:
                        pe.wait_ge(even_kept, this(i, 2 * u + 1, 2 * NU))
                        transposes(u, 2)
                pe.wait_ge(rb_kept, n(i, NU - 1))
                pe.wait_ge(on_kept, n(i, NU - 1))
                for h in range(H1):
                    done = nc.tensor.matmul(psum[:, 7, 0:128], on[:, h, :, :], k.value_out[:, h, :],
                                            start=(h == 0), stop=(h == H1 - 1))
                done.then_inc(y_ready, 1)

        @block.vector
        def _(dve):
            open_sems(dve, NB, q_lo_kept)
            open_sems(dve, 2 * NU, halfmax_ready, even_kept)
            open_sems(dve, NU, max_ready, total_ready, rinv_ready, on_kept)
            open_sems(dve, 1, ybo_ready, r_kept)
            dve.wait_ge(on_zeroed, 1)
            with dve.Fori(0, PAIRS) as i:
                for c in range(NB):
                    dve.wait_ge(q_hi_kept, this(i, c + 1, NB))
                    order = lambda v: v[:, :, :, c * HB:(c + 1) * HB].rearrange("p b s h -> p h b s")
                    for b_ in range(2):
                        done = nc.vector.scalar_tensor_tensor(
                            q_lo[:, b_, :, c * HB:(c + 1) * HB].rearrange("p s h -> p h s"),
                            psum[:, 6 + c % 2, 0:HB * 2 * S].rearrange("p (h b s) -> p h b s", h=HB, b=2)[:, :, b_, :],
                            SCALE, q_hi[:, b_, :, c * HB:(c + 1) * HB].bitcast(fp32).rearrange("p s h -> p h s"),
                            ALU.mult, ALU.subtract)
                    done.then_inc(q_lo_kept, 1)
                for step in range(NU + 2):
                    u = step
                    if u < NU:
                        for half in range(2):
                            dve.wait_ge(scores_ready, this(i, 2 * u + half + 1, 2 * NU))
                            nc.vector.tensor_reduce(halfmax[:, u % 2, half:half + 1], psum[:, 2 * half:2 * half + 2, 0:WIDTH[half]],
                                                    AX.XY, ALU.max, negate=True).then_inc(halfmax_ready, 1)
                        dve.wait_ge(halfmax_ready, this(i, 2 * u + 2, 2 * NU))
                        nc.vector.tensor_tensor(negmax[:, u % 2, :], halfmax[:, u % 2, 0:1], halfmax[:, u % 2, 1:2],
                                                ALU.min).then_inc(max_ready, 1)
                    u = step - 1
                    if 0 <= u < NU:
                        dve.wait_ge(exp_ready, this(i, 2 * u + 2, 2 * NU))
                        nc.vector.tensor_tensor(total[:, u % 2, :], rs[:, u % 2, 0:1], rs[:, u % 2, 1:2], ALU.add)\
                            .then_inc(total_ready, 1)
                        dve.wait_ge(prT_ready, this(i, 3 * u + 1, 3 * NU))
                        dve.wait_ge(pv_ready, before(i, u, 2))
                        nc.vector.tensor_copy(prT[:, u % 2, 0:4, :].rearrange("p a b -> p (a b)"), psum[0:KP, 4, :])\
                            .then_inc(even_kept, 1)
                        dve.wait_ge(total_ready, n(i, u))
                        nc.vector.reciprocal(rinv[:, u % 2, :], total[:, u % 2, :]).then_inc(rinv_ready, 1)
                    u = step - 2
                    if 0 <= u < NU:
                        h, p0 = u // UPS, (u % UPS) * UQ
                        dve.wait_ge(pv_ready, n(i, u))
                        dve.wait_ge(rb_kept, n(i, u))
                        if u == 0:
                            dve.wait_ge(y_ready, last(i))
                        nc.vector.tensor_tensor(on[:, :, h, p0:p0 + UQ],
                                                psum[:, 6, 0:128].rearrange("p (s h) -> p h s", h=H1),
                                                rb[:, u % 2, :].rearrange("p (s h) -> p h s", h=H1), ALU.mult)\
                            .then_inc(on_kept, 1)
                    u = step - 1
                    if 0 <= u < NU:
                        dve.wait_ge(prT_ready, this(i, 3 * u + 3, 3 * NU))
                        nc.vector.tensor_copy(prT[:, u % 2, 8:12, :].rearrange("p a b -> p (a b)"), psum[0:KP, 4, :])\
                            .then_inc(even_kept, 1)
                dve.wait_ge(y_ready, this(i))
                nc.vector.tensor_tensor(ybo[:, :], psum[:, 7, 0:128], k.bout_row1x[:, :], ALU.add).then_inc(ybo_ready, 1)
                dve.wait_ge(ybo_ready, this(i))
                nc.vector.scalar_tensor_tensor(k.r_tok[:, bass.ds(i, 1), :], ybo[:, :].unsqueeze(1), k.gate_tanh[:, :],
                                               k.x_tok[:, bass.ds(i, 1), :], ALU.mult, ALU.add).then_inc(r_kept, 1)

        @block.scalar
        def _(act):
            open_sems(act, NB, q_hi_kept)
            open_sems(act, 2 * NU, exp_ready)
            open_sems(act, NU, odd_kept, rb_kept)
            with act.Fori(0, PAIRS) as i:
                act.wait_ge(scores_ready, last(i, 2 * NU, 2 * NU))
                for c in range(NB):
                    act.wait_ge(q_ready, this(i, c + 1, NB))
                    for b_ in range(2):
                        done = nc.scalar.activation(
                            q_hi[:, b_, :, c * HB:(c + 1) * HB].rearrange("p s h -> p h s"),
                            psum[:, 6 + c % 2, 0:HB * 2 * S].rearrange("p (h b s) -> p h b s", h=HB, b=2)[:, :, b_, :],
                            ACT.Copy, scale=SCALE)
                    done.then_inc(q_hi_kept, 1)
                for step in range(NU + 2):
                    u = step - 2
                    if 0 <= u < NU:
                        act.wait_ge(rb_ready, n(i, u))
                        act.wait_ge(on_kept, before(i, u, 2))
                        nc.scalar.activation(rb[:, u % 2, :], psum[:, 7, 128:256], ACT.Copy).then_inc(rb_kept, 1)
                    u = step
                    if u < NU:
                        act.wait_ge(max_ready, n(i, u))
                        act.wait_ge(prT_ready, this(i, 3 * (u - 1), 3 * NU) if u >= 2 else last(i, 3 * (u + NU - 1), 3 * NU))
                        act.wait_ge(total_ready, before(i, u, 2))
                        for half in range(2):
                            keys = slice(FIRST[half], FIRST[half] + 2 * WIDTH[half])
                            nc.scalar.activation(pr[:, u % 2, keys].rearrange("p (a c) -> p a c", a=2),
                                                 psum[:, 2 * half:2 * half + 2, 0:WIDTH[half]], ACT.Exp, bias=negmax[:, u % 2, :],
                                                 accum_out=rs[:, u % 2, half:half + 1]).then_inc(exp_ready, 1)
                    u = step - 1
                    if 0 <= u < NU:
                        act.wait_ge(prT_ready, this(i, 3 * u + 2, 3 * NU))
                        act.wait_ge(pv_ready, before(i, u, 2))
                        nc.scalar.activation(prT[:, u % 2, 4:8, :].rearrange("p a b -> p (a b)"), psum[0:KP, 5, :],
                                             ACT.Copy).then_inc(odd_kept, 1)


def cross_norm_phase(k):
    nc = k.nc
    with ExitStack() as ctx:
        t = Tail(k, ctx, "xn", router=k.router1)
        psum = ctx.enter_context(nc.psum_tensor("xn_psum", [128, 8, 512], fp32))
        block = ctx.enter_context(nc.Block())
        n = lambda i, p: this(i, p + 1, CK)
        b = lambda i, p: last(i, p + 1, CK)

        @block.gpsimd
        def _(pool):
            t.open_pool(pool)
            with pool.Fori(0, CHUNKS) as i:
                for p in range(CK):
                    t.pool_rstd(pool, i, p)
                for p in range(CK):
                    t.pool_store(pool, i, p)

        @block.tensor
        def _(pe):
            t.open_tensor(pe)
            with pe.Fori(0, CHUNKS) as i:
                for p in range(CK):
                    pe.wait_ge(t.feat_stored, n(i, p - 2) if p >= 2 else b(i, p + 2))
                    t.tensor_transpose(pe, i, p, psum[:, p % 2, 0:128])
                    pe.wait_ge(t.logits_kept, n(i, p - 2) if p >= 2 else b(i, p + 2))
                    t.tensor_logits(pe, i, p, psum[:, 2 + p % 2, 0:E])

        @block.vector
        def _(dve):
            t.open_vector(dve)
            with dve.Fori(0, CHUNKS) as i:
                for p in range(CK):
                    nc.vector.tensor_copy(t.r[:, p:p + 1, :], k.r_tok[:, bass.ds(i * CK + p, 1), :]).then_inc(t.r_ready, 1)
                for p in range(CK):
                    t.vector_moments(dve, i, p)
                for p in range(CK):
                    t.vector_normalise(dve, i, p)
                for p in range(CK):
                    t.vector_logits(dve, i, p, psum[:, 2 + p % 2, 0:E])

        @block.scalar
        def _(act):
            t.open_scalar(act)
            with act.Fori(0, CHUNKS) as i:
                for p in range(CK):
                    t.scalar_store(act, i, p, psum[:, p % 2, 0:128])


def declare(k, ctx):
    sb = lambda name, shape, dt=fp32: k.sb(ctx, name, shape, dt)
    k.x_tok = sb("x_tok", [128, PAIRS, D])
    k.x_feat = sb("x_feat", [128, B, S])
    k.ident = sb("ident", [128, 128])
    k.window_mask = sb("window_mask", [128, S])
    k.head_mask = sb("head_mask", [128, H0])
    k.value_mask = sb("value_mask", [128, H0 // 2, 2, DH0])
    k.minus_half = sb("minus_half", [128, 1])
    k.eps = sb("eps", [128, 1])
    k.expert_index_u = sb("expert_index_u", [128, E], u32)
    k.expert_index = sb("expert_index", [128, E])
    k.wqT0, k.wkT0, k.wvT0, k.woT0 = (sb(n, [128, D]) for n in ("wqT0", "wkT0", "wvT0", "woT0"))
    k.bq0, k.bk0, k.bv0 = (sb(n, [128, 1]) for n in ("bq0", "bk0", "bv0"))
    k.bo_row0 = sb("bo_row0", [128, D])
    k.wqT0x, k.wk0x, k.wvT0x, k.woT0x = (sb(n, [128, D]) for n in ("wqT0x", "wk0x", "wvT0x", "woT0x"))
    k.bq0x, k.bv0x = (sb(n, [128, 1]) for n in ("bq0x", "bv0x"))
    k.bo_row0x = sb("bo_row0x", [128, D])
    k.cross_row = sb("cross_row", [128, D])
    k.router0 = sb("router0", [128, E])
    k.up0 = sb("up0", [128, E, U0])
    k.up_bias0 = sb("up_bias0", [128, E, U0 // 128])
    k.down0 = sb("down0", [128, E, U0 // 128, D])
    k.down_bias0 = sb("down_bias0", [128, E])
    k.ln_g1, k.ln_b1, k.mix_b1, k.bi1, k.bg1, k.bso1 = (sb(n, [128, 1]) for n in ("ln_g1", "ln_b1", "mix_b1", "bi1", "bg1", "bso1"))
    k.mix_w1 = sb("mix_w1", [128, 3])
    k.wi1, k.wg1, k.wout1 = (sb(n, [128, D]) for n in ("wi1", "wg1", "wout1"))
    k.wsin1, k.wd1, k.wsel1 = (sb(n, [128, 32]) for n in ("wsin1", "wd1", "wsel1"))
    k.wso1 = sb("wso1", [32, D])
    k.bsin1, k.bd1, k.bsel1 = (sb(n, [32, 1]) for n in ("bsin1", "bd1", "bsel1"))
    k.bout_row1 = sb("bout_row1", [128, D])
    k.gamma1, k.beta1 = (sb(n, [128, 1]) for n in ("gamma1", "beta1"))
    k.key_query = sb("key_query", [128, H1, D])
    k.value_out = sb("value_out", [128, H1, D])
    k.bout_row1x = sb("bout_row1x", [128, D])
    k.gate_in, k.gate_tanh = sb("gate_in", [128, 1]), sb("gate_tanh", [128, 1])
    k.router1 = sb("router1", [128, E])
    k.router_bias_row1 = sb("router_bias_row1", [128, E])
    k.gate1 = sb("gate1", [128, E + 1, I1])
    k.up1 = sb("up1", [128, E + 1, I1])
    k.down1 = sb("down1", [128, E + 1, I1 // 128, D])
    k.r_tok = sb("r_tok", [128, PAIRS, D])
    k.logits = sb("logits", [128, PAIRS, E])
    k.expert_weights = sb("expert_weights", [128, PAIRS, E])
    sem = lambda name: k.sem(ctx, name)
    k.weights_loaded, k.fold_loaded = sem("weights_loaded"), sem("fold_loaded")
    k.late_weights_loaded = ctx.enter_context(k.nc.semaphore("late_weights_loaded"))
    k.loads = [
        ("L0_wqT", k.wqT0[:, :]), ("L0_wkT", k.wkT0[:, :]), ("L0_wvT", k.wvT0[:, :]), ("L0_woT", k.woT0[:, :]),
        ("L0_bq", k.bq0[:, :]), ("L0_bk", k.bk0[:, :]), ("L0_bv", k.bv0[:, :]), ("L0_bo", k.bo_row0[:, :]),
        ("X0_wqT", k.wqT0x[:, :]), ("X0_wk", k.wk0x[:, :]), ("X0_wvT", k.wvT0x[:, :]), ("X0_woT", k.woT0x[:, :]),
        ("X0_bq", k.bq0x[:, :]), ("X0_bv", k.bv0x[:, :]), ("X0_bo", k.bo_row0x[:, :]), ("gate", k.gate_in[:, :]),
    ]
    k.late_loads = [
        ("F0_router", k.router0[:, :]), ("F0_up", k.up0[:, :, :]), ("F0_up_bias", k.up_bias0[:, :, :]),
        ("F0_down", k.down0[:, :, :, :]), ("F0_down_bias", k.down_bias0[:, :]),
        ("L1_ln_g", k.ln_g1[:, :]), ("L1_ln_b", k.ln_b1[:, :]), ("L1_mix_b", k.mix_b1[:, :]),
        ("L1_bi", k.bi1[:, :]), ("L1_bg", k.bg1[:, :]), ("L1_bso", k.bso1[:, :]), ("L1_mix_w", k.mix_w1[:, :]),
        ("L1_wi", k.wi1[:, :]), ("L1_wg", k.wg1[:, :]), ("L1_wout", k.wout1[:, :]),
        ("L1_wsin", k.wsin1[:, :]), ("L1_wd", k.wd1[:, :]), ("L1_wsel", k.wsel1[:, :]), ("L1_wso", k.wso1[:, :]),
        ("L1_bsin", k.bsin1[:, :]), ("L1_bd", k.bd1[:, :]), ("L1_bsel", k.bsel1[:, :]), ("L1_bout", k.bout_row1[:, :]),
        ("L1_gamma", k.gamma1[:, :]), ("L1_beta", k.beta1[:, :]), ("X1_bout", k.bout_row1x[:, :]),
        ("F1_router", k.router1[:, :]), ("F1_router_bias", k.router_bias_row1[:, :]),
        ("F1_gate", k.gate1[:, 0:E, :]), ("F1_up", k.up1[:, 0:E, :]), ("F1_down", k.down1[:, 0:E, :, :]),
        ("F1_gate_s", k.gate1[:, E, :]), ("F1_up_s", k.up1[:, E, :]), ("F1_down_s", k.down1[:, E, :, :]),
    ]


ROWS = ("L0_bo", "X0_bo", "L1_bout", "X1_bout", "F1_router_bias", "gate")


def layouts(a):
    c = np.ascontiguousarray
    col = lambda v: c(v.reshape(-1, 1))
    ctx = a["ctx_1024"]
    w_kv = a["L1_xattn_w_kv"]
    heads = lambda w: c(w.reshape(D, H1, DH1).transpose(2, 1, 0))
    out = {
        "x_pairs": c(a["x"].reshape(PAIRS, 2, S, D).transpose(1, 2, 0, 3)),
        "xT": c(a["x"].transpose(2, 0, 1)),
        "ctxT": c(ctx.transpose(0, 2, 1)),
        "ctxN": c(ctx.reshape(B, KT, KP, D).transpose(0, 2, 1, 3)),
        "L0_wqT": c(a["L0_attn_wq"].T), "L0_wkT": c(a["L0_attn_wk"].T),
        "L0_wvT": c(a["L0_attn_wv"].T), "L0_woT": c(a["L0_attn_wo"].T),
        "L0_bq": col(a["L0_attn_bq"]), "L0_bk": col(a["L0_attn_bk"]), "L0_bv": col(a["L0_attn_bv"]), "L0_bo": a["L0_attn_bo"],
        "X0_wqT": c(a["L0_xattn_Wq"].T), "X0_wk": a["L0_xattn_Wk"], "X0_wvT": c(a["L0_xattn_Wv"].T),
        "X0_woT": c(a["L0_xattn_Wo"].T), "X0_bq": col(a["L0_xattn_bq"]), "X0_bv": col(a["L0_xattn_bv"]), "X0_bo": a["L0_xattn_bo"],
        "F0_router": c(a["L0_ffn_w_router"].T), "F0_up": c(a["L0_ffn_w_up"].transpose(2, 0, 1)),
        "F0_up_bias": c(a["L0_ffn_b_up"].reshape(E, U0 // 128, 128).transpose(2, 0, 1)),
        "F0_down": c(a["L0_ffn_w_down"].reshape(E, D, U0 // 128, 128).transpose(3, 0, 2, 1)),
        "F0_down_bias": c(a["L0_ffn_b_down"].T),
        "L1_ln_g": col(a["L1_attn_ln_g"]), "L1_ln_b": col(a["L1_attn_ln_b"]), "L1_mix_b": col(a["L1_attn_mix_b"]),
        "L1_mix_w": c(a["L1_attn_mix_w"].reshape(D, 3)),
        "L1_wi": a["L1_attn_Wi"], "L1_wg": a["L1_attn_Wg"], "L1_wout": a["L1_attn_Wout"], "L1_wsin": a["L1_attn_Wsin"],
        "L1_wd": a["L1_attn_Wd"], "L1_wsel": a["L1_attn_Wsel"], "L1_wso": a["L1_attn_Wso"],
        "L1_bi": col(a["L1_attn_bi"]), "L1_bg": col(a["L1_attn_bg"]), "L1_bso": col(a["L1_attn_bso"]),
        "L1_bsin": col(a["L1_attn_bsin"]), "L1_bd": col(a["L1_attn_bd"]), "L1_bsel": col(a["L1_attn_bsel"]),
        "L1_bout": a["L1_attn_bout"],
        "L1_gamma": col(a["L1_xattn_ln_gamma"]), "L1_beta": col(a["L1_xattn_ln_beta"]),
        "L1_wqT": heads(a["L1_xattn_w_q"]), "L1_wkT": heads(c(w_kv[:, :H1 * DH1])), "L1_wvT": heads(c(w_kv[:, H1 * DH1:])),
        "L1_wo": c(a["L1_xattn_w_out"].reshape(H1, DH1, D).transpose(1, 0, 2)),
        "X1_bout": a["L1_xattn_b_out"], "gate": a["L1_xattn_gate"],
        "F1_router": c(a["L1_ffn_router_w"].T), "F1_router_bias": a["L1_ffn_routing_bias"],
        "F1_gate": c(a["L1_ffn_gate_w"].transpose(1, 0, 2)), "F1_up": c(a["L1_ffn_up_w"].transpose(1, 0, 2)),
        "F1_down": c(a["L1_ffn_down_w"].reshape(E, I1 // 128, 128, D).transpose(2, 0, 1, 3)),
        "F1_gate_s": c(a["L1_ffn_shared_gate"].T), "F1_up_s": c(a["L1_ffn_shared_up"].T),
        "F1_down_s": c(a["L1_ffn_shared_down"].reshape(D, I1 // 128, 128).transpose(2, 1, 0)),
    }
    return {name: c(v) for name, v in out.items()}


PHASES = (setup_phase, self_attention_phase, context_attention_phase, expert_phase0, state_space_phase,
          cross_attention_phase, cross_norm_phase, expert_phase1)


def build(nc, dram, out):
    with ExitStack() as ctx:
        k = Core(nc, ctx, dram)
        k.out = out
        declare(k, ctx)
        for phase in PHASES:
            phase(k)
            k.clear_semaphores()


def kernel(**inputs):
    import concourse.bacc as bacc
    from concourse.bass_utils import run_bass_kernel_spmd

    arrays = {"in_" + name: a for name, a in layouts({n: np.asarray(v) for n, v in inputs.items()}).items()}
    nc = bacc.Bacc("TRN2", target_bir_lowering=False, num_devices=1)
    dram = {}
    for name, a in arrays.items():
        ap = nc.dram_tensor(name, list(a.shape), fp32, kind="ExternalInput").ap()
        name = name[3:]
        dram[name] = ap.partition_broadcast(128) if name in ROWS else ap
    out = nc.dram_tensor("out_0", [B, S, D], fp32, kind="ExternalOutput").ap()
    build(nc, dram, out)
    r = run_bass_kernel_spmd(nc, [arrays], core_ids=[0])
    return r.results[0]["out_0"]
```

```python
from contextlib import ExitStack

import numpy as np
import concourse.bass as bass
from concourse import mybir

fp32 = mybir.dt.float32
fp32r = mybir.dt.float32r
u32 = mybir.dt.uint32
ALU = mybir.AluOpType
ACT = mybir.ActivationFunctionType
AX = mybir.AxisListType

B, S, D = 32, 56, 128
SP = 64
PAIRS = B // 2
CK = 4
CHUNKS = PAIRS // CK
CB = 2 * CK
CT = CB * S
C, KT, KP = 1500, 12, 125
H0, DH0, WIN = 16, 8, 32
H1, DH1 = 16, 64
E, U0, I1 = 8, 512, 256
EPS = 1e-5
NEG = -1.0e30


def this(i, n=1, per=1):
    return i * per + (per + n)


def last(i, n=1, per=1):
    return i * per + n


class Core:

    def __init__(self, nc, ctx, dram):
        self.nc, self.ctx, self.dram = nc, ctx, dram
        self.used = []

    def sb(self, ctx, name, shape, dt=fp32):
        return ctx.enter_context(self.nc.sbuf_tensor(name, shape, dt))

    def sem(self, ctx, name):
        handle = ctx.enter_context(self.nc.semaphore(name))
        self.used.append(handle.num)
        return handle

    def clear_semaphores(self):
        nums, self.used = sorted(self.used), []
        with self.nc.Block() as block:
            @block.gpsimd
            def _(pool):
                start = nums[0]
                for a, b in zip(nums, nums[1:] + [None]):
                    if b != a + 1:
                        pool.sem_clear(range(start, a + 1))
                        start = b


def setup_phase(k):
    nc, d = k.nc, k.dram
    with ExitStack() as ctx:
        consts_built = k.sem(ctx, "consts_built")
        pads_zeroed = k.sem(ctx, "pads_zeroed")
        x_loaded = k.sem(ctx, "x_loaded")
        tanh_gate_ready = k.sem(ctx, "tanh_gate_ready")
        row_ready = k.sem(ctx, "row_ready")
        psum = ctx.enter_context(nc.psum_tensor("setup_psum", [128, 8, 512], fp32))
        consts_ready = k.sem(ctx, "consts_ready")
        block = ctx.enter_context(nc.Block())

        @block.sync
        def _(sp):
            for name, dst in k.loads:
                sp.dma_start(dst, d[name]).then_inc(k.weights_loaded, 16)
            sp.dma_start(k.x_feat[:, :, :], d["xT"]).then_inc(x_loaded, 16)
            sp.wait_ge(pads_zeroed, 1)
            for h in range(2):
                sp.dma_start(k.x_tok[h * SP:h * SP + S, :, :], d["x_pairs"][h]).then_inc(x_loaded, 16)
            sp.wait_ge(x_loaded, 3 * 16)

        @block.gpsimd
        def _(pool):
            n = 0

            def step(instruction):
                nonlocal n
                n += 1
                instruction.then_inc(consts_built, 1)

            step(pool.memset(k.ident[:, :], 0.0))
            step(pool.memset(k.window_mask[:, :], 0.0))
            step(pool.memset(k.head_mask[:, :], 1.0))
            step(pool.memset(k.value_mask[:, :, :, :], 1.0))
            step(pool.memset(k.minus_half[:, :], -0.5))
            step(pool.memset(k.eps[:, :], EPS))
            pool.wait_ge(consts_built, n)
            step(pool.affine_select(out=k.ident[:, :], in_=k.ident[:, :], compare_op=ALU.not_equal,
                                    fill=1.0, base=0, pattern=[[-1, 128]], channel_multiplier=1))
            for half in range(2):
                rows = k.window_mask[half * SP:(half + 1) * SP, :]
                pool.wait_ge(consts_built, n)
                step(pool.affine_select(out=rows, in_=rows, compare_op=ALU.is_ge, fill=NEG,
                                        base=WIN, pattern=[[-1, S]], channel_multiplier=1))
                pool.wait_ge(consts_built, n)
                step(pool.affine_select(out=rows, in_=rows, compare_op=ALU.is_ge, fill=NEG,
                                        base=WIN, pattern=[[1, S]], channel_multiplier=-1))
            pool.wait_ge(consts_built, n)
            step(pool.affine_select(out=k.head_mask[:, :], in_=k.head_mask[:, :], compare_op=ALU.is_ge,
                                    fill=0.0, base=0, pattern=[[-DH0, H0]], channel_multiplier=1))
            pool.wait_ge(consts_built, n)
            step(pool.affine_select(out=k.head_mask[:, :], in_=k.head_mask[:, :], compare_op=ALU.is_ge,
                                    fill=0.0, base=DH0 - 1, pattern=[[DH0, H0]], channel_multiplier=-1))
            pool.wait_ge(consts_built, n)
            even = k.value_mask[:, :, 0, :]
            step(pool.affine_select(out=even, in_=even, compare_op=ALU.is_ge, fill=0.0,
                                    base=S - 1, pattern=[[0, H0 // 2], [0, DH0]], channel_multiplier=-1))
            odd = k.value_mask[:, :, 1, :]
            step(pool.affine_select(out=odd, in_=odd, compare_op=ALU.is_ge, fill=0.0,
                                    base=-S, pattern=[[0, H0 // 2], [0, DH0]], channel_multiplier=1))
            step(pool.iota(k.expert_index_u[:, :], pattern=[[1, E]], base=0, channel_multiplier=0))
            pool.wait_ge(consts_built, n)
            step(pool.tensor_copy(k.expert_index[:, :], k.expert_index_u[:, :]))
            pool.wait_ge(consts_built, n)

        @block.vector
        def _(dve):
            dve.memset(k.x_tok[:, :, :], 0.0).then_inc(pads_zeroed, 1)
            dve.wait_ge(row_ready, 1)
            nc.vector.tensor_tensor(k.cross_row[:, :], psum[:, 0, 0:D], k.bo_row0x[:, :], ALU.add)\
                .then_inc(consts_ready, 1)
            nc.vector.tensor_scalar(k.bq0_scaled[:, :], k.bq0[:, :], DH0 ** -0.5, None, ALU.mult).then_inc(consts_ready, 1)
            dve.wait_ge(consts_ready, 2)
            dve.wait_ge(tanh_gate_ready, 1)
            dve.wait_ge(pads_zeroed, 1)

        @block.tensor
        def _(pe):
            pe.wait_ge(k.weights_loaded, 16 * len(k.loads))
            nc.tensor.matmul(psum[:, 0, 0:D], k.bv0x[:, 0:1].to_broadcast([128, 128]), k.woT0x[:, :],
                             start=True, stop=True).then_inc(row_ready, 1)

        @block.scalar
        def _(act):
            act.wait_ge(k.weights_loaded, 16 * len(k.loads))
            nc.scalar.activation(k.gate_tanh[:, :], k.gate_in[:, :], ACT.Tanh).then_inc(tanh_gate_ready, 1)


def open_sems(engine, per, *sems):
    for s in sems:
        engine.sem_inc(s, per)


class Tail:

    def __init__(self, k, ctx, tag, inner=None, router=None, final=False, per=None):
        sem = lambda name: k.sem(ctx, f"{tag}_{name}")
        self.k, self.inner, self.router, self.final = k, inner, router, final
        self.per = per or CK
        self.r = k.sb(ctx, tag + "_r", [128, self.per, D])
        self.moments = k.sb(ctx, tag + "_moments", [128, self.per, 6])
        self.mean_var = k.sb(ctx, tag + "_mean_var", [128, self.per, 2])
        self.var_eps = k.sb(ctx, tag + "_var_eps", [128, self.per, 1])
        self.rstd = k.sb(ctx, tag + "_rstd", [128, self.per, 1])
        self.xn = k.sb(ctx, tag + "_xn", [128, self.per, D])
        self.r_ready = sem("r_ready")
        self.moments_ready = sem("moments_ready")
        self.mean_var_ready = sem("mean_var_ready")
        self.var_eps_ready = sem("var_eps_ready")
        self.aggregating = sem("aggregating")
        self.storing = sem("storing")
        self.rstd_ready = sem("rstd_ready")
        self.xn_ready = sem("xn_ready")
        self.xnT_ready = sem("xnT_ready")
        self.feat_stored = sem("feat_stored")
        self.tok_stored = sem("tok_stored")
        if inner:
            self.moments2 = k.sb(ctx, tag + "_moments2", [128, self.per, 6])
            self.mean_var2 = k.sb(ctx, tag + "_mean_var2", [128, self.per, 2])
            self.var_eps2 = k.sb(ctx, tag + "_var_eps2", [128, self.per, 1])
            self.rstd2 = k.sb(ctx, tag + "_rstd2", [128, self.per, 1])
            self.xn2 = k.sb(ctx, tag + "_xn2", [128, self.per, D])
            self.moments2_ready = sem("moments2_ready")
            self.mean_var2_ready = sem("mean_var2_ready")
            self.var_eps2_ready = sem("var_eps2_ready")
            self.rstd2_ready = sem("rstd2_ready")
            self.xn2_ready = sem("xn2_ready")
        if router is not None:
            self.xnT = k.sb(ctx, tag + "_xnT", [128, 128])
            self.xnT_kept = sem("xnT_kept")
            self.logits_ready = sem("logits_ready")
            self.logits_kept = sem("logits_kept")
        self.out = self.xn2 if inner else self.xn
        self.out_ready = self.xn2_ready if inner else self.xn_ready

    def open_vector(self, dve):
        open_sems(dve, self.per, self.r_ready, self.moments_ready, self.mean_var_ready, self.xn_ready)
        if self.inner:
            open_sems(dve, self.per, self.moments2_ready, self.mean_var2_ready, self.xn2_ready)

        if self.router is not None:
            open_sems(dve, self.per, self.logits_kept)

    def open_pool(self, pool):
        open_sems(pool, self.per, self.var_eps_ready, self.rstd_ready, self.tok_stored)
        if self.inner:
            open_sems(pool, self.per, self.var_eps2_ready, self.rstd2_ready)

    def open_tensor(self, pe):
        open_sems(pe, self.per, self.xnT_ready)
        if self.router is not None:
            open_sems(pe, self.per, self.logits_ready)

    def open_scalar(self, act):
        open_sems(act, self.per, self.feat_stored)
        if self.router is not None:
            open_sems(act, self.per, self.xnT_kept)

    def vector_moments(self, dve, i, p):
        nc = self.k.nc
        dve.wait_ge(self.r_ready, this(i, p + 1, self.per))
        nc.vector.bn_stats(self.moments[:, p, :], self.r[:, p, :]).then_inc(self.moments_ready, 1)
        dve.wait_ge(self.moments_ready, this(i, p + 1, self.per))
        dve.sem_inc(self.aggregating, 1)
        nc.vector.bn_aggr(self.mean_var[:, p, :], self.moments[:, p, :]).then_inc(self.mean_var_ready, 1)

    def pool_rstd(self, pool, i, p):
        pool.wait_ge(self.mean_var_ready, this(i, p + 1, self.per))
        pool.tensor_tensor(self.var_eps[:, p, :], self.mean_var[:, p, 1:2], self.k.eps[:, :], ALU.add)\
            .then_inc(self.var_eps_ready, 1)
        pool.wait_ge(self.var_eps_ready, this(i, p + 1, self.per))
        pool.wait_ge(self.xn_ready, last(i, p + 1, self.per))
        pool.tensor_tensor(self.rstd[:, p, :], self.var_eps[:, p, :], self.k.minus_half[:, :], ALU.pow)\
            .then_inc(self.rstd_ready, 1)

    def vector_normalise(self, dve, i, p):
        nc = self.k.nc
        dve.wait_ge(self.rstd_ready, this(i, p + 1, self.per))
        if self.final:
            nc.vector.tensor_scalar(self.k.x_tok[:, bass.ds(i * self.per + p, 1), :], self.r[:, p:p + 1, :],
                                    self.mean_var[:, p, 0:1], self.rstd[:, p, :], ALU.subtract, ALU.mult)\
                .then_inc(self.xn_ready, 1)
            return
        if not self.inner:
            dve.wait_ge(self.xnT_ready, last(i, p + 1, self.per))
        dve.wait_ge(self.tok_stored, last(i, p + 1, self.per))
        nc.vector.tensor_scalar(self.xn[:, p, :], self.r[:, p, :], self.mean_var[:, p, 0:1],
                                self.rstd[:, p, :], ALU.subtract, ALU.mult).then_inc(self.xn_ready, 1)

    def vector_inner_moments(self, dve, i, p):
        nc = self.k.nc
        dve.wait_ge(self.xn_ready, this(i, p + 1, self.per))
        nc.vector.bn_stats(self.moments2[:, p, :], self.xn[:, p, :]).then_inc(self.moments2_ready, 1)
        dve.wait_ge(self.moments2_ready, this(i, p + 1, self.per))
        dve.sem_inc(self.aggregating, 1)
        nc.vector.bn_aggr(self.mean_var2[:, p, :], self.moments2[:, p, :]).then_inc(self.mean_var2_ready, 1)

    def pool_inner_rstd(self, pool, i, p):
        pool.wait_ge(self.mean_var2_ready, this(i, p + 1, self.per))
        pool.tensor_tensor(self.var_eps2[:, p, :], self.mean_var2[:, p, 1:2], self.k.eps[:, :], ALU.add)\
            .then_inc(self.var_eps2_ready, 1)
        pool.wait_ge(self.var_eps2_ready, this(i, p + 1, self.per))
        pool.wait_ge(self.xn2_ready, last(i, p + 1, self.per))
        pool.tensor_tensor(self.rstd2[:, p, :], self.var_eps2[:, p, :], self.k.minus_half[:, :], ALU.pow)\
            .then_inc(self.rstd2_ready, 1)

    def vector_inner_normalise(self, dve, i, p):
        nc = self.k.nc
        dve.wait_ge(self.rstd2_ready, this(i, p + 1, self.per))
        dve.wait_ge(self.xnT_ready, last(i, p + 1, self.per))
        nc.vector.tensor_scalar(self.xn2[:, p, :], self.xn[:, p, :], self.mean_var2[:, p, 0:1],
                                self.rstd2[:, p, :], ALU.subtract, ALU.mult).then_inc(self.xn2_ready, 1)

    def pool_store(self, pool, i, p):
        pool.wait_ge(self.xn_ready, this(i, p + 1, self.per))
        pool.sem_inc(self.storing, 1)
        pool.tensor_copy(self.k.x_tok[:, bass.ds(i * self.per + p, 1), :], self.xn[:, p:p + 1, :])\
            .then_inc(self.tok_stored, 1)

    def tensor_transpose(self, pe, i, p, bank):
        pe.wait_ge(self.out_ready, this(i, p + 1, self.per))
        pe.transpose(bank, self.out[:, p, :], self.k.ident[:, :]).then_inc(self.xnT_ready, 1)

    def scalar_store(self, act, i, p, bank):
        k = self.k
        act.wait_ge(self.xnT_ready, this(i, p + 1, self.per))
        if self.router is not None:
            act.wait_ge(self.logits_ready, last(i, self.per, self.per) if p == 0 else this(i, p, self.per))
            k.nc.scalar.activation(self.xnT[:, :], bank, ACT.Copy).then_inc(self.xnT_kept, 1)
        src = bank.rearrange("p (b s) -> p b s", b=2)[:, :, 0:S]
        dst = k.x_feat[:, bass.ds(2 * (i * self.per + p), 2), :]
        if self.inner:
            gain, bias = self.inner
            k.nc.scalar.activation(dst, src, ACT.Identity, bias=bias, scale=gain)\
                .then_inc(self.feat_stored, 1)
        else:
            k.nc.scalar.activation(dst, src, ACT.Copy).then_inc(self.feat_stored, 1)


    def tensor_logits(self, pe, i, p, bank):
        pe.wait_ge(self.xnT_kept, this(i, p + 1, self.per))
        pe.matmul(bank, self.xnT[:, :], self.router[:, :], start=True, stop=True).then_inc(self.logits_ready, 1)

    def vector_logits(self, dve, i, p, bank):
        dve.wait_ge(self.logits_ready, this(i, p + 1, self.per))
        self.k.nc.vector.tensor_copy(self.k.logits[:, bass.ds(i * self.per + p, 1), :],
                                     bank.unsqueeze(1)).then_inc(self.logits_kept, 1)


class PairSteps:

    PER = 2

    def __init__(self, **lag):
        self.lag = lag
        self.fill = -(-max(lag.values()) // self.PER) * self.PER

    def count(self, i, s, lag):
        pairs = s - lag + 1
        if isinstance(i, int):
            pairs = max(min(pairs, PAIRS - i * self.PER), -i * self.PER)
        return this(i, pairs, self.PER)

    def pair(self, i, s, stage):
        d = s - self.lag[stage]
        if isinstance(i, int) and not 0 <= i * self.PER + d < PAIRS:
            return None
        return i + d // self.PER, d % self.PER

    def run(self, engine, step):
        PER = self.PER
        for s in range(self.fill):
            step(s // PER, s % PER)
        with engine.Fori(self.fill // PER, PAIRS // PER) as i:
            for s in range(PER):
                step(i, s)
        for s in range(PAIRS, PAIRS + max(self.lag.values())):
            step(s // PER, s % PER)


def self_attention_phase(k):
    nc = k.nc
    HP = H0 // 2
    steps = PairSteps(project=0, scores=1, transpose=2, attend=3, output=4, norm=5)
    PER, pair, n = steps.PER, steps.pair, steps.count
    with ExitStack() as ctx:
        t = Tail(k, ctx, "sa", per=PER)
        sem = lambda name: k.sem(ctx, "sa_" + name)
        xdup = k.sb(ctx, "sa_xdup", [128, PER, 2, 2, S])
        xbo = k.sb(ctx, "sa_xbo", [128, PER, D])
        qs = k.sb(ctx, "sa_qs", [128, PER, 2, SP])
        kf = k.sb(ctx, "sa_kf", [128, PER, 2, S])
        kexp = k.sb(ctx, "sa_kexp", [128, PER, 2, H0, S])
        vexp = k.sb(ctx, "sa_vexp", [2 * S, PER, 2, D])
        sm = k.sb(ctx, "sa_sm", [128, PER, H0, S])
        pr = k.sb(ctx, "sa_pr", [128, PER, H0, S])
        mx = k.sb(ctx, "sa_mx", [128, PER, H0])
        rs = k.sb(ctx, "sa_rs", [128, PER, H0])
        rinv = k.sb(ctx, "sa_rinv", [128, PER, H0])
        prT = k.sb(ctx, "sa_prT", [2 * S, PER, HP, 128])
        on = k.sb(ctx, "sa_on", [128, PER, D])
        oT = k.sb(ctx, "sa_oT", [128, PER, 128])
        psum = ctx.enter_context(nc.psum_tensor("sa_psum", [128, 8, 512], fp32))
        late_weights_loaded = sem("late_weights_loaded")
        qs_zeroed, kq_ready, v_ready = sem("qs_zeroed"), sem("kq_ready"), sem("v_ready")
        q_kept, k_kept, v_kept, xdup_ready = sem("q_kept"), sem("k_kept"), sem("v_kept"), sem("xdup_ready")
        xbo_ready, keys_ready, scores_ready = sem("xbo_ready"), sem("keys_ready"), sem("scores_ready")
        masked, max_ready, shifted = sem("masked"), sem("max_ready"), sem("shifted")
        exp_ready, sum_ready, rinv_ready = sem("exp_ready"), sem("sum_ready"), sem("rinv_ready")
        prT_ready, prT_kept = sem("prT_ready"), sem("prT_kept")
        o_ready, o_kept, oT_ready, oT_kept, y_ready = sem("o_ready"), sem("o_kept"), sem("oT_ready"), sem("oT_kept"), sem("y_ready")
        block = ctx.enter_context(nc.Block())

        @block.sync
        def _(sp):
            for name, dst in k.late_loads:
                sp.dma_start(dst, k.dram[name]).then_inc(late_weights_loaded, 16)
            for p in range(2):
                sp.dma_start(k.ctxT[:, p, :, :], k.dram["ctxT"][2 * p:2 * p + 2, :, :].rearrange("b d c -> d b c"))\
                    .then_inc(k.ctxT_loaded[p], 16)
                sp.dma_start(k.ctxN[:, p, :, :], k.dram["ctxN"][2 * p:2 * p + 2, :, :, :].rearrange("b q t d -> q b (t d)"))\
                    .then_inc(k.ctxN_loaded[p], 16)
            sp.wait_ge(late_weights_loaded, 16 * len(k.late_loads))

        @block.gpsimd
        def _(pool):
            open_sems(pool, PER, xbo_ready, keys_ready)
            t.open_pool(pool)

            def step(i, s):
                at = pair(i, s, "norm")
                if at:
                    t.pool_store(pool, *at)
                at = pair(i, s, "project")
                if at:
                    j, p = at
                    pool.wait_ge(k_kept, this(j, p + 1, PER))
                    pool.wait_ge(scores_ready, last(j, p + 1, PER))
                    for half in range(2):
                        done = pool.tensor_tensor(kexp[:, p, half, :, :],
                                                  kf[:, p, half, :].unsqueeze(1).to_broadcast([128, H0, S]),
                                                  k.head_mask[:, :].unsqueeze(2).to_broadcast([128, H0, S]), ALU.mult)
                    done.then_inc(keys_ready, 1)
                at = pair(i, s, "attend")
                if at:
                    j, p = at
                    pool.wait_ge(t.r_ready, last(j, p + 1, PER))
                    pool.tensor_tensor(xbo[:, p:p + 1, :], k.x_tok[:, bass.ds(j * PER + p, 1), :],
                                       k.bo_row0[:, :].unsqueeze(1), ALU.add).then_inc(xbo_ready, 1)
                at = pair(i, s, "output")
                if at:
                    t.pool_rstd(pool, *at)

            steps.run(pool, step)

        @block.tensor
        def _(pe):
            open_sems(pe, PER, kq_ready, v_ready, scores_ready, prT_ready, o_ready, oT_ready, y_ready)
            t.open_tensor(pe)
            pe.wait_ge(qs_zeroed, 1)

            def step(i, s):
                at = pair(i, s, "project")
                if at:
                    j, p = at
                    x = k.x_feat[:, bass.ds(2 * (j * PER + p), 2), :]
                    pe.wait_ge(q_kept, this(j, p, PER))
                    nc.tensor.matmul(psum[:, 3, 0:2 * S], k.wkT0[:, :], x, start=True, stop=True)
                    nc.tensor.matmul(psum[:, 3, 2 * S:4 * S], k.wqT0[:, :], x, start=True, stop=True).then_inc(kq_ready, 1)
                at = pair(i, s, "scores")
                if at:
                    j, p = at
                    pe.wait_ge(q_kept, this(j, p + 1, PER))
                    pe.wait_ge(keys_ready, this(j, p + 1, PER))
                    pe.wait_ge(masked, this(j, p, PER))
                    for half in range(2):
                        for hh in range(2):
                            done = nc.tensor.matmul(psum[half * SP:(half + 1) * SP, hh, 0:8 * S], qs[:, p, half, :],
                                                    kexp[:, p, half, hh * 8:(hh + 1) * 8, :], start=True, stop=True)
                    done.then_inc(scores_ready, 1)
                at = pair(i, s, "output")
                if at:
                    j, p = at
                    pe.wait_ge(o_kept, this(j, p + 1, PER))
                    pe.wait_ge(t.r_ready, this(j, p, PER))
                    nc.tensor.transpose(psum[:, 7, 0:128], on[:, p, :], k.ident[:, :]).then_inc(oT_ready, 1)
                at = pair(i, s, "transpose")
                if at:
                    j, p = at
                    pe.wait_ge(exp_ready, this(j, p + 1, PER))
                    pe.wait_ge(prT_kept, this(j, p, PER))
                    for hp in range(HP):
                        done = nc.tensor.transpose(psum[0:2 * S, 4 + hp // 4, (hp % 4) * 128:(hp % 4 + 1) * 128],
                                                   pr[:, p, 2 * hp:2 * hp + 2, :], k.ident[:, :])
                    done.then_inc(prT_ready, 1)
                    pe.wait_ge(xdup_ready, this(j, p + 1, PER))
                    pe.wait_ge(v_kept, this(j, p, PER))
                    for half in range(2):
                        done = nc.tensor.matmul(psum[0:2 * S, 2, half * D:(half + 1) * D],
                                                xdup[:, p, half, :, :], k.wvT0[:, :], start=True, stop=True)
                    done.then_inc(v_ready, 1)
                at = pair(i, s, "norm")
                if at:
                    pe.wait_ge(oT_kept, n(i, s, 4))
                    pe.wait_ge(t.r_ready, n(i, s, 5))
                    t.tensor_transpose(pe, *at, psum[:, 7, 256:384])
                at = pair(i, s, "output")
                if at:
                    j, p = at
                    pe.wait_ge(oT_kept, this(j, p + 1, PER))
                    pe.wait_ge(t.feat_stored, n(i, s, 5))
                    nc.tensor.matmul(psum[:, 7, 128:256], oT[:, p, :], k.woT0[:, :], start=True, stop=True)\
                        .then_inc(y_ready, 1)
                at = pair(i, s, "attend")
                if at:
                    j, p = at
                    pe.wait_ge(prT_kept, this(j, p + 1, PER))
                    pe.wait_ge(v_kept, this(j, p + 1, PER))
                    pe.wait_ge(o_kept, this(j, p, PER))
                    for half in range(2):
                        for hp in range(HP):
                            done = nc.tensor.matmul(psum[half * SP:(half + 1) * SP, 6, hp * 16:(hp + 1) * 16],
                                                    prT[:, p, hp, half * SP:(half + 1) * SP],
                                                    vexp[:, p, half, hp * 16:(hp + 1) * 16], start=True, stop=True)
                    done.then_inc(o_ready, 1)

            steps.run(pe, step)

        @block.vector
        def _(dve):
            open_sems(dve, PER, masked, max_ready, shifted, sum_ready, rinv_ready, o_kept, v_kept)
            t.open_vector(dve)
            dve.memset(qs[:, :, :, :], 0.0).then_inc(qs_zeroed, 1)

            def step(i, s):
                at = pair(i, s, "norm")
                if at:
                    t.vector_normalise(dve, *at)
                at = pair(i, s, "scores")
                if at:
                    j, p = at
                    dve.wait_ge(scores_ready, this(j, p + 1, PER))
                    dve.wait_ge(exp_ready, last(j, p + 1, PER))
                    nc.vector.tensor_tensor(sm[:, p, :, :].rearrange("p (a h) s -> p a h s", a=2),
                                            psum[:, 0:2, 0:8 * S].rearrange("p a (h s) -> p a h s", h=8),
                                            k.window_mask[:, :].unsqueeze(1).unsqueeze(1)
                                            .to_broadcast([128, 2, 8, S]), ALU.add).then_inc(masked, 1)
                    dve.wait_ge(masked, this(j, p + 1, PER))
                    nc.vector.reduce_max(mx[:, p, :], sm[:, p, :, :], AX.X).then_inc(max_ready, 1)
                    dve.wait_ge(max_ready, this(j, p + 1, PER))
                    nc.vector.tensor_tensor(sm[:, p, :, :], sm[:, p, :, :],
                                            mx[:, p, :].unsqueeze(2).to_broadcast([128, H0, S]),
                                            ALU.subtract).then_inc(shifted, 1)
                at = pair(i, s, "transpose")
                if at:
                    j, p = at
                    dve.wait_ge(exp_ready, this(j, p + 1, PER))
                    nc.vector.reduce_sum(rs[:, p, :], pr[:, p, :, :], AX.X).then_inc(sum_ready, 1)
                    dve.wait_ge(sum_ready, this(j, p + 1, PER))
                    nc.vector.reciprocal(rinv[:, p, :], rs[:, p, :]).then_inc(rinv_ready, 1)
                    dve.wait_ge(v_ready, this(j, p + 1, PER))
                    dve.wait_ge(o_ready, last(j, p + 1, PER))
                    nc.vector.tensor_tensor(vexp[:, p, :, :],
                                            psum[0:2 * S, 2, 0:2 * D].rearrange("p (b d) -> p b d", b=2),
                                            k.value_mask[0:2 * S, :, :, :].rearrange("p a c j -> p (a c j)")
                                            .unsqueeze(1).to_broadcast([2 * S, 2, D]), ALU.mult).then_inc(v_kept, 1)
                at = pair(i, s, "output")
                if at:
                    j, p = at
                    dve.wait_ge(y_ready, this(j, p + 1, PER))
                    dve.wait_ge(xbo_ready, this(j, p + 1, PER))
                    nc.vector.tensor_tensor(t.r[:, p, :], psum[:, 7, 128:256], xbo[:, p, :], ALU.add)\
                        .then_inc(t.r_ready, 1)
                    t.vector_moments(dve, j, p)
                at = pair(i, s, "attend")
                if at:
                    j, p = at
                    dve.wait_ge(rinv_ready, this(j, p + 1, PER))
                    dve.wait_ge(o_ready, this(j, p + 1, PER))
                    dve.wait_ge(oT_ready, last(j, p + 1, PER))
                    nc.vector.tensor_tensor(on[:, p, :].rearrange("p (h d) -> p h d", h=H0),
                                            psum[:, 6, 0:128].rearrange("p (h d) -> p h d", h=H0),
                                            rinv[:, p, :].unsqueeze(2).to_broadcast([128, H0, DH0]),
                                            ALU.mult).then_inc(o_kept, 1)

            steps.run(dve, step)

        @block.scalar
        def _(act):
            open_sems(act, PER, exp_ready, prT_kept, oT_kept, k_kept, q_kept, xdup_ready)
            t.open_scalar(act)
            act.wait_ge(qs_zeroed, 1)

            def step(i, s):
                at = pair(i, s, "project")
                if at:
                    j, p = at
                    act.wait_ge(kq_ready, this(j, p + 1, PER))
                    act.wait_ge(keys_ready, last(j, p + 1, PER))
                    nc.scalar.activation(kf[:, p, :, :], psum[:, 3, 0:2 * S].rearrange("p (b s) -> p b s", b=2),
                                         ACT.Identity, bias=k.bk0[:, :]).then_inc(k_kept, 1)
                    act.wait_ge(scores_ready, last(j, p + 1, PER))
                    nc.scalar.activation(qs[:, p, :, 0:S], psum[:, 3, 2 * S:4 * S].rearrange("p (b s) -> p b s", b=2),
                                         ACT.Identity, bias=k.bq0_scaled[:, :], scale=DH0 ** -0.5).then_inc(q_kept, 1)
                at = pair(i, s, "output")
                if at:
                    j, p = at
                    act.wait_ge(oT_ready, this(j, p + 1, PER))
                    act.wait_ge(y_ready, last(j, p + 1, PER))
                    nc.scalar.activation(oT[:, p, :], psum[:, 7, 0:128], ACT.Identity, bias=k.bv0[:, :])\
                        .then_inc(oT_kept, 1)
                at = pair(i, s, "scores")
                if at:
                    j, p = at
                    act.wait_ge(v_ready, last(j, p + 1, PER))
                    nc.scalar.activation(xdup[:, p, :, :, :], k.x_feat[:, bass.ds(2 * (j * PER + p), 2), :]
                                         .unsqueeze(2).to_broadcast([128, 2, 2, S]), ACT.Copy).then_inc(xdup_ready, 1)
                at = pair(i, s, "transpose")
                if at:
                    j, p = at
                    act.wait_ge(prT_ready, this(j, p + 1, PER))
                    act.wait_ge(o_ready, last(j, p + 1, PER))
                    nc.scalar.activation(prT[:, p, :, :].rearrange("p (a h) s -> p a (h s)", a=2),
                                         psum[0:2 * S, 4:6, :], ACT.Copy).then_inc(prT_kept, 1)
                at = pair(i, s, "norm")
                if at:
                    t.scalar_store(act, *at, psum[:, 7, 256:384])
                at = pair(i, s, "scores")
                if at:
                    j, p = at
                    act.wait_ge(shifted, this(j, p + 1, PER))
                    act.wait_ge(prT_ready, last(j, p + 1, PER))
                    act.wait_ge(sum_ready, last(j, p + 1, PER))
                    nc.scalar.activation(pr[:, p, :, :], sm[:, p, :, :], ACT.Exp).then_inc(exp_ready, 1)

            steps.run(act, step)


def context_attention_phase(k):
    nc = k.nc
    Q4 = C // 4
    steps = PairSteps(project=0, scores=1, transpose=2, values=3, output=4, norm=5)
    PER, pair, n = steps.PER, steps.pair, steps.count
    with ExitStack() as ctx:
        t = Tail(k, ctx, "ca", router=k.router0, per=PER)
        sem = lambda name: k.sem(ctx, "ca_" + name)
        qp = k.sb(ctx, "ca_qp", [128, 2, S])
        qk = k.sb(ctx, "ca_qk", [128, 2, 2, SP])
        ctxT, ctxN, ctxT_loaded, ctxN_loaded = k.ctxT, k.ctxN, k.ctxT_loaded, k.ctxN_loaded
        pr = k.sb(ctx, "ca_pr", [128, 2, C])
        prT = k.sb(ctx, "ca_prT", [KP, 2, KT, 128])
        negmax = k.sb(ctx, "ca_negmax", [128, 2, 1])
        rs = k.sb(ctx, "ca_rs", [128, 2, 1])
        rinv = k.sb(ctx, "ca_rinv", [128, 2, 1])
        xb = k.sb(ctx, "ca_xb", [128, 2, D])
        oT = k.sb(ctx, "ca_oT", [128, 2, 128])
        vT = k.sb(ctx, "ca_vT", [128, 2, 128])
        psum = ctx.enter_context(nc.psum_tensor("ca_psum", [128, 8, 512], fp32))
        qk_zeroed, qp_ready, qp_kept, qk_ready, qk_kept = sem("qk_zeroed"), sem("qp_ready"), sem("qp_kept"), sem("qk_ready"), sem("qk_kept")
        scores_ready, max_ready, exp_ready, rinv_ready = sem("scores_ready"), sem("max_ready"), sem("exp_ready"), sem("rinv_ready")
        prT_ready, even_kept, odd_kept = sem("prT_ready"), sem("even_kept"), sem("odd_kept")
        pv_ready, oT_kept, vT_ready, vT_kept, y_ready, xb_ready = (
            sem("pv_ready"), sem("oT_kept"), sem("vT_ready"), sem("vT_kept"), sem("y_ready"), sem("xb_ready"))
        k.used += k.context_semaphores
        block = ctx.enter_context(nc.Block())

        @block.sync
        def _(sp):
            def load_T(i, p):
                sp.wait_ge(scores_ready, last(i, p + 1, PER))
                sp.dma_start(ctxT[:, p, :, :],
                             k.dram["ctxT"][bass.ds(4 * i + 2 * p, 2), :, :].rearrange("b d c -> d b c"))\
                    .then_inc(ctxT_loaded[p], 16)

            def load_N(i, p):
                sp.wait_ge(pv_ready, last(i, p + 1, PER))
                sp.dma_start(ctxN[:, p, :, :],
                             k.dram["ctxN"][bass.ds(4 * i + 2 * p, 2), :, :, :].rearrange("b q t d -> q b (t d)"))\
                    .then_inc(ctxN_loaded[p], 16)

            for p in range(PER):
                load_T(1, p)
            with sp.Fori(1, PAIRS // PER - 1) as i:
                for p in range(PER):
                    load_T(i + 1, p)
                    load_N(i, p)
            for p in range(PER):
                load_N(PAIRS // PER - 1, p)

        @block.gpsimd
        def _(pool):
            open_sems(pool, PER, xb_ready)
            t.open_pool(pool)

            def step(i, s):
                at = pair(i, s, "norm")
                if at:
                    t.pool_store(pool, *at)
                at = pair(i, s, "values")
                if at:
                    j, p = at
                    pool.wait_ge(t.r_ready, last(j, p + 1, PER))
                    pool.tensor_tensor(xb[:, p:p + 1, :], k.x_tok[:, bass.ds(j * PER + p, 1), :],
                                       k.cross_row[:, :].unsqueeze(1), ALU.add).then_inc(xb_ready, 1)
                at = pair(i, s, "output")
                if at:
                    t.pool_rstd(pool, *at)

            steps.run(pool, step)

        @block.tensor
        def _(pe):
            open_sems(pe, PER, qp_ready, qk_ready, scores_ready, pv_ready, vT_ready, y_ready)
            open_sems(pe, 3 * PER, prT_ready)
            t.open_tensor(pe)
            pe.wait_ge(qk_zeroed, 1)

            def transposes(j, p, r):
                for c in range(4):
                    kt = 4 * r + c
                    done = nc.tensor.transpose(psum[0:KP, 4 + r % 2, c * 128:(c + 1) * 128],
                                               pr[:, p, kt * KP:(kt + 1) * KP], k.ident[:, :])
                done.then_inc(prT_ready, 1)

            def step(i, s):
                at = pair(i, s, "project")
                if at:
                    j, p = at
                    pe.wait_ge(qk_kept, n(i, s, 1))
                    pe.wait_ge(t.logits_kept, n(i, s, 6))
                    pe.wait_ge(t.r_ready, n(i, s, 5))
                    nc.tensor.matmul(psum[:, 7, 0:2 * S], k.wqT0x[:, :], k.x_feat[:, bass.ds(2 * (j * PER + p), 2), :],
                                     start=True, stop=True).then_inc(qp_ready, 1)
                at = pair(i, s, "output")
                if at:
                    j, p = at
                    pe.wait_ge(oT_kept, this(j, p + 1, PER))
                    pe.wait_ge(qp_kept, n(i, s, 0))
                    pe.wait_ge(t.logits_kept, n(i, s, 6))
                    nc.tensor.matmul(psum[:, 7, 0:128], k.wvT0x[:, :], oT[:, p, :], start=True, stop=True)\
                        .then_inc(vT_ready, 1)
                at = pair(i, s, "scores")
                if at:
                    j, p = at
                    pe.wait_ge(qk_kept, this(j, p + 1, PER))
                    pe.wait_ge(ctxT_loaded[p], (j + 1) * 16)
                    pe.wait_ge(exp_ready, this(j, p, PER))
                    for half in range(2):
                        for c in range(4):
                            done = nc.tensor.matmul(psum[half * SP:(half + 1) * SP, c, 0:Q4], qk[:, p, half, :],
                                                    ctxT[:, p, half, c * Q4:(c + 1) * Q4], start=True, stop=True)
                    done.then_inc(scores_ready, 1)
                at = pair(i, s, "norm")
                if at:
                    pe.wait_ge(qp_kept, n(i, s, 0))
                    pe.wait_ge(vT_kept, n(i, s, 4))
                    t.tensor_transpose(pe, *at, psum[:, 7, 256:384])
                at = pair(i, s, "transpose")
                if at:
                    j, p = at
                    pe.wait_ge(exp_ready, this(j, p + 1, PER))
                    pe.wait_ge(even_kept, this(j, 2 * p, 2 * PER))
                    transposes(j, p, 0)
                    pe.wait_ge(odd_kept, this(j, p, PER))
                    transposes(j, p, 1)
                at = pair(i, s, "project")
                if at:
                    j, p = at
                    pe.wait_ge(qp_kept, this(j, p + 1, PER))
                    pe.wait_ge(vT_kept, n(i, s, 4))
                    pe.wait_ge(t.feat_stored, n(i, s, 5))
                    nc.tensor.matmul(psum[:, 7, 0:2 * S], k.wk0x[:, :], qp[:, :, :], start=True, stop=True)\
                        .then_inc(qk_ready, 1)
                at = pair(i, s, "output")
                if at:
                    j, p = at
                    pe.wait_ge(vT_kept, this(j, p + 1, PER))
                    pe.wait_ge(qk_kept, n(i, s, 0))
                    pe.wait_ge(t.feat_stored, n(i, s, 5))
                    nc.tensor.matmul(psum[:, 7, 128:256], vT[:, p, :], k.woT0x[:, :], start=True, stop=True)\
                        .then_inc(y_ready, 1)
                at = pair(i, s, "values")
                if at:
                    j, p = at
                    pe.wait_ge(ctxN_loaded[p], (j + 1) * 16)
                    pe.wait_ge(even_kept, this(j, 2 * p + 2, 2 * PER))
                    pe.wait_ge(odd_kept, this(j, p + 1, PER))
                    pe.wait_ge(oT_kept, this(j, p, PER))
                    for half in range(2):
                        for kt in range(KT):
                            done = nc.tensor.matmul(psum[:, 6, half * SP:(half + 1) * SP], ctxN[:, p, half, kt * D:(kt + 1) * D],
                                                    prT[:, p, kt, half * SP:(half + 1) * SP],
                                                    start=(kt == 0), stop=(kt == KT - 1))
                    done.then_inc(pv_ready, 1)
                at = pair(i, s, "norm")
                if at:
                    pe.wait_ge(t.feat_stored, n(i, s, 5))
                    pe.wait_ge(t.r_ready, n(i, s, 4))
                    pe.wait_ge(qk_kept, n(i, s, 0))
                    t.tensor_logits(pe, *at, psum[:, 7, 384:384 + E])
                at = pair(i, s, "transpose")
                if at:
                    j, p = at
                    pe.wait_ge(even_kept, this(j, 2 * p + 1, 2 * PER))
                    transposes(j, p, 2)

            steps.run(pe, step)

        @block.vector
        def _(dve):
            open_sems(dve, PER, max_ready, rinv_ready, vT_kept, qp_kept)
            open_sems(dve, 2 * PER, even_kept)
            t.open_vector(dve)
            dve.memset(qk[:, :, :, :], 0.0).then_inc(qk_zeroed, 1)

            def step(i, s):
                at = pair(i, s, "project")
                if at:
                    j, p = at
                    dve.wait_ge(qp_ready, this(j, p + 1, PER))
                    dve.wait_ge(qk_ready, this(j, p, PER))
                    nc.vector.tensor_scalar(qp[:, :, :].rearrange("p b s -> p (b s)"), psum[:, 7, 0:2 * S], k.bq0x[:, :],
                                            D ** -0.5, ALU.add, ALU.mult).then_inc(qp_kept, 1)
                at = pair(i, s, "output")
                if at:
                    j, p = at
                    dve.wait_ge(vT_ready, this(j, p + 1, PER))
                    dve.wait_ge(y_ready, last(j, p + 1, PER))
                    nc.vector.tensor_copy(vT[:, p, :], psum[:, 7, 0:128]).then_inc(vT_kept, 1)
                at = pair(i, s, "norm")
                if at:
                    t.vector_normalise(dve, *at)
                at = pair(i, s, "scores")
                if at:
                    j, p = at
                    dve.wait_ge(scores_ready, this(j, p + 1, PER))
                    nc.vector.tensor_reduce(negmax[:, p, :], psum[:, 0:4, 0:Q4], AX.XY, ALU.max, negate=True)\
                        .then_inc(max_ready, 1)
                at = pair(i, s, "transpose")
                if at:
                    j, p = at
                    dve.wait_ge(prT_ready, this(j, 3 * p + 1, 3 * PER))
                    dve.wait_ge(pv_ready, last(j, p + 1, PER))
                    nc.vector.tensor_copy(prT[:, p, 0:4, :].rearrange("p a b -> p (a b)"), psum[0:KP, 4, :])\
                        .then_inc(even_kept, 1)
                at = pair(i, s, "output")
                if at:
                    j, p = at
                    dve.wait_ge(y_ready, this(j, p + 1, PER))
                    dve.wait_ge(xb_ready, this(j, p + 1, PER))
                    nc.vector.scalar_tensor_tensor(t.r[:, p, :], psum[:, 7, 128:256], rinv[:, p, :], xb[:, p, :],
                                                   ALU.mult, ALU.add).then_inc(t.r_ready, 1)
                    t.vector_moments(dve, j, p)
                at = pair(i, s, "norm")
                if at:
                    t.vector_logits(dve, *at, psum[:, 7, 384:384 + E])
                at = pair(i, s, "transpose")
                if at:
                    j, p = at
                    dve.wait_ge(t.r_ready, last(j, p + 1, PER))
                    dve.wait_ge(exp_ready, this(j, p + 1, PER))
                    nc.vector.reciprocal(rinv[:, p, :], rs[:, p, :]).then_inc(rinv_ready, 1)
                    dve.wait_ge(prT_ready, this(j, 3 * p + 3, 3 * PER))
                    nc.vector.tensor_copy(prT[:, p, 8:12, :].rearrange("p a b -> p (a b)"), psum[0:KP, 4, :])\
                        .then_inc(even_kept, 1)

            steps.run(dve, step)

        @block.scalar
        def _(act):
            open_sems(act, PER, exp_ready, odd_kept, oT_kept, qk_kept)
            t.open_scalar(act)
            act.wait_ge(qk_zeroed, 1)

            def step(i, s):
                at = pair(i, s, "norm")
                if at:
                    t.scalar_store(act, *at, psum[:, 7, 256:384])
                at = pair(i, s, "transpose")
                if at:
                    j, p = at
                    act.wait_ge(prT_ready, this(j, 3 * p + 2, 3 * PER))
                    act.wait_ge(pv_ready, last(j, p + 1, PER))
                    nc.scalar.activation(prT[:, p, 4:8, :].rearrange("p a b -> p (a b)"), psum[0:KP, 5, :],
                                         ACT.Copy).then_inc(odd_kept, 1)
                at = pair(i, s, "project")
                if at:
                    j, p = at
                    act.wait_ge(qk_ready, this(j, p + 1, PER))
                    act.wait_ge(scores_ready, last(j, p + 1, PER))
                    nc.scalar.activation(qk[:, p, :, 0:S], psum[:, 7, 0:2 * S].rearrange("p (b s) -> p b s", b=2),
                                         ACT.Copy).then_inc(qk_kept, 1)
                at = pair(i, s, "scores")
                if at:
                    j, p = at
                    act.wait_ge(max_ready, this(j, p + 1, PER))
                    act.wait_ge(prT_ready, last(j, 3 * p + 3, 3 * PER))
                    act.wait_ge(rinv_ready, last(j, p + 1, PER))
                    nc.scalar.activation(pr[:, p, :].rearrange("p (a c) -> p a c", a=4), psum[:, 0:4, 0:Q4],
                                         ACT.Exp, bias=negmax[:, p, :], accum_out=rs[:, p, :]).then_inc(exp_ready, 1)
                at = pair(i, s, "values")
                if at:
                    j, p = at
                    act.wait_ge(pv_ready, this(j, p + 1, PER))
                    act.wait_ge(vT_ready, last(j, p + 1, PER))
                    nc.scalar.activation(oT[:, p, :], psum[:, 6, 0:128], ACT.Copy).then_inc(oT_kept, 1)

            steps.run(act, step)


def routing_phase(k, layer):
    nc = k.nc
    with ExitStack() as ctx:
        sem = lambda name: k.sem(ctx, f"route{layer}_{name}")
        sb = lambda name, shape, dt=fp32: k.sb(ctx, f"route{layer}_{name}", shape, dt)
        best = sb("best", [128, PAIRS, 8])
        index_u = sb("index_u", [128, PAIRS, 8], u32)
        index = sb("index", [128, PAIRS, 2])
        gap, e2, total, inv, w2 = (sb(x, [128, PAIRS, 1]) for x in ("gap", "e2", "total", "inv", "w2"))
        hot = sb("hot", [128, PAIRS, E])
        first = sb("first", [128, PAIRS, E])
        biased = sb("biased", [128, PAIRS, E])
        step_done, exp_ready, biased_ready, gap_ready = sem("step_done"), sem("exp_ready"), sem("biased_ready"), sem("gap_ready")
        fold_loaded, fold_ready, fold_kept = sem("fold_loaded"), sem("fold_ready"), sem("fold_kept")
        psum = ctx.enter_context(nc.psum_tensor(f"route{layer}_psum", [128, 8, 512], fp32))
        high_kept, low_kept, down_low_kept = {name: sem(name + "_high_kept") for name in k.parts}, sem("low_kept"), sem("down_low_kept")
        block = ctx.enter_context(nc.Block())
        FOLDS = 2 * H1 // 4 if layer == 0 else 0
        if layer == 0:
            wqT1, wkT1, wvT1, wo1 = (sb(x, [2 * DH1, H1 // 2, D]) for x in ("wqT1", "wkT1", "wvT1", "wo1"))
            fold_loads = ("L1_wqT", wqT1), ("L1_wkT", wkT1), ("L1_wvT", wvT1), ("L1_wo", wo1)
        NE = E if layer == 0 else E + 1
        if layer == 1:
            loaded = {name: sem(name + "_loaded") for name in k.expert_loads}

        def split_ready(engine, name):
            if layer == 1:
                engine.wait_ge(loaded[name], 16 * len(k.expert_loads[name]))

        flat = lambda v: v.rearrange("p a b -> p (a b)") if len(v.shape) == 3 else v

        @block.sync
        def _(sp):
            if layer == 0:
                for name, dst in fold_loads:
                    sp.dma_start(dst[:, :, :], k.dram[name]).then_inc(fold_loaded, 16)
                return
            for name, loads in k.expert_loads.items():
                for array, dst in loads:
                    sp.dma_start(dst, k.dram[array]).then_inc(loaded[name], 16)

        wide = lambda v: v.to_broadcast([128, PAIRS, E])
        experts = k.expert_index[:, :].unsqueeze(1).to_broadcast([128, PAIRS, E])

        @block.gpsimd
        def _(pool):
            n = 0
            for name, (source, high, low) in k.parts.items():
                split_ready(pool, name)
                if name == "down":
                    continue
                for e in range(NE):
                    n += 1
                    pool.wait_ge(high_kept[name], e + 1)
                    pool.tensor_tensor(flat(low[:, e]), flat(source[:, e]), flat(high[:, e]).bitcast(fp32), ALU.subtract)\
                        .then_inc(low_kept, 1)
            pool.wait_ge(low_kept, n)

        @block.vector
        def _(dve):
            n = 0

            def step(instruction):
                nonlocal n
                n += 1
                instruction.then_inc(step_done, 1)
                dve.wait_ge(step_done, n)

            values = k.logits
            if layer == 1:
                nc.vector.tensor_tensor(biased[:, :, :], k.logits[:, :, :],
                                        k.router_bias_row1[:, :].unsqueeze(1).to_broadcast([128, PAIRS, E]),
                                        ALU.add).then_inc(biased_ready, 1)
                dve.wait_ge(exp_ready, 1)
                values = first
            for g in range(PAIRS):
                last_max = nc.vector.max(best[:, g, :], values[:, g, :])
            step(last_max)
            for g in range(PAIRS):
                last_index = nc.vector.max_index(index_u[:, g, :], best[:, g, :], values[:, g, :])
            step(last_index)
            step(nc.vector.tensor_copy(index[:, :, :], index_u[:, :, 0:2]))
            if layer == 0:
                nc.vector.tensor_tensor(gap[:, :, :], best[:, :, 1:2], best[:, :, 0:1], ALU.subtract).then_inc(gap_ready, 1)
                dve.wait_ge(exp_ready, 1)
                step(nc.vector.tensor_scalar(total[:, :, :], e2[:, :, :], 1.0, None, ALU.add))
                step(nc.vector.reciprocal(inv[:, :, :], total[:, :, :]))
                w1 = inv
                step(nc.vector.tensor_tensor(w2[:, :, :], e2[:, :, :], inv[:, :, :], ALU.mult))
            else:
                step(nc.vector.tensor_tensor(total[:, :, :], best[:, :, 1:2], best[:, :, 0:1], ALU.add))
                step(nc.vector.reciprocal(inv[:, :, :], total[:, :, :]))
                w1 = gap
                step(nc.vector.tensor_tensor(gap[:, :, :], best[:, :, 0:1], inv[:, :, :], ALU.mult))
                step(nc.vector.tensor_tensor(w2[:, :, :], best[:, :, 1:2], inv[:, :, :], ALU.mult))
            step(nc.vector.tensor_tensor(hot[:, :, :], experts, wide(index[:, :, 0:1]), ALU.is_equal))
            step(nc.vector.tensor_tensor(biased[:, :, :], hot[:, :, :], wide(w1[:, :, :]), ALU.mult))
            step(nc.vector.tensor_tensor(hot[:, :, :], experts, wide(index[:, :, 1:2]), ALU.is_equal))
            step(nc.vector.tensor_tensor(first[:, :, :], hot[:, :, :], wide(w2[:, :, :]), ALU.mult))
            step(nc.vector.tensor_tensor(k.expert_weights[:, :, :], biased[:, :, :], first[:, :, :], ALU.add))
            source, high, low = k.parts["down"]
            split_ready(dve, "down")
            for e in range(NE):
                dve.wait_ge(high_kept["down"], e + 1)
                nc.vector.tensor_tensor(flat(low[:, e]), flat(source[:, e]), flat(high[:, e]).bitcast(fp32), ALU.subtract)\
                    .then_inc(down_low_kept, 1)

        @block.tensor
        def _(pe):
            if FOLDS:
                pe.wait_ge(fold_loaded, 16 * len(fold_loads))
            for g in range(FOLDS):
                a, b = (wqT1, wkT1) if g < FOLDS // 2 else (wvT1, wo1)
                for j in range(4):
                    h = 4 * (g % (FOLDS // 2)) + j
                    rows, h = slice(h // 8 * DH1, (h // 8 + 1) * DH1), h % 8
                    done = nc.tensor.matmul(psum[:, g, j * D:(j + 1) * D], a[rows, h, :], b[rows, h, :], start=True, stop=True)
                done.then_inc(fold_ready, 1)

        @block.scalar
        def _(act):
            if layer == 1:
                act.wait_ge(biased_ready, 1)
                nc.scalar.activation(first[:, :, :], biased[:, :, :], ACT.Sigmoid).then_inc(exp_ready, 1)
            else:
                act.wait_ge(gap_ready, 1)
                nc.scalar.activation(e2[:, :, :], gap[:, :, :], ACT.Exp).then_inc(exp_ready, 1)
            for name, (source, high, low) in k.parts.items():
                split_ready(act, name)
                for e in range(NE):
                    nc.scalar.activation(high[:, e], source[:, e], ACT.Copy).then_inc(high_kept[name], 1)
            for g in range(FOLDS):
                dst = k.key_query if g < FOLDS // 2 else k.value_out
                h = 4 * (g % (FOLDS // 2))
                act.wait_ge(fold_ready, g + 1)
                nc.scalar.activation(dst[:, h:h + 4, :], psum[:, g, :].rearrange("p (h n) -> p h n", h=4), ACT.Copy)\
                    .then_inc(fold_kept, 1)


def expert_phase(k, layer):
    nc = k.nc
    HT = (U0 if layer == 0 else I1) // 128
    NE = E if layer == 0 else E + 1
    part_of = lambda name, e, cols: [v[:, e, cols] for v in k.parts[name][1:]]
    with ExitStack() as ctx:
        tag = f"moe{layer}"
        inner = (k.ln_g1[:, :], k.ln_b1[:, :]) if layer == 0 else None
        final = layer == 1
        t = Tail(k, ctx, tag, inner=inner, final=final)
        sem = lambda name: k.sem(ctx, f"{tag}_{name}")
        sb = lambda name, shape, dt=fp32: k.sb(ctx, f"{tag}_{name}", shape, dt)
        x_hi, x_lo = sb("x_hi", [128, CT], fp32r), sb("x_lo", [128, CT], fp32r)
        wc = sb("wc", [128, CK, E])
        spread = sb("spread", [128, 3, CT])
        hid = sb("hid", [128, 2, CT])
        hid_hi, hid_lo = sb("hid_hi", [128, 2, HT, CT], fp32r), sb("hid_lo", [128, 2, HT, CT], fp32r)
        act_out = sb("act_out", [128, 2, CT])
        part = sb("part", [128, 2, CT])
        acc = sb("acc", [128, CB, S])
        mixed = sb("mixed", [128, CB, SP])
        psum = ctx.enter_context(nc.psum_tensor(f"{tag}_psum", [128, 8, 512], fp32))
        mixed_zeroed, x_hi_ready, x_lo_ready, wc_ready, spread_ready, spread_kept = (
            sem("mixed_zeroed"), sem("x_hi_ready"), sem("x_lo_ready"), sem("wc_ready"), sem("spread_ready"), sem("spread_kept"))
        up_ready, hid_ready, silu_ready, down_ready, part_ready, acc_ready, y_ready = (
            sem("up_ready"), sem("hid_ready"), sem("silu_ready"), sem("down_ready"), sem("part_ready"),
            sem("acc_ready"), sem("y_ready"))
        out_stored, hi_ready, lo_ready = sem("out_stored"), sem("hi_ready"), sem("lo_ready")
        block = ctx.enter_context(nc.Block())

        def run(engine, chunk, tail):
            chunk(0, lambda e, at: None, first=True)
            with engine.Fori(1, CHUNKS - 1) as i:
                chunk(i, lambda e, at: tail(i - 1, e, at))
            chunk(CHUNKS - 1, lambda e, at: tail(CHUNKS - 2, e, at), end=True)
            for e in range(1, CK + 3):
                for at in range(3):
                    tail(CHUNKS - 1, e, at, after=True)

        n = lambda i, p: this(i, p + 1, CK)
        b = lambda i, p: last(i, p + 1, CK)
        NT = NE * HT

        def slot(i, e):
            if e >= 2:
                return this(i, e - 1, NE)
            return last(i, NE if (NE - 1) % 2 == e else NE - 1, NE)

        def hid_tile(i, j, back=0):
            return this(i, j + 1 - back, NT) if j >= back else last(i, NT + j + 1 - back, NT)

        @block.gpsimd
        def _(pool):
            open_sems(pool, 1, wc_ready)
            open_sems(pool, NE - 1, acc_ready)
            t.open_pool(pool)
            pool.memset(mixed[:, :, :], 0.0).then_inc(mixed_zeroed, 1)
            pool.wait_ge(mixed_zeroed, 1)

            def chunk(i, tail, first=False, end=False):
                pool.wait_ge(spread_ready, last(i, E, E))
                pool.tensor_copy(wc[:, :, :], k.expert_weights[:, bass.ds(i * CK, CK), :]).then_inc(wc_ready, 1)
                tail(1, 1)
                for e in range(1, NE):
                    pool.wait_ge(part_ready, this(i, e + 1, NE))
                    if e > 1:
                        pool.wait_ge(acc_ready, this(i, e - 1, NE - 1))
                    total = acc[:, :, :]
                    if e == NE - 1:
                        pool.wait_ge(y_ready, b(i, CK - 1))
                        total = mixed[:, :, 0:S]
                    pool.tensor_tensor(total, acc[:, :, :], part[:, e % 2, :].rearrange("p (b s) -> p b s", b=CB), ALU.add)\
                        .then_inc(acc_ready, 1)
                    if e + 1 < NE:
                        tail(e + 1, 1)

            def tail(i, e, at, after=False):
                if at != 1:
                    return
                if 0 <= e - 1 < CK:
                    t.pool_rstd(pool, i, e - 1)
                if 0 <= e - 2 < CK:
                    if inner:
                        t.pool_inner_rstd(pool, i, e - 2)
                    if not final:
                        t.pool_store(pool, i, e - 2)

            run(pool, chunk, tail)

        @block.sync
        def _(sp):
            if not final:
                return
            with sp.Fori(0, CHUNKS) as i:
                sp.wait_ge(t.xn_ready, n(i, CK - 1))
                for h in range(2):
                    sp.dma_start(k.out[bass.ds(i * CB, CB), :, :].rearrange("(g h) s d -> h s g d", h=2)[h],
                                 k.x_tok[h * SP:h * SP + S, bass.ds(i * CK, CK), :]).then_inc(out_stored, 16)
            sp.wait_ge(out_stored, CHUNKS * 2 * 16)

        @block.tensor
        def _(pe):
            open_sems(pe, E, spread_ready)
            open_sems(pe, NT * (1 if layer == 0 else 2), up_ready)
            open_sems(pe, NE, down_ready)
            open_sems(pe, CK, y_ready)
            t.open_tensor(pe)

            def split_product(out, w, x, start, stop):
                (w_hi, w_lo), (m_hi, m_lo) = w, x
                nc.tensor.matmul(out, w_hi, m_hi, start=start, stop=False)
                nc.tensor.matmul(out, w_hi, m_lo, start=False, stop=False)
                return nc.tensor.matmul(out, w_lo, m_hi, start=False, stop=stop)

            def chunk(i, tail, first=False, end=False):
                x = (x_hi[:, :], x_lo[:, :])

                def spread_weights(e):
                    if e >= 2:
                        pe.wait_ge(spread_kept, this(i, e - 1, E))
                    if not first:
                        if 0 <= e - 3 < CK:
                            pe.wait_ge(t.r_ready, last(i, e - 2, CK))
                        if 0 <= e - 5 < CK and not final:
                            pe.wait_ge(t.feat_stored, last(i, e - 4, CK))
                    for p in range(CK):
                        done = nc.tensor.transpose(psum[:, 6 + e % 2, p * 128:(p + 1) * 128],
                                                   wc[:, p, e:e + 1].to_broadcast([128, 128]), k.ident[:, :])
                    done.then_inc(spread_ready, 1)

                def hidden(e):
                    for j in range(HT):
                        u = e * HT + j
                        if layer == 0:
                            pe.wait_ge(hi_ready, hid_tile(i, u, 4))
                            split_product(psum[:, u % 4, 0:CT], part_of("up", e, slice(j * 128, (j + 1) * 128)), x,
                                          True, True).then_inc(up_ready, 1)
                        else:
                            pe.wait_ge(hid_ready, hid_tile(i, u, 2))
                            for c, w in enumerate(("gate", "up")):
                                split_product(psum[:, 2 * c + u % 2, 0:CT], part_of(w, e, slice(j * 128, (j + 1) * 128)), x,
                                              True, True).then_inc(up_ready, 1)

                def project(e):
                    pe.wait_ge(part_ready, slot(i, e))
                    for j in range(HT):
                        pe.wait_ge(lo_ready, this(i, e * HT + j + 1, NT))
                        done = split_product(psum[:, 4 + e % 2, 0:CT], part_of("down", e, j),
                                             (hid_hi[:, e % 2, j, :], hid_lo[:, e % 2, j, :]), j == 0, j == HT - 1)
                    done.then_inc(down_ready, 1)

                pe.wait_ge(x_lo_ready, this(i))
                hidden(0)
                pe.wait_ge(wc_ready, this(i))
                pe.wait_ge(spread_kept, last(i, E, E))
                if not first:
                    pe.wait_ge(t.r_ready, last(i, 0, CK))
                    if not final:
                        pe.wait_ge(t.feat_stored, last(i, 0, CK))
                spread_weights(0)
                spread_weights(1)
                for e in range(1, NE):
                    hidden(e)
                    if e + 1 < E:
                        spread_weights(e + 1)
                    tail(e, 0)
                    project(e - 1)
                    tail(e, 2)
                project(NE - 1)

            def tail(i, e, at, after=False):
                bank = 6 + e % 2
                if 0 <= e - 5 and after and not final:
                    pe.wait_ge(t.feat_stored, this(i, e - 4, CK))
                if at == 0 and 0 <= e - 1 < CK:
                    if e == 1:
                        pe.wait_ge(acc_ready, this(i, NE - 1, NE - 1))
                    if after:
                        pe.wait_ge(spread_kept, this(i, E, E))
                        if e >= 3:
                            pe.wait_ge(t.r_ready, this(i, e - 2, CK))
                    else:
                        pe.wait_ge(spread_kept, this(i + 1, e + 1, E))
                    nc.tensor.transpose(psum[:, bank, 0:128], mixed[:, 2 * (e - 1):2 * e, :], k.ident[:, :])\
                        .then_inc(y_ready, 1)
                if at == 2 and 0 <= e - 3 < CK and not final:
                    pe.wait_ge(t.r_ready, this(i, min(e, CK), CK))
                    if not after:
                        pe.wait_ge(spread_kept, this(i + 1, e + 1, E))
                    t.tensor_transpose(pe, i, e - 3, psum[:, bank, 128:256])

            run(pe, chunk, tail)

        @block.vector
        def _(dve):
            open_sems(dve, NE, part_ready)
            open_sems(dve, E, spread_kept)
            open_sems(dve, 1, x_lo_ready)
            open_sems(dve, NT, lo_ready)
            if layer == 1:
                open_sems(dve, NT, hid_ready)
            t.open_vector(dve)

            def x_low(i):
                dve.wait_ge(x_hi_ready, this(i))
                nc.vector.tensor_tensor(x_lo[:, :].rearrange("p (b s) -> p b s", b=CB), k.x_feat[:, bass.ds(i * CB, CB), :],
                                        x_hi[:, :].bitcast(fp32).rearrange("p (b s) -> p b s", b=CB), ALU.subtract)\
                    .then_inc(x_lo_ready, 1)

            def low(i, u):
                dve.wait_ge(hi_ready, this(i, u + 1, NT))
                e, j = u // HT, u % HT
                if j == 0:
                    dve.wait_ge(down_ready, slot(i, e))
                nc.vector.tensor_tensor(hid_lo[:, e % 2, j, :], hid[:, u % 2, :], hid_hi[:, e % 2, j, :].bitcast(fp32),
                                        ALU.subtract).then_inc(lo_ready, 1)

            x_low(0)

            def chunk(i, tail, first=False, end=False):
                def keep_spread(e):
                    dve.wait_ge(spread_ready, this(i, e + 1, E))
                    dve.wait_ge(part_ready, this(i, e - 2, NE) if e >= 3 else last(i, E, NE))
                    nc.vector.tensor_copy(spread[:, e % 3, :].rearrange("p (b s) -> p b s", b=CB),
                                          psum[:, 6 + e % 2, :].rearrange("p (b s) -> p b s", b=CB)[:, :, 0:S])\
                        .then_inc(spread_kept, 1)

                def hidden(e):
                    for j in range(HT):
                        u = e * HT + j
                        if layer == 0:
                            low(i, u)
                            continue
                        dve.wait_ge(silu_ready, this(i, u + 1, NT))
                        dve.wait_ge(up_ready, this(i, 2 * u + 2, 2 * NT))
                        dve.wait_ge(hi_ready, hid_tile(i, u, 2))
                        dve.wait_ge(lo_ready, hid_tile(i, u, 2))
                        nc.vector.tensor_tensor(hid[:, u % 2, :], act_out[:, u % 2, :], psum[:, 2 + u % 2, 0:CT],
                                                ALU.mult).then_inc(hid_ready, 1)
                        if j:
                            low(i, u - 1)
                    if layer == 1:
                        low(i, e * HT + HT - 1)

                def weigh(e):
                    dve.wait_ge(down_ready, this(i, e + 1, NE))
                    src = psum[:, 4 + e % 2, 0:CT]
                    if e == 0:
                        dve.wait_ge(acc_ready, last(i, NE - 1, NE - 1))
                        dve.wait_ge(spread_kept, this(i, 1, E))
                        split = lambda v: v.rearrange("p (b s) -> p b s", b=CB)
                        if layer == 0:
                            nc.vector.scalar_tensor_tensor(acc[:, :, :], split(src), k.down_bias0[:, 0:1],
                                                           split(spread[:, 0, :]), ALU.add, ALU.mult)\
                                .then_inc(part_ready, 1)
                        else:
                            nc.vector.tensor_tensor(acc[:, :, :], split(src), split(spread[:, 0, :]), ALU.mult)\
                                .then_inc(part_ready, 1)
                        return
                    dve.wait_ge(acc_ready, this(i, e - 2, NE - 1) if e > 2 else last(i, NE - 1, NE - 1))
                    if layer == 0:
                        dve.wait_ge(spread_kept, this(i, e + 1, E))
                        nc.vector.scalar_tensor_tensor(part[:, e % 2, :], src, k.down_bias0[:, e:e + 1],
                                                       spread[:, e % 3, :], ALU.add, ALU.mult).then_inc(part_ready, 1)
                    elif e < E:
                        dve.wait_ge(spread_kept, this(i, e + 1, E))
                        nc.vector.tensor_tensor(part[:, e % 2, :], src, spread[:, e % 3, :], ALU.mult).then_inc(part_ready, 1)
                    else:
                        nc.vector.tensor_copy(part[:, e % 2, :], src).then_inc(part_ready, 1)

                hidden(0)
                keep_spread(0)
                keep_spread(1)
                for e in range(1, NE):
                    hidden(e)
                    if e + 1 < E:
                        keep_spread(e + 1)
                    tail(e, 1)
                    weigh(e - 1)
                if not end:
                    x_low(i + 1)
                weigh(NE - 1)

            def tail(i, e, at, after=False):
                if at != 1:
                    return
                p = e - 1
                if 0 <= p < CK:
                    dve.wait_ge(y_ready, n(i, p))
                    nc.vector.tensor_tensor(t.r[:, p:p + 1, :], psum[:, 6 + e % 2, 0:128].unsqueeze(1),
                                            k.x_tok[:, bass.ds(i * CK + p, 1), :], ALU.add).then_inc(t.r_ready, 1)
                    t.vector_moments(dve, i, p)
                p = e - 2
                if 0 <= p < CK:
                    t.vector_normalise(dve, i, p)
                    if inner:
                        t.vector_inner_moments(dve, i, p)
                p = e - 3
                if inner and 0 <= p < CK:
                    t.vector_inner_normalise(dve, i, p)

            run(dve, chunk, tail)

        @block.scalar
        def _(act):
            open_sems(act, NT, hi_ready)
            open_sems(act, 1, x_hi_ready)
            if layer == 1:
                open_sems(act, NT, silu_ready)
            t.open_scalar(act)

            def x_high(i):
                act.wait_ge(up_ready, last(i, NT, NT) if layer == 0 else last(i, 2 * NT, 2 * NT))
                nc.scalar.activation(x_hi[:, :].rearrange("p (b s) -> p b s", b=CB), k.x_feat[:, bass.ds(i * CB, CB), :],
                                     ACT.Copy).then_inc(x_hi_ready, 1)

            x_high(0)

            def chunk(i, tail, first=False, end=False):
                def high(u):
                    e, j = u // HT, u % HT
                    act.wait_ge(hid_ready, this(i, u + 1, NT))
                    if j == 0:
                        act.wait_ge(down_ready, slot(i, e))
                    nc.scalar.activation(hid_hi[:, e % 2, j, :], hid[:, u % 2, :], ACT.Copy).then_inc(hi_ready, 1)

                for e in range(NE):
                    for j in range(HT):
                        u = e * HT + j
                        if layer == 0:
                            act.wait_ge(up_ready, this(i, u + 1, NT))
                            act.wait_ge(lo_ready, hid_tile(i, u, 2))
                            gelu = dict(func=ACT.Gelu, bias=k.up_bias0[:, e, j:j + 1])
                            nc.scalar.activation(hid[:, u % 2, :], psum[:, u % 4, 0:CT], **gelu)
                            if j == 0:
                                act.wait_ge(down_ready, slot(i, e))
                            nc.scalar.activation(hid_hi[:, e % 2, j, :], psum[:, u % 4, 0:CT], **gelu).then_inc(hi_ready, 1)
                        else:
                            act.wait_ge(up_ready, this(i, 2 * u + 1, 2 * NT))
                            act.wait_ge(hid_ready, hid_tile(i, u, 2))
                            nc.scalar.activation(act_out[:, u % 2, :], psum[:, u % 2, 0:CT], ACT.Silu)\
                                .then_inc(silu_ready, 1)
                            if j:
                                high(u - 1)
                    if layer == 1:
                        high(e * HT + HT - 1)
                    if e == NE - 1 and not end:
                        x_high(i + 1)
                    tail(e, 2)

            def tail(i, e, at, after=False):
                if at == 2 and 0 <= e - 3 < CK and not final:
                    t.scalar_store(act, i, e - 3, psum[:, 6 + e % 2, 128:256])

            run(act, chunk, tail)


def expert_phase0(k):
    routing_phase(k, 0)
    k.clear_semaphores()
    expert_phase(k, 0)


def expert_phase1(k):
    routing_phase(k, 1)
    k.clear_semaphores()
    expert_phase(k, 1)


def state_space_phase(k):
    nc = k.nc
    N1 = 32
    with ExitStack() as ctx:
        t = Tail(k, ctx, "ss", inner=(k.gamma1[:, :], k.beta1[:, :]))
        sem = lambda name: k.sem(ctx, "ss_" + name)
        sb = lambda name, shape: k.sb(ctx, "ss_" + name, shape)
        hp = sb("hp", [128, CB, S + 2])
        tap0, tap1, mixed = sb("tap0", [128, CT]), sb("tap1", [128, CT]), sb("mixed", [128, CT])
        u, g = sb("u", [128, CT]), sb("g", [128, CT])
        xs, decay, sel = sb("xs", [N1, CT]), sb("decay", [N1, CT]), sb("sel", [N1, CT])
        keep, drive, states, chosen = sb("keep", [N1, CT]), sb("drive", [N1, CT]), sb("states", [N1, CT]), sb("chosen", [N1, CT])
        diff, gdiff = sb("diff", [128, CT]), sb("gdiff", [128, CT])
        z = sb("z", [128, CB, SP])
        xb, xb2 = sb("xb", [128, CK, D]), sb("xb2", [128, CK, D])
        psum = ctx.enter_context(nc.psum_tensor("ss_psum", [128, 8, 512], fp32))
        zeroed, h_ready, xb_ready, xb2_ready = sem("zeroed"), sem("h_ready"), sem("xb_ready"), sem("xb2_ready")
        step_done, proj_ready, act_ready = sem("step_done"), sem("proj_ready"), sem("act_ready")
        state_out_ready, out_ready = sem("state_out_ready"), sem("out_ready")
        block = ctx.enter_context(nc.Block())
        n = lambda i, p: this(i, p + 1, CK)
        b = lambda i, p: last(i, p + 1, CK)
        TAP0, TAP1, MIXED, ONE_MINUS, DRIVE, RESET, STATES, CHOSEN, DIFF, GDIFF, Z = range(1, 12)
        NV = Z
        XS, DECAY, SEL, U, G = range(5)

        @block.gpsimd
        def _(pool):
            open_sems(pool, 1, h_ready)
            open_sems(pool, CK, xb_ready, xb2_ready)
            t.open_pool(pool)
            pool.memset(hp[:, :, :], 0.0).then_inc(zeroed, 1)
            pool.memset(z[:, :, :], 0.0).then_inc(zeroed, 1)
            pool.wait_ge(zeroed, 2)
            with pool.Fori(0, CHUNKS) as i:
                pool.wait_ge(step_done, last(i, MIXED, NV))
                pool.tensor_copy(hp[:, :, 1:S + 1], k.x_feat[:, bass.ds(i * CB, CB), :]).then_inc(h_ready, 1)
                for p in range(CK):
                    pool.tensor_tensor(xb[:, p:p + 1, :], k.x_tok[:, bass.ds(i * CK + p, 1), :],
                                       k.bout_row1[:, :].unsqueeze(1), ALU.add).then_inc(xb_ready, 1)
                for p in range(CK):
                    pool.wait_ge(xb_ready, n(i, p))
                    pool.wait_ge(t.r_ready, b(i, p))
                    pool.sem_inc(t.storing, 1)
                    pool.tensor_tensor(xb2[:, p:p + 1, :], xb[:, p:p + 1, :], k.x_tok[:, bass.ds(i * CK + p, 1), :],
                                       ALU.add).then_inc(xb2_ready, 1)
                for p in range(CK):
                    t.pool_rstd(pool, i, p)
                for p in range(CK):
                    t.pool_inner_rstd(pool, i, p)
                for p in range(CK):
                    t.pool_store(pool, i, p)

        @block.tensor
        def _(pe):
            open_sems(pe, 5, proj_ready)
            open_sems(pe, 1, state_out_ready)
            open_sems(pe, CK, out_ready)
            t.open_tensor(pe)
            with pe.Fori(0, CHUNKS) as i:
                pe.wait_ge(step_done, this(i, MIXED, NV))
                pe.wait_ge(act_ready, last(i, 5, 5))
                for bank, w, rows in ((XS, k.wsin1, N1), (DECAY, k.wd1, N1), (SEL, k.wsel1, N1), (U, k.wi1, D), (G, k.wg1, D)):
                    nc.tensor.matmul(psum[0:rows, bank, 0:CT], w[:, :], mixed[:, :], start=True, stop=True)\
                        .then_inc(proj_ready, 1)
                pe.wait_ge(step_done, this(i, CHOSEN, NV))
                nc.tensor.matmul(psum[:, 5, 0:CT], k.wso1[:, :], chosen[:, :], start=True, stop=True)\
                    .then_inc(state_out_ready, 1)
                pe.wait_ge(step_done, this(i, Z, NV))
                for p in range(CK):
                    pe.wait_ge(t.r_ready, n(i, p - 1) if p else b(i, CK - 1))
                    nc.tensor.matmul(psum[:, 6, 0:D], z[:, 2 * p:2 * p + 2, :], k.wout1[:, :], start=True, stop=True)\
                        .then_inc(out_ready, 1)
                for p in range(CK):
                    pe.wait_ge(t.feat_stored, n(i, p - 1) if p else b(i, CK - 1))
                    t.tensor_transpose(pe, i, p, psum[:, 7, 0:128])

        @block.vector
        def _(dve):
            open_sems(dve, NV, step_done)
            t.open_vector(dve)
            dve.wait_ge(zeroed, 2)
            with dve.Fori(0, CHUNKS) as i:
                def follows(step):
                    dve.wait_ge(step_done, this(i, step, NV))

                dve.wait_ge(h_ready, this(i))
                nc.vector.tensor_scalar(tap0[:, :], hp[:, :, 0:S], k.mix_w1[:, 0:1], k.mix_b1[:, :], ALU.mult, ALU.add)\
                    .then_inc(step_done, 1)
                follows(TAP0)
                nc.vector.scalar_tensor_tensor(tap1[:, :].rearrange("p (b s) -> p b s", b=CB), hp[:, :, 1:S + 1],
                                               k.mix_w1[:, 1:2], tap0[:, :].rearrange("p (b s) -> p b s", b=CB),
                                               ALU.mult, ALU.add).then_inc(step_done, 1)
                follows(TAP1)
                dve.wait_ge(proj_ready, last(i, 5, 5))
                nc.vector.scalar_tensor_tensor(mixed[:, :].rearrange("p (b s) -> p b s", b=CB), hp[:, :, 2:S + 2],
                                               k.mix_w1[:, 2:3], tap1[:, :].rearrange("p (b s) -> p b s", b=CB),
                                               ALU.mult, ALU.add).then_inc(step_done, 1)
                dve.wait_ge(act_ready, this(i, DECAY + 1, 5))
                nc.vector.tensor_scalar(keep[:, :], decay[:, :], -1.0, 1.0, ALU.mult, ALU.add).then_inc(step_done, 1)
                follows(ONE_MINUS)
                nc.vector.tensor_tensor(drive[:, :], keep[:, :], xs[:, :], ALU.mult).then_inc(step_done, 1)
                nc.vector.memset(decay[:, :].rearrange("p (b s) -> p b s", b=CB)[:, :, 0:1], 0.0).then_inc(step_done, 1)
                follows(RESET)
                nc.vector.tensor_tensor_scan(states[:, :], decay[:, :], drive[:, :], 0.0, ALU.mult, ALU.add)\
                    .then_inc(step_done, 1)
                follows(STATES)
                dve.wait_ge(act_ready, this(i, SEL + 1, 5))
                dve.wait_ge(state_out_ready, last(i))
                nc.vector.tensor_tensor(chosen[:, :], states[:, :], sel[:, :], ALU.mult).then_inc(step_done, 1)
                dve.wait_ge(state_out_ready, this(i))
                dve.wait_ge(act_ready, this(i, 5, 5))
                nc.vector.scalar_tensor_tensor(diff[:, :], psum[:, 5, 0:CT], k.bso1[:, :], u[:, :],
                                               ALU.add, ALU.subtract).then_inc(step_done, 1)
                follows(DIFF)
                nc.vector.tensor_tensor(gdiff[:, :], diff[:, :], g[:, :], ALU.mult).then_inc(step_done, 1)
                follows(GDIFF)
                dve.wait_ge(out_ready, b(i, CK - 1))
                nc.vector.tensor_tensor(z[:, :, 0:S], gdiff[:, :].rearrange("p (b s) -> p b s", b=CB),
                                        u[:, :].rearrange("p (b s) -> p b s", b=CB), ALU.add).then_inc(step_done, 1)
                for p in range(CK):
                    dve.wait_ge(out_ready, n(i, p))
                    dve.wait_ge(xb2_ready, n(i, p))
                    nc.vector.tensor_tensor(t.r[:, p, :], psum[:, 6, 0:D], xb2[:, p, :], ALU.add).then_inc(t.r_ready, 1)
                    t.vector_moments(dve, i, p)
                for p in range(CK):
                    t.vector_normalise(dve, i, p)
                for p in range(CK):
                    t.vector_inner_moments(dve, i, p)
                for p in range(CK):
                    t.vector_inner_normalise(dve, i, p)

        @block.scalar
        def _(act):
            open_sems(act, 5, act_ready)
            t.open_scalar(act)
            with act.Fori(0, CHUNKS) as i:
                act.wait_ge(step_done, last(i, Z, NV))
                for bank, dst, f, bias in ((XS, xs, ACT.Tanh, k.bsin1), (DECAY, decay, ACT.Sigmoid, k.bd1),
                                           (SEL, sel, ACT.Sigmoid, k.bsel1), (U, u, ACT.Tanh, k.bi1),
                                           (G, g, ACT.Sigmoid, k.bg1)):
                    act.wait_ge(proj_ready, this(i, bank + 1, 5))
                    rows = D if bank >= U else N1
                    nc.scalar.activation(dst[:, :], psum[0:rows, bank, 0:CT], f, bias=bias[:, :]).then_inc(act_ready, 1)
                for p in range(CK):
                    t.scalar_store(act, i, p, psum[:, 7, 0:128])


def cross_attention_phase(k):
    nc = k.nc
    WIDTH = (2 * (C // 8) + 2, C // 2 - 2 * (C // 8) - 2)
    FIRST = (0, 2 * WIDTH[0])
    UQ = 128 // H1
    UPS = S // UQ
    NU = 2 * UPS
    GROUPS = [[h * UPS + u for u in g] for h in range(2) for g in ((0, 1), (2, 3), (4, 5), (6,))]
    NG = len(GROUPS)
    GROUP_END = [3, 5, 7, 8, 10, 12, 14, 15]
    SPREAD_AT = [2, 5, 7, 8, 10, 12, 14, 15]
    SLOT = {u: 2 * (j % 2) + e for j, g in enumerate([g for g in GROUPS if len(g) == 2]) for e, u in enumerate(g)}
    SINGLE = [g[0] for g in GROUPS if len(g) == 1]
    HB = 4
    NB = H1 // HB
    PROJECTED = {0: (1, 0), 1: (1, 1), 4: (1, 2), 5: (1, 3), 8: (2, 0), 9: (2, 1), 10: (2, 2), 11: (2, 3)}
    SCALE = DH1 ** -0.5
    NLO = 3 * (NU - len(SINGLE))
    with ExitStack() as ctx:
        t = Tail(k, ctx, "xa", router=k.router1, per=1)
        sem = lambda name: k.sem(ctx, "xa_" + name)
        sb = lambda name, shape, dt=fp32: k.sb(ctx, "xa_" + name, shape, dt)
        q_hi, q_lo = sb("q_hi", [128, 2, S, H1], fp32r), sb("q_lo", [128, 2, S, H1], fp32r)
        ctxT = sb("ctxT", [128, C])
        c_hi, c_lo = sb("c_hi", [128, 2, C], fp32r), sb("c_lo", [128, 2, C], fp32r)
        ctxN = sb("ctxN", [KP, 2, KT * D])
        n_hi, n_lo = sb("n_hi", [KP, 2, KT * D], fp32r), sb("n_lo", [KP, 2, KT * D], fp32r)
        pr = sb("pr", [128, 2, C])
        prT_hi, prT_lo = sb("prT_hi", [KP, 4, KT, 128], fp32r), sb("prT_lo", [KP, 4, KT, 128], fp32r)
        prT_single = sb("prT_single", [KP, KT, 128])
        halfmax = sb("halfmax", [128, 2, 2])
        negmax = sb("negmax", [128, 2, 1])
        rs = sb("rs", [128, 2, 2])
        total = sb("total", [128, 2, 1])
        rinv = sb("rinv", [128, NU, 1])
        rb = sb("rb", [128, 2, 256])
        on = sb("on", [128, H1, 2, SP])
        ybo = sb("ybo", [128, D])
        psum = ctx.enter_context(nc.psum_tensor("xa_psum", [128, 8, 512], fp32))
        ctxT_loaded, ctxN_loaded = sem("ctxT_loaded"), [sem("ctxN_loaded0"), sem("ctxN_loaded1")]
        q_ready, q_hi_kept, q_lo_kept = sem("q_ready"), sem("q_hi_kept"), sem("q_lo_kept")
        c_hi_ready, c_lo_ready, splitting = sem("c_hi_ready"), sem("c_lo_ready"), sem("splitting")
        n_hi_ready, n_lo_ready = sem("n_hi_ready"), sem("n_lo_ready")
        scores_ready, halfmax_ready, max_ready, exp_ready = sem("scores_ready"), sem("halfmax_ready"), sem("max_ready"), sem("exp_ready")
        total_ready, rinv_ready, rb_ready, rb_kept = sem("total_ready"), sem("rinv_ready"), sem("rb_ready"), sem("rb_kept")
        prT_ready, hi_kept, lo_kept, pv_ready, on_kept = sem("prT_ready"), sem("hi_kept"), sem("lo_kept"), sem("pv_ready"), sem("on_kept")
        on_zeroed, y_ready, ybo_ready = sem("on_zeroed"), sem("y_ready"), sem("ybo_ready")
        block = ctx.enter_context(nc.Block())

        n = lambda i, u: this(i, u + 1, NU)

        def q_count(i, h, c):
            return this(i, h * NB + c + 1, 2 * NB)

        def lo_count(i, u, r):
            return this(i, 3 * sum(v not in SINGLE for v in range(u)) + r + 1, NLO)

        def groups_before(i, s):
            return this(i, sum(e < s for e in GROUP_END[:NG - 2]) + min(0, s - 2), NG)

        def spreads_before(i, s):
            return this(i, sum(e < s for e in SPREAD_AT[:NG - 2]) + min(0, s - 2), NG)

        def group_at(steps, i, s, first):
            if s in steps:
                return i, steps.index(s)
            if s + NU in steps and not first:
                return i - 1, steps.index(s + NU)
            return None

        def run(engine, step, prologue, epilogue):
            prologue()
            for s in range(UPS):
                step(0, s, first=True)
            with engine.Fori(0, PAIRS - 1) as i:
                for s in range(UPS, NU):
                    step(i, s)
                for s in range(UPS):
                    step(i + 1, s)
            for s in range(UPS, NU):
                step(PAIRS - 1, s, end=True)
            epilogue()

        @block.sync
        def _(sp):
            with sp.Fori(0, PAIRS) as i:
                for h in range(2):
                    sp.wait_ge(c_lo_ready, this(i, h, 2))
                    sp.dma_start(ctxT[:, :].unsqueeze(1),
                                 k.dram["ctxT"][bass.ds(2 * i + h, 1), :, :].rearrange("b d c -> d b c"))\
                        .then_inc(ctxT_loaded, 16)
                    sp.wait_ge(pv_ready, last(i, (h + 1) * NG // 2, NG))
                    sp.dma_start(ctxN[:, h:h + 1, :],
                                 k.dram["ctxN"][bass.ds(2 * i + h, 1), :, :, :].rearrange("b q t d -> q b (t d)"))\
                        .then_inc(ctxN_loaded[h], 16)

        @block.gpsimd
        def _(pool):
            open_sems(pool, 2, c_hi_ready, c_lo_ready, n_hi_ready, n_lo_ready)
            t.open_pool(pool)
            pool.memset(on[:, :, :, :], 0.0).then_inc(on_zeroed, 1)
            def split(i):
                for h in range(2):
                    pool.wait_ge(ctxT_loaded, i * 32 + 16 * (h + 1))
                    pool.wait_ge(scores_ready, last(i, 2 * (h + 1) * UPS, 2 * NU))
                    pool.sem_inc(splitting, 1)
                    pool.tensor_copy(c_hi[:, h, :], ctxT[:, :]).then_inc(c_hi_ready, 1)
                    pool.wait_ge(c_hi_ready, this(i, h + 1, 2))
                    pool.tensor_tensor(c_lo[:, h, :], ctxT[:, :], c_hi[:, h, :].bitcast(fp32), ALU.subtract)\
                        .then_inc(c_lo_ready, 1)
                    pool.wait_ge(ctxN_loaded[h], (i + 1) * 16)
                    pool.wait_ge(pv_ready, last(i, (h + 1) * NG // 2, NG))
                    pool.sem_inc(splitting, 1)
                    pool.tensor_copy(n_hi[:, h, :], ctxN[:, h, :]).then_inc(n_hi_ready, 1)
                    pool.wait_ge(n_hi_ready, this(i, h + 1, 2))
                    pool.tensor_tensor(n_lo[:, h, :], ctxN[:, h, :], n_hi[:, h, :].bitcast(fp32), ALU.subtract)\
                        .then_inc(n_lo_ready, 1)

            split(0)
            with pool.Fori(1, PAIRS) as i:
                split(i)
                t.pool_rstd(pool, i - 1, 0)
                t.pool_store(pool, i - 1, 0)
            t.pool_rstd(pool, PAIRS - 1, 0)
            t.pool_store(pool, PAIRS - 1, 0)

        @block.tensor
        def _(pe):
            open_sems(pe, 2 * NB, q_ready)
            open_sems(pe, 2 * NU, scores_ready)
            open_sems(pe, 3 * NU, prT_ready)
            open_sems(pe, NG, pv_ready, rb_ready)
            open_sems(pe, 1, y_ready)
            t.open_tensor(pe)

            def project(i, h, c):
                for j in range(HB):
                    done = nc.tensor.matmul(psum[:, 7, j * S:(j + 1) * S], k.key_query[:, c * HB + j, :],
                                            k.x_feat[:, bass.ds(2 * i + h, 1), :], start=True, stop=True)
                done.then_inc(q_ready, 1)

            def scores(i, u):
                h, p0 = u // UPS, (u % UPS) * UQ
                if u % UPS == 0:
                    pe.wait_ge(q_lo_kept, q_count(i, h, NB - 1))
                    pe.wait_ge(c_lo_ready, this(i, h + 1, 2))
                qh = q_hi[:, h, p0:p0 + UQ, :].rearrange("p a b -> p (a b)")
                ql = q_lo[:, h, p0:p0 + UQ, :].rearrange("p a b -> p (a b)")
                for half in range(2):
                    pe.wait_ge(exp_ready, this(i, 2 * (u - 1) + half + 1, 2 * NU))
                    for j in range(2 * half, 2 * half + 2):
                        w = WIDTH[half]
                        keys = slice(FIRST[half] + (j % 2) * w, FIRST[half] + (j % 2 + 1) * w)
                        nc.tensor.matmul(psum[:, j, 0:w], qh, c_hi[:, h, keys], start=True, stop=False)
                        nc.tensor.matmul(psum[:, j, 0:w], qh, c_lo[:, h, keys], start=False, stop=False)
                        done = nc.tensor.matmul(psum[:, j, 0:w], ql, c_hi[:, h, keys], start=False, stop=True)
                    done.then_inc(scores_ready, 1)

            def transposes(i, u, r):
                pe.wait_ge(exp_ready, this(i, 2 * u + (1 if r == 0 else 2), 2 * NU))
                v, q = (u, 0) if r == 2 else (u - 1, 2 if r == 0 else 1)
                if v % NU in SINGLE:
                    pe.wait_ge(hi_kept, this(i, 3 * v + q + 1, 3 * NU))
                else:
                    pe.wait_ge(lo_kept, lo_count(i, v, q))
                for j in range(4):
                    kt = 4 * r + j
                    done = nc.tensor.transpose(psum[0:KP, 4 + r % 2, j * 128:(j + 1) * 128],
                                               pr[:, u % 2, kt * KP:(kt + 1) * KP], k.ident[:, :])
                done.then_inc(prT_ready, 1)

            def spread(i, g):
                pe.wait_ge(rinv_ready, n(i, GROUPS[g][-1]))
                for e, u in enumerate(GROUPS[g]):
                    done = nc.tensor.transpose(psum[:, 7, 256 + 128 * e:384 + 128 * e],
                                               rinv[:, u, :].to_broadcast([128, 128]), k.ident[:, :])
                done.then_inc(rb_ready, 1)

            def values_pair(i, g, part):
                u, h = GROUPS[g][1], GROUPS[g][0] // UPS
                if part == 0:
                    pe.wait_ge(n_lo_ready, this(i, h + 1, 2))
                    pe.wait_ge(on_kept, this(i, g, NG))
                pe.wait_ge(lo_kept, lo_count(i, u, 1 + part))
                out = psum[:, 6, 0:256].rearrange("p (a b) -> p a b", a=2)
                s0 = SLOT[u] - 1
                for kt in range(part * KT // 2, (part + 1) * KT // 2):
                    nh, nl = (v[:, h, kt * D:(kt + 1) * D] for v in (n_hi, n_lo))
                    ph, pl = (v[:, s0:s0 + 2, kt, :] for v in (prT_hi, prT_lo))
                    nc.tensor.matmul(out, nh, ph, start=(kt == 0), stop=False)
                    nc.tensor.matmul(out, nh, pl, start=False, stop=False)
                    done = nc.tensor.matmul(out, nl, ph, start=False, stop=(kt == KT - 1))
                if part:
                    done.then_inc(pv_ready, 1)

            def values_single(i, g):
                u, h = GROUPS[g][0], GROUPS[g][0] // UPS
                pe.wait_ge(ctxN_loaded[h], (i + 1) * 16)
                pe.wait_ge(on_kept, this(i, g, NG))
                pe.wait_ge(hi_kept, this(i, 3 * u + 3, 3 * NU))
                for kt in range(KT):
                    done = nc.tensor.matmul(psum[:, 6, 0:128], ctxN[:, h, kt * D:(kt + 1) * D], prT_single[:, kt, :],
                                            start=(kt == 0), stop=(kt == KT - 1))
                done.then_inc(pv_ready, 1)

            def values(i, s, first):
                for j, e in ((i, 0), (i - 1, NU)) if not first else ((i, 0),):
                    for g, end in enumerate(GROUP_END):
                        if len(GROUPS[g]) == 1 and s + e == end:
                            values_single(j, g)
                        elif len(GROUPS[g]) == 2 and s + e in (end - 1, end):
                            values_pair(j, g, s + e - end + 1)

            def outputs(i, half):
                if half == 0:
                    pe.wait_ge(on_kept, this(i, NG, NG))
                for h in range(half * H1 // 2, (half + 1) * H1 // 2):
                    done = nc.tensor.matmul(psum[:, 7, 0:128], on[:, h, :, :], k.value_out[:, h, :],
                                            start=(h == 0), stop=(h == H1 - 1))
                if half:
                    done.then_inc(y_ready, 1)

            def step(i, s, first=False, end=False):
                if s in PROJECTED and not (end and PROJECTED[s][0] == 2):
                    h, c = PROJECTED[s]
                    pe.wait_ge(rb_kept, spreads_before(i, s))
                    pe.wait_ge(q_lo_kept, q_count(i, h, c - 1))
                    pe.wait_ge(ybo_ready, this(i, 0 if s >= 4 else -1, 1) if not first else 1)
                    project(i, h, c)
                if s + 1 < NU or not end:
                    scores(i, s + 1) if s + 1 < NU else scores(i + 1, 0)
                g = group_at(SPREAD_AT, i, s, first)
                if g:
                    if s in PROJECTED and not (end and PROJECTED[s][0] == 2):
                        pe.wait_ge(q_lo_kept, q_count(i, *PROJECTED[s]))
                    else:
                        pe.wait_ge(rb_kept, spreads_before(i, s))
                        if s == 12 and not end:
                            pe.wait_ge(q_lo_kept, q_count(i, 2, NB - 1))
                        if s == 7:
                            pe.wait_ge(t.logits_kept, this(i, 0, 1))
                    spread(*g)
                transposes(i, s, 0)
                transposes(i, s, 1)
                if s in (2, 3) and not first:
                    pe.wait_ge(rb_kept, spreads_before(i, 3))
                    outputs(i - 1, s - 2)
                if s == 6 and not first:
                    pe.wait_ge(rb_kept, spreads_before(i, s))
                    t.tensor_transpose(pe, i - 1, 0, psum[:, 7, 128:256])
                values(i, s, first)
                if s == 6 and not first:
                    pe.wait_ge(t.feat_stored, this(i, 0, 1))
                    t.tensor_logits(pe, i - 1, 0, psum[:, 7, 0:E])
                transposes(i, s, 2)

            def prologue():
                for c in range(NB):
                    if c:
                        pe.wait_ge(q_lo_kept, q_count(0, 0, c - 1))
                    project(0, 0, c)
                scores(0, 0)

            def epilogue():
                i = PAIRS - 1
                for e in range(2):
                    pe.wait_ge(rb_kept, this(i, NG - 2 + e, NG))
                    spread(i, NG - 2 + e)
                    if e == 0:
                        values_pair(i, NG - 2, 1)
                    else:
                        values_single(i, NG - 1)
                pe.wait_ge(rb_kept, this(i, NG, NG))
                for half in range(2):
                    outputs(i, half)
                pe.wait_ge(ybo_ready, this(i))
                t.tensor_transpose(pe, i, 0, psum[:, 7, 128:256])
                pe.wait_ge(t.feat_stored, this(i))
                t.tensor_logits(pe, i, 0, psum[:, 7, 0:E])

            run(pe, step, prologue, epilogue)

        @block.vector
        def _(dve):
            open_sems(dve, 2 * NB, q_lo_kept)
            open_sems(dve, 2 * NU, halfmax_ready)
            open_sems(dve, NLO, lo_kept)
            open_sems(dve, NU, max_ready, total_ready, rinv_ready)
            open_sems(dve, NG, on_kept)
            open_sems(dve, 1, ybo_ready)
            t.open_vector(dve)
            dve.wait_ge(on_zeroed, 1)

            def q_split(i, h, c):
                dve.wait_ge(q_hi_kept, q_count(i, h, c))
                nc.vector.scalar_tensor_tensor(
                    q_lo[:, h % 2, :, c * HB:(c + 1) * HB].rearrange("p s h -> p h s"),
                    psum[:, 7, 0:HB * S].rearrange("p (h s) -> p h s", h=HB),
                    SCALE, q_hi[:, h % 2, :, c * HB:(c + 1) * HB].bitcast(fp32).rearrange("p s h -> p h s"),
                    ALU.mult, ALU.subtract).then_inc(q_lo_kept, 1)

            def maxima(i, u):
                for half in range(2):
                    dve.wait_ge(scores_ready, this(i, 2 * u + half + 1, 2 * NU))
                    nc.vector.tensor_reduce(halfmax[:, u % 2, half:half + 1], psum[:, 2 * half:2 * half + 2, 0:WIDTH[half]],
                                            AX.XY, ALU.max, negate=True).then_inc(halfmax_ready, 1)
                dve.wait_ge(halfmax_ready, this(i, 2 * u + 2, 2 * NU))
                nc.vector.tensor_tensor(negmax[:, u % 2, :], halfmax[:, u % 2, 0:1], halfmax[:, u % 2, 1:2],
                                        ALU.min).then_inc(max_ready, 1)

            def low_part(i, u, r):
                if u not in SINGLE:
                    dve.wait_ge(hi_kept, this(i, 3 * u + r + 1, 3 * NU))
                    tiles = slice(4 * r, 4 * r + 4)
                    nc.vector.tensor_tensor(prT_lo[:, SLOT[u], tiles, :].rearrange("p a b -> p (a b)"), psum[0:KP, 4 + r % 2, :],
                                            prT_hi[:, SLOT[u], tiles, :].rearrange("p a b -> p (a b)").bitcast(fp32),
                                            ALU.subtract).then_inc(lo_kept, 1)

            def inverse(i, u):
                dve.wait_ge(exp_ready, this(i, 2 * u + 2, 2 * NU))
                nc.vector.tensor_tensor(total[:, u % 2, :], rs[:, u % 2, 0:1], rs[:, u % 2, 1:2], ALU.add)\
                    .then_inc(total_ready, 1)
                dve.wait_ge(total_ready, n(i, u))
                nc.vector.reciprocal(rinv[:, u, :], total[:, u % 2, :]).then_inc(rinv_ready, 1)

            def normalise(i, g):
                dve.wait_ge(pv_ready, this(i, g + 1, NG))
                dve.wait_ge(rb_kept, this(i, g + 1, NG))
                if g == 0:
                    dve.wait_ge(y_ready, this(i, 0, 1))
                u, m = GROUPS[g][0], len(GROUPS[g])
                h, p0 = u // UPS, (u % UPS) * UQ
                nc.vector.tensor_tensor(on[:, :, h, p0:p0 + m * UQ],
                                        psum[:, 6, 0:128 * m].rearrange("p (s h) -> p h s", h=H1),
                                        rb[:, g % 2, 0:128 * m].rearrange("p (s h) -> p h s", h=H1), ALU.mult)\
                    .then_inc(on_kept, 1)

            def residual(i):
                dve.wait_ge(y_ready, this(i))
                nc.vector.tensor_tensor(ybo[:, :], psum[:, 7, 0:128], k.bout_row1x[:, :], ALU.add).then_inc(ybo_ready, 1)
                dve.wait_ge(ybo_ready, this(i))
                nc.vector.scalar_tensor_tensor(t.r[:, :, :], ybo[:, :].unsqueeze(1), k.gate_tanh[:, :],
                                               k.x_tok[:, bass.ds(i, 1), :], ALU.mult, ALU.add).then_inc(t.r_ready, 1)
                t.vector_moments(dve, i, 0)

            def step(i, s, first=False, end=False):
                if s:
                    low_part(i, s - 1, 2)
                elif not first:
                    low_part(i - 1, NU - 1, 2)
                if s in PROJECTED and not (end and PROJECTED[s][0] == 2):
                    q_split(i, *PROJECTED[s])
                if s + 1 < NU or not end:
                    maxima(i, s + 1) if s + 1 < NU else maxima(i + 1, 0)
                inverse(i, s)
                low_part(i, s, 0)
                low_part(i, s, 1)
                if s == 3 and not first:
                    residual(i - 1)
                if s == 5 and not first:
                    t.vector_normalise(dve, i - 1, 0)
                if s == 6 and not first:
                    t.vector_logits(dve, i - 1, 0, psum[:, 7, 0:E])
                g = group_at(GROUP_END, i, s, first)
                if g:
                    normalise(*g)

            def prologue():
                for c in range(NB):
                    q_split(0, 0, c)
                maxima(0, 0)

            def epilogue():
                i = PAIRS - 1
                low_part(i, NU - 1, 2)
                normalise(i, NG - 2)
                normalise(i, NG - 1)
                residual(i)
                t.vector_normalise(dve, i, 0)
                t.vector_logits(dve, i, 0, psum[:, 7, 0:E])

            run(dve, step, prologue, epilogue)

        @block.scalar
        def _(act):
            open_sems(act, 2 * NB, q_hi_kept)
            open_sems(act, 2 * NU, exp_ready)
            open_sems(act, 3 * NU, hi_kept)
            open_sems(act, NG, rb_kept)
            t.open_scalar(act)

            def q_high(i, h, c):
                if c == 0:
                    act.wait_ge(scores_ready, this(i, 2 * (h - 1) * UPS, 2 * NU))
                act.wait_ge(q_ready, q_count(i, h, c))
                nc.scalar.activation(
                    q_hi[:, h % 2, :, c * HB:(c + 1) * HB].rearrange("p s h -> p h s"),
                    psum[:, 7, 0:HB * S].rearrange("p (h s) -> p h s", h=HB), ACT.Copy, scale=SCALE).then_inc(q_hi_kept, 1)

            def high_part(i, u, r):
                act.wait_ge(prT_ready, this(i, 3 * u + r + 1, 3 * NU))
                act.wait_ge(pv_ready, groups_before(i, u))
                dst = prT_single[:, 4 * r:4 * r + 4, :] if u in SINGLE else prT_hi[:, SLOT[u], 4 * r:4 * r + 4, :]
                nc.scalar.activation(dst.rearrange("p a b -> p (a b)"), psum[0:KP, 4 + r % 2, :], ACT.Copy)\
                    .then_inc(hi_kept, 1)

            def exponentials(i, u):
                act.wait_ge(max_ready, n(i, u))
                act.wait_ge(prT_ready, this(i, 3 * (u - 1), 3 * NU))
                act.wait_ge(total_ready, n(i, u - 2))
                for half in range(2):
                    keys = slice(FIRST[half], FIRST[half] + 2 * WIDTH[half])
                    nc.scalar.activation(pr[:, u % 2, keys].rearrange("p (a c) -> p a c", a=2),
                                         psum[:, 2 * half:2 * half + 2, 0:WIDTH[half]], ACT.Exp, bias=negmax[:, u % 2, :],
                                         accum_out=rs[:, u % 2, half:half + 1]).then_inc(exp_ready, 1)

            def keep_spread(i, g):
                act.wait_ge(rb_ready, this(i, g + 1, NG))
                act.wait_ge(on_kept, this(i, g - 1, NG))
                m = 128 * len(GROUPS[g])
                nc.scalar.activation(rb[:, g % 2, 0:m], psum[:, 7, 256:256 + m], ACT.Copy).then_inc(rb_kept, 1)

            def step(i, s, first=False, end=False):
                if s:
                    high_part(i, s - 1, 2)
                elif not first:
                    high_part(i - 1, NU - 1, 2)
                if s in PROJECTED and not (end and PROJECTED[s][0] == 2):
                    q_high(i, *PROJECTED[s])
                g = group_at(SPREAD_AT, i, s, first)
                if g:
                    keep_spread(*g)
                high_part(i, s, 0)
                high_part(i, s, 1)
                if s == 6 and not first:
                    t.scalar_store(act, i - 1, 0, psum[:, 7, 128:256])
                if s + 1 < NU or not end:
                    exponentials(i, s + 1) if s + 1 < NU else exponentials(i + 1, 0)

            def prologue():
                for c in range(NB):
                    q_high(0, 0, c)
                exponentials(0, 0)

            def epilogue():
                i = PAIRS - 1
                high_part(i, NU - 1, 2)
                keep_spread(i, NG - 2)
                keep_spread(i, NG - 1)
                t.scalar_store(act, i, 0, psum[:, 7, 128:256])

            run(act, step, prologue, epilogue)


def declare(k, ctx):
    sb = lambda name, shape, dt=fp32: k.sb(ctx, name, shape, dt)
    k.x_tok = sb("x_tok", [128, PAIRS, D])
    k.x_feat = sb("x_feat", [128, B, S])
    k.ident = sb("ident", [128, 128])
    k.window_mask = sb("window_mask", [128, S])
    k.head_mask = sb("head_mask", [128, H0])
    k.value_mask = sb("value_mask", [128, H0 // 2, 2, DH0])
    k.minus_half = sb("minus_half", [128, 1])
    k.eps = sb("eps", [128, 1])
    k.expert_index_u = sb("expert_index_u", [128, E], u32)
    k.expert_index = sb("expert_index", [128, E])
    k.wqT0, k.wkT0, k.wvT0, k.woT0 = (sb(n, [128, D]) for n in ("wqT0", "wkT0", "wvT0", "woT0"))
    k.bq0, k.bk0, k.bv0 = (sb(n, [128, 1]) for n in ("bq0", "bk0", "bv0"))
    k.bq0_scaled = sb("bq0_scaled", [128, 1])
    k.bo_row0 = sb("bo_row0", [128, D])
    k.wqT0x, k.wk0x, k.wvT0x, k.woT0x = (sb(n, [128, D]) for n in ("wqT0x", "wk0x", "wvT0x", "woT0x"))
    k.bq0x, k.bv0x = (sb(n, [128, 1]) for n in ("bq0x", "bv0x"))
    k.bo_row0x = sb("bo_row0x", [128, D])
    k.cross_row = sb("cross_row", [128, D])
    k.router0 = sb("router0", [128, E])
    k.ln_g1, k.ln_b1, k.mix_b1, k.bi1, k.bg1, k.bso1 = (sb(n, [128, 1]) for n in ("ln_g1", "ln_b1", "mix_b1", "bi1", "bg1", "bso1"))
    k.mix_w1 = sb("mix_w1", [128, 3])
    k.wi1, k.wg1, k.wout1 = (sb(n, [128, D]) for n in ("wi1", "wg1", "wout1"))
    k.wsin1, k.wd1, k.wsel1 = (sb(n, [128, 32]) for n in ("wsin1", "wd1", "wsel1"))
    k.wso1 = sb("wso1", [32, D])
    k.bsin1, k.bd1, k.bsel1 = (sb(n, [32, 1]) for n in ("bsin1", "bd1", "bsel1"))
    k.bout_row1 = sb("bout_row1", [128, D])
    k.gamma1, k.beta1 = (sb(n, [128, 1]) for n in ("gamma1", "beta1"))
    k.key_query = sb("key_query", [128, H1, D])
    k.value_out = sb("value_out", [128, H1, D])
    k.bout_row1x = sb("bout_row1x", [128, D])
    k.gate_in, k.gate_tanh = sb("gate_in", [128, 1]), sb("gate_tanh", [128, 1])
    k.router1 = sb("router1", [128, E])
    k.router_bias_row1 = sb("router_bias_row1", [128, E])
    k.logits = sb("logits", [128, PAIRS, E])
    k.expert_weights = sb("expert_weights", [128, PAIRS, E])
    sem = lambda name: k.sem(ctx, name)
    k.weights_loaded = sem("weights_loaded")
    k.loads = [
        ("L0_wqT", k.wqT0[:, :]), ("L0_wkT", k.wkT0[:, :]), ("L0_wvT", k.wvT0[:, :]), ("L0_woT", k.woT0[:, :]),
        ("L0_bq", k.bq0[:, :]), ("L0_bk", k.bk0[:, :]), ("L0_bv", k.bv0[:, :]), ("L0_bo", k.bo_row0[:, :]),
        ("X0_wqT", k.wqT0x[:, :]), ("X0_wk", k.wk0x[:, :]), ("X0_wvT", k.wvT0x[:, :]), ("X0_woT", k.woT0x[:, :]),
        ("X0_bq", k.bq0x[:, :]), ("X0_bv", k.bv0x[:, :]), ("X0_bo", k.bo_row0x[:, :]), ("gate", k.gate_in[:, :]),
    ]
    k.late_loads = [
        ("F0_router", k.router0[:, :]),
        ("L1_ln_g", k.ln_g1[:, :]), ("L1_ln_b", k.ln_b1[:, :]), ("L1_mix_b", k.mix_b1[:, :]),
        ("L1_bi", k.bi1[:, :]), ("L1_bg", k.bg1[:, :]), ("L1_bso", k.bso1[:, :]), ("L1_mix_w", k.mix_w1[:, :]),
        ("L1_wi", k.wi1[:, :]), ("L1_wg", k.wg1[:, :]), ("L1_wout", k.wout1[:, :]),
        ("L1_wsin", k.wsin1[:, :]), ("L1_wd", k.wd1[:, :]), ("L1_wsel", k.wsel1[:, :]), ("L1_wso", k.wso1[:, :]),
        ("L1_bsin", k.bsin1[:, :]), ("L1_bd", k.bd1[:, :]), ("L1_bsel", k.bsel1[:, :]), ("L1_bout", k.bout_row1[:, :]),
        ("L1_gamma", k.gamma1[:, :]), ("L1_beta", k.beta1[:, :]), ("X1_bout", k.bout_row1x[:, :]),
        ("F1_router", k.router1[:, :]), ("F1_router_bias", k.router_bias_row1[:, :]),
    ]


def declare_weights0(k, ctx):
    sb = lambda name, shape: k.sb(ctx, name, shape)
    k.up0 = sb("up0", [128, E, U0])
    k.up_bias0 = sb("up_bias0", [128, E, U0 // 128])
    k.down0 = sb("down0", [128, E, U0 // 128, D])
    k.down_bias0 = sb("down_bias0", [128, E])
    k.late_loads += [("F0_up", k.up0[:, :, :]), ("F0_up_bias", k.up_bias0[:, :, :]),
                     ("F0_down", k.down0[:, :, :, :]), ("F0_down_bias", k.down_bias0[:, :])]


def declare_context_ring(k, ctx):
    k.ctxT = k.sb(ctx, "ctxT", [128, 2, 2, C])
    k.ctxN = k.sb(ctx, "ctxN", [KP, 2, 2, KT * D])
    k.ctxT_loaded = [ctx.enter_context(k.nc.semaphore(f"ctxT_loaded{p}")) for p in range(2)]
    k.ctxN_loaded = [ctx.enter_context(k.nc.semaphore(f"ctxN_loaded{p}")) for p in range(2)]
    k.context_semaphores = [s.num for s in k.ctxT_loaded + k.ctxN_loaded]


def declare_parts(k, ctx, layer, **weights):
    k.parts = {}
    for name, source in weights.items():
        shape = list(source.shape)
        k.parts[name] = (source, k.sb(ctx, f"{name}_hi{layer}", shape, fp32r), k.sb(ctx, f"{name}_lo{layer}", shape, fp32r))


def declare_weights1(k, ctx):
    sb = lambda name, shape: k.sb(ctx, name, shape)
    k.gate1 = sb("gate1", [128, E + 1, I1])
    k.up1 = sb("up1", [128, E + 1, I1])
    k.down1 = sb("down1", [128, E + 1, I1 // 128, D])
    k.expert_loads = {
        "gate": [("F1_gate", k.gate1[:, 0:E, :]), ("F1_gate_s", k.gate1[:, E, :])],
        "up": [("F1_up", k.up1[:, 0:E, :]), ("F1_up_s", k.up1[:, E, :])],
        "down": [("F1_down", k.down1[:, 0:E, :, :]), ("F1_down_s", k.down1[:, E, :, :])],
    }


ROWS = ("L0_bo", "X0_bo", "L1_bout", "X1_bout", "F1_router_bias", "gate")


def layouts(a):
    c = np.ascontiguousarray
    col = lambda v: c(v.reshape(-1, 1))
    ctx = a["ctx_1024"]
    w_kv = a["L1_xattn_w_kv"]
    halves = lambda w: c(w.reshape(DH1, 2, H1 // 2, D).transpose(1, 0, 2, 3).reshape(2 * DH1, H1 // 2, D))
    heads = lambda w: halves(w.reshape(D, H1, DH1).transpose(2, 1, 0))
    out = {
        "x_pairs": c(a["x"].reshape(PAIRS, 2, S, D).transpose(1, 2, 0, 3)),
        "xT": c(a["x"].transpose(2, 0, 1)),
        "ctxT": c(ctx.transpose(0, 2, 1)),
        "ctxN": c(ctx.reshape(B, KT, KP, D).transpose(0, 2, 1, 3)),
        "L0_wqT": c(a["L0_attn_wq"].T), "L0_wkT": c(a["L0_attn_wk"].T),
        "L0_wvT": c(a["L0_attn_wv"].T), "L0_woT": c(a["L0_attn_wo"].T),
        "L0_bq": col(a["L0_attn_bq"]), "L0_bk": col(a["L0_attn_bk"]), "L0_bv": col(a["L0_attn_bv"]), "L0_bo": a["L0_attn_bo"],
        "X0_wqT": c(a["L0_xattn_Wq"].T), "X0_wk": a["L0_xattn_Wk"], "X0_wvT": c(a["L0_xattn_Wv"].T),
        "X0_woT": c(a["L0_xattn_Wo"].T), "X0_bq": col(a["L0_xattn_bq"]), "X0_bv": col(a["L0_xattn_bv"]), "X0_bo": a["L0_xattn_bo"],
        "F0_router": c(a["L0_ffn_w_router"].T), "F0_up": c(a["L0_ffn_w_up"].transpose(2, 0, 1)),
        "F0_up_bias": c(a["L0_ffn_b_up"].reshape(E, U0 // 128, 128).transpose(2, 0, 1)),
        "F0_down": c(a["L0_ffn_w_down"].reshape(E, D, U0 // 128, 128).transpose(3, 0, 2, 1)),
        "F0_down_bias": c(a["L0_ffn_b_down"].T),
        "L1_ln_g": col(a["L1_attn_ln_g"]), "L1_ln_b": col(a["L1_attn_ln_b"]), "L1_mix_b": col(a["L1_attn_mix_b"]),
        "L1_mix_w": c(a["L1_attn_mix_w"].reshape(D, 3)),
        "L1_wi": a["L1_attn_Wi"], "L1_wg": a["L1_attn_Wg"], "L1_wout": a["L1_attn_Wout"], "L1_wsin": a["L1_attn_Wsin"],
        "L1_wd": a["L1_attn_Wd"], "L1_wsel": a["L1_attn_Wsel"], "L1_wso": a["L1_attn_Wso"],
        "L1_bi": col(a["L1_attn_bi"]), "L1_bg": col(a["L1_attn_bg"]), "L1_bso": col(a["L1_attn_bso"]),
        "L1_bsin": col(a["L1_attn_bsin"]), "L1_bd": col(a["L1_attn_bd"]), "L1_bsel": col(a["L1_attn_bsel"]),
        "L1_bout": a["L1_attn_bout"],
        "L1_gamma": col(a["L1_xattn_ln_gamma"]), "L1_beta": col(a["L1_xattn_ln_beta"]),
        "L1_wqT": heads(a["L1_xattn_w_q"]), "L1_wkT": heads(c(w_kv[:, :H1 * DH1])), "L1_wvT": heads(c(w_kv[:, H1 * DH1:])),
        "L1_wo": halves(a["L1_xattn_w_out"].reshape(H1, DH1, D).transpose(1, 0, 2)),
        "X1_bout": a["L1_xattn_b_out"], "gate": a["L1_xattn_gate"],
        "F1_router": c(a["L1_ffn_router_w"].T), "F1_router_bias": a["L1_ffn_routing_bias"],
        "F1_gate": c(a["L1_ffn_gate_w"].transpose(1, 0, 2)), "F1_up": c(a["L1_ffn_up_w"].transpose(1, 0, 2)),
        "F1_down": c(a["L1_ffn_down_w"].reshape(E, I1 // 128, 128, D).transpose(2, 0, 1, 3)),
        "F1_gate_s": c(a["L1_ffn_shared_gate"].T), "F1_up_s": c(a["L1_ffn_shared_up"].T),
        "F1_down_s": c(a["L1_ffn_shared_down"].reshape(D, I1 // 128, 128).transpose(2, 1, 0)),
    }
    return {name: c(v) for name, v in out.items()}
def build(nc, dram, out):
    with ExitStack() as ctx:
        k = Core(nc, ctx, dram)
        k.out = out
        declare(k, ctx)

        def run(*phases):
            for phase in phases:
                phase(k)
                k.clear_semaphores()

        with ExitStack() as layer0:
            declare_weights0(k, layer0)
            with ExitStack() as ring:
                declare_context_ring(k, ring)
                run(setup_phase, self_attention_phase, context_attention_phase)
            with ExitStack() as parts:
                declare_parts(k, parts, 0, up=k.up0, down=k.down0)
                run(expert_phase0)
        run(state_space_phase, cross_attention_phase)
        with ExitStack() as layer1:
            declare_weights1(k, layer1)
            declare_parts(k, layer1, 1, gate=k.gate1, up=k.up1, down=k.down1)
            run(expert_phase1)


def kernel(**inputs):
    import concourse.bacc as bacc
    from concourse.bass_utils import run_bass_kernel_spmd

    arrays = {"in_" + name: a for name, a in layouts({n: np.asarray(v) for n, v in inputs.items()}).items()}
    nc = bacc.Bacc("TRN2", target_bir_lowering=False, num_devices=1)
    dram = {}
    for name, a in arrays.items():
        ap = nc.dram_tensor(name, list(a.shape), fp32, kind="ExternalInput").ap()
        name = name[3:]
        dram[name] = ap.partition_broadcast(128) if name in ROWS else ap
    out = nc.dram_tensor("out_0", [B, S, D], fp32, kind="ExternalOutput").ap()
    build(nc, dram, out)
    r = run_bass_kernel_spmd(nc, [arrays], core_ids=[0])
    return r.results[0]["out_0"]
```

```python
from contextlib import ExitStack

import numpy as np
import concourse.bass as bass
from concourse import mybir

fp32 = mybir.dt.float32
fp32r = mybir.dt.float32r
u32 = mybir.dt.uint32
ALU = mybir.AluOpType
ACT = mybir.ActivationFunctionType
AX = mybir.AxisListType

B, S, D = 32, 56, 128
SP = 64
PAIRS = B // 2
CK = 4
CHUNKS = PAIRS // CK
CB = 2 * CK
CT = CB * S
C, KT, KP = 1500, 12, 125
H0, DH0, WIN = 16, 8, 32
H1, DH1 = 16, 64
E, U0, I1 = 8, 512, 256
EPS = 1e-5
NEG = -1.0e30


def this(i, n=1, per=1):
    return i * per + (per + n)


def last(i, n=1, per=1):
    return i * per + n


class Core:

    def __init__(self, nc, ctx, dram):
        self.nc, self.ctx, self.dram = nc, ctx, dram
        self.used = []

    def sb(self, ctx, name, shape, dt=fp32):
        return ctx.enter_context(self.nc.sbuf_tensor(name, shape, dt))

    def sem(self, ctx, name):
        handle = ctx.enter_context(self.nc.semaphore(name))
        self.used.append(handle.num)
        return handle

    def clear_semaphores(self):
        nums, self.used = sorted(self.used), []
        with self.nc.Block() as block:
            @block.gpsimd
            def _(pool):
                start = nums[0]
                for a, b in zip(nums, nums[1:] + [None]):
                    if b != a + 1:
                        pool.sem_clear(range(start, a + 1))
                        start = b


def setup_phase(k):
    nc, d = k.nc, k.dram
    with ExitStack() as ctx:
        consts_built = k.sem(ctx, "consts_built")
        pads_zeroed = k.sem(ctx, "pads_zeroed")
        x_loaded = k.sem(ctx, "x_loaded")
        tanh_gate_ready = k.sem(ctx, "tanh_gate_ready")
        row_ready = k.sem(ctx, "row_ready")
        psum = ctx.enter_context(nc.psum_tensor("setup_psum", [128, 8, 512], fp32))
        consts_ready = k.sem(ctx, "consts_ready")
        block = ctx.enter_context(nc.Block())

        @block.sync
        def _(sp):
            for name, dst in k.loads:
                sp.dma_start(dst, d[name]).then_inc(k.weights_loaded, 16)
            sp.dma_start(k.x_feat[:, :, :], d["xT"]).then_inc(x_loaded, 16)
            sp.wait_ge(pads_zeroed, 1)
            for h in range(2):
                sp.dma_start(k.x_tok[h * SP:h * SP + S, :, :], d["x_pairs"][h]).then_inc(x_loaded, 16)
            sp.wait_ge(x_loaded, 3 * 16)

        @block.gpsimd
        def _(pool):
            n = 0

            def step(instruction):
                nonlocal n
                n += 1
                instruction.then_inc(consts_built, 1)

            step(pool.memset(k.ident[:, :], 0.0))
            step(pool.memset(k.window_mask[:, :], 0.0))
            step(pool.memset(k.head_mask[:, :], 1.0))
            step(pool.memset(k.value_mask[:, :, :, :], 1.0))
            step(pool.memset(k.minus_half[:, :], -0.5))
            step(pool.memset(k.eps[:, :], EPS))
            pool.wait_ge(consts_built, n)
            step(pool.affine_select(out=k.ident[:, :], in_=k.ident[:, :], compare_op=ALU.not_equal,
                                    fill=1.0, base=0, pattern=[[-1, 128]], channel_multiplier=1))
            for half in range(2):
                rows = k.window_mask[half * SP:(half + 1) * SP, :]
                pool.wait_ge(consts_built, n)
                step(pool.affine_select(out=rows, in_=rows, compare_op=ALU.is_ge, fill=NEG,
                                        base=WIN, pattern=[[-1, S]], channel_multiplier=1))
                pool.wait_ge(consts_built, n)
                step(pool.affine_select(out=rows, in_=rows, compare_op=ALU.is_ge, fill=NEG,
                                        base=WIN, pattern=[[1, S]], channel_multiplier=-1))
            pool.wait_ge(consts_built, n)
            step(pool.affine_select(out=k.head_mask[:, :], in_=k.head_mask[:, :], compare_op=ALU.is_ge,
                                    fill=0.0, base=0, pattern=[[-DH0, H0]], channel_multiplier=1))
            pool.wait_ge(consts_built, n)
            step(pool.affine_select(out=k.head_mask[:, :], in_=k.head_mask[:, :], compare_op=ALU.is_ge,
                                    fill=0.0, base=DH0 - 1, pattern=[[DH0, H0]], channel_multiplier=-1))
            pool.wait_ge(consts_built, n)
            even = k.value_mask[:, :, 0, :]
            step(pool.affine_select(out=even, in_=even, compare_op=ALU.is_ge, fill=0.0,
                                    base=S - 1, pattern=[[0, H0 // 2], [0, DH0]], channel_multiplier=-1))
            odd = k.value_mask[:, :, 1, :]
            step(pool.affine_select(out=odd, in_=odd, compare_op=ALU.is_ge, fill=0.0,
                                    base=-S, pattern=[[0, H0 // 2], [0, DH0]], channel_multiplier=1))
            step(pool.iota(k.expert_index_u[:, :], pattern=[[1, E]], base=0, channel_multiplier=0))
            pool.wait_ge(consts_built, n)
            step(pool.tensor_copy(k.expert_index[:, :], k.expert_index_u[:, :]))
            pool.wait_ge(consts_built, n)

        @block.vector
        def _(dve):
            dve.memset(k.x_tok[:, :, :], 0.0).then_inc(pads_zeroed, 1)
            dve.wait_ge(row_ready, 1)
            nc.vector.tensor_tensor(k.cross_row[:, :], psum[:, 0, 0:D], k.bo_row0x[:, :], ALU.add)\
                .then_inc(consts_ready, 1)
            nc.vector.tensor_copy(k.value_out0[:, :], psum[:, 0, D:2 * D]).then_inc(consts_ready, 1)
            nc.vector.tensor_scalar(k.bq0_scaled[:, :], k.bq0[:, :], DH0 ** -0.5, None, ALU.mult).then_inc(consts_ready, 1)
            dve.wait_ge(consts_ready, 3)
            dve.wait_ge(tanh_gate_ready, 1)
            dve.wait_ge(pads_zeroed, 1)

        @block.tensor
        def _(pe):
            pe.wait_ge(k.weights_loaded, 16 * len(k.loads))
            nc.tensor.matmul(psum[:, 0, 0:D], k.bv0x[:, 0:1].to_broadcast([128, 128]), k.woT0x[:, :],
                             start=True, stop=True)
            nc.tensor.matmul(psum[:, 0, D:2 * D], k.wv0x[:, :], k.woT0x[:, :], start=True, stop=True).then_inc(row_ready, 1)

        @block.scalar
        def _(act):
            act.wait_ge(k.weights_loaded, 16 * len(k.loads))
            nc.scalar.activation(k.gate_tanh[:, :], k.gate_in[:, :], ACT.Tanh).then_inc(tanh_gate_ready, 1)


def open_sems(engine, per, *sems):
    for s in sems:
        engine.sem_inc(s, per)


class Tail:

    def __init__(self, k, ctx, tag, inner=None, router=None, final=False, per=None):
        sem = lambda name: k.sem(ctx, f"{tag}_{name}")
        self.k, self.inner, self.router, self.final = k, inner, router, final
        self.per = per or CK
        self.r = k.sb(ctx, tag + "_r", [128, self.per, D])
        self.moments = k.sb(ctx, tag + "_moments", [128, self.per, 6])
        self.mean_var = k.sb(ctx, tag + "_mean_var", [128, self.per, 2])
        self.var_eps = k.sb(ctx, tag + "_var_eps", [128, self.per, 1])
        self.rstd = k.sb(ctx, tag + "_rstd", [128, self.per, 1])
        self.xn = k.sb(ctx, tag + "_xn", [128, self.per, D])
        self.r_ready = sem("r_ready")
        self.moments_ready = sem("moments_ready")
        self.mean_var_ready = sem("mean_var_ready")
        self.var_eps_ready = sem("var_eps_ready")
        self.aggregating = sem("aggregating")
        self.storing = sem("storing")
        self.rstd_ready = sem("rstd_ready")
        self.xn_ready = sem("xn_ready")
        self.xnT_ready = sem("xnT_ready")
        self.feat_stored = sem("feat_stored")
        self.tok_stored = sem("tok_stored")
        if inner:
            self.moments2 = k.sb(ctx, tag + "_moments2", [128, self.per, 6])
            self.mean_var2 = k.sb(ctx, tag + "_mean_var2", [128, self.per, 2])
            self.var_eps2 = k.sb(ctx, tag + "_var_eps2", [128, self.per, 1])
            self.rstd2 = k.sb(ctx, tag + "_rstd2", [128, self.per, 1])
            self.xn2 = k.sb(ctx, tag + "_xn2", [128, self.per, D])
            self.moments2_ready = sem("moments2_ready")
            self.mean_var2_ready = sem("mean_var2_ready")
            self.var_eps2_ready = sem("var_eps2_ready")
            self.rstd2_ready = sem("rstd2_ready")
            self.xn2_ready = sem("xn2_ready")
        if router is not None:
            self.xnT = k.sb(ctx, tag + "_xnT", [128, 128])
            self.xnT_kept = sem("xnT_kept")
            self.logits_ready = sem("logits_ready")
            self.logits_kept = sem("logits_kept")
        self.out = self.xn2 if inner else self.xn
        self.out_ready = self.xn2_ready if inner else self.xn_ready

    def open_vector(self, dve):
        open_sems(dve, self.per, self.r_ready, self.moments_ready, self.mean_var_ready, self.xn_ready)
        if self.inner:
            open_sems(dve, self.per, self.moments2_ready, self.mean_var2_ready, self.xn2_ready)

        if self.router is not None:
            open_sems(dve, self.per, self.logits_kept)

    def open_pool(self, pool):
        open_sems(pool, self.per, self.var_eps_ready, self.rstd_ready, self.tok_stored)
        if self.inner:
            open_sems(pool, self.per, self.var_eps2_ready, self.rstd2_ready)

    def open_tensor(self, pe):
        open_sems(pe, self.per, self.xnT_ready)
        if self.router is not None:
            open_sems(pe, self.per, self.logits_ready)

    def open_scalar(self, act):
        open_sems(act, self.per, self.feat_stored)
        if self.router is not None:
            open_sems(act, self.per, self.xnT_kept)

    def vector_moments(self, dve, i, p):
        nc = self.k.nc
        dve.wait_ge(self.r_ready, this(i, p + 1, self.per))
        nc.vector.bn_stats(self.moments[:, p, :], self.r[:, p, :]).then_inc(self.moments_ready, 1)
        dve.wait_ge(self.moments_ready, this(i, p + 1, self.per))
        dve.sem_inc(self.aggregating, 1)
        nc.vector.bn_aggr(self.mean_var[:, p, :], self.moments[:, p, :]).then_inc(self.mean_var_ready, 1)

    def pool_rstd(self, pool, i, p):
        pool.wait_ge(self.mean_var_ready, this(i, p + 1, self.per))
        pool.tensor_tensor(self.var_eps[:, p, :], self.mean_var[:, p, 1:2], self.k.eps[:, :], ALU.add)\
            .then_inc(self.var_eps_ready, 1)
        pool.wait_ge(self.var_eps_ready, this(i, p + 1, self.per))
        pool.wait_ge(self.xn_ready, last(i, p + 1, self.per))
        pool.tensor_tensor(self.rstd[:, p, :], self.var_eps[:, p, :], self.k.minus_half[:, :], ALU.pow)\
            .then_inc(self.rstd_ready, 1)

    def vector_normalise(self, dve, i, p):
        nc = self.k.nc
        dve.wait_ge(self.rstd_ready, this(i, p + 1, self.per))
        if self.final:
            nc.vector.tensor_scalar(self.k.x_tok[:, bass.ds(i * self.per + p, 1), :], self.r[:, p:p + 1, :],
                                    self.mean_var[:, p, 0:1], self.rstd[:, p, :], ALU.subtract, ALU.mult)\
                .then_inc(self.xn_ready, 1)
            return
        if not self.inner:
            dve.wait_ge(self.xnT_ready, last(i, p + 1, self.per))
        dve.wait_ge(self.tok_stored, last(i, p + 1, self.per))
        nc.vector.tensor_scalar(self.xn[:, p, :], self.r[:, p, :], self.mean_var[:, p, 0:1],
                                self.rstd[:, p, :], ALU.subtract, ALU.mult).then_inc(self.xn_ready, 1)

    def vector_inner_moments(self, dve, i, p):
        nc = self.k.nc
        dve.wait_ge(self.xn_ready, this(i, p + 1, self.per))
        nc.vector.bn_stats(self.moments2[:, p, :], self.xn[:, p, :]).then_inc(self.moments2_ready, 1)
        dve.wait_ge(self.moments2_ready, this(i, p + 1, self.per))
        dve.sem_inc(self.aggregating, 1)
        nc.vector.bn_aggr(self.mean_var2[:, p, :], self.moments2[:, p, :]).then_inc(self.mean_var2_ready, 1)

    def pool_inner_rstd(self, pool, i, p):
        pool.wait_ge(self.mean_var2_ready, this(i, p + 1, self.per))
        pool.tensor_tensor(self.var_eps2[:, p, :], self.mean_var2[:, p, 1:2], self.k.eps[:, :], ALU.add)\
            .then_inc(self.var_eps2_ready, 1)
        pool.wait_ge(self.var_eps2_ready, this(i, p + 1, self.per))
        pool.wait_ge(self.xn2_ready, last(i, p + 1, self.per))
        pool.tensor_tensor(self.rstd2[:, p, :], self.var_eps2[:, p, :], self.k.minus_half[:, :], ALU.pow)\
            .then_inc(self.rstd2_ready, 1)

    def vector_inner_normalise(self, dve, i, p):
        nc = self.k.nc
        dve.wait_ge(self.rstd2_ready, this(i, p + 1, self.per))
        dve.wait_ge(self.xnT_ready, last(i, p + 1, self.per))
        nc.vector.tensor_scalar(self.xn2[:, p, :], self.xn[:, p, :], self.mean_var2[:, p, 0:1],
                                self.rstd2[:, p, :], ALU.subtract, ALU.mult).then_inc(self.xn2_ready, 1)

    def pool_store(self, pool, i, p):
        pool.wait_ge(self.xn_ready, this(i, p + 1, self.per))
        pool.sem_inc(self.storing, 1)
        pool.tensor_copy(self.k.x_tok[:, bass.ds(i * self.per + p, 1), :], self.xn[:, p:p + 1, :])\
            .then_inc(self.tok_stored, 1)

    def tensor_transpose(self, pe, i, p, bank):
        pe.wait_ge(self.out_ready, this(i, p + 1, self.per))
        pe.transpose(bank, self.out[:, p, :], self.k.ident[:, :]).then_inc(self.xnT_ready, 1)

    def scalar_store(self, act, i, p, bank):
        k = self.k
        act.wait_ge(self.xnT_ready, this(i, p + 1, self.per))
        if self.router is not None:
            act.wait_ge(self.logits_ready, last(i, self.per, self.per) if p == 0 else this(i, p, self.per))
            k.nc.scalar.activation(self.xnT[:, :], bank, ACT.Copy).then_inc(self.xnT_kept, 1)
        src = bank.rearrange("p (b s) -> p b s", b=2)[:, :, 0:S]
        dst = k.x_feat[:, bass.ds(2 * (i * self.per + p), 2), :]
        if self.inner:
            gain, bias = self.inner
            k.nc.scalar.activation(dst, src, ACT.Identity, bias=bias, scale=gain)\
                .then_inc(self.feat_stored, 1)
        else:
            k.nc.scalar.activation(dst, src, ACT.Copy).then_inc(self.feat_stored, 1)


    def tensor_logits(self, pe, i, p, bank):
        pe.wait_ge(self.xnT_kept, this(i, p + 1, self.per))
        pe.matmul(bank, self.xnT[:, :], self.router[:, :], start=True, stop=True).then_inc(self.logits_ready, 1)

    def vector_logits(self, dve, i, p, bank):
        dve.wait_ge(self.logits_ready, this(i, p + 1, self.per))
        self.k.nc.vector.tensor_copy(self.k.logits[:, bass.ds(i * self.per + p, 1), :],
                                     bank.unsqueeze(1)).then_inc(self.logits_kept, 1)


class PairSteps:

    PER = 2

    def __init__(self, **lag):
        self.lag = lag
        self.fill = -(-max(lag.values()) // self.PER) * self.PER

    def count(self, i, s, lag):
        pairs = s - lag + 1
        if isinstance(i, int):
            pairs = max(min(pairs, PAIRS - i * self.PER), -i * self.PER)
        return this(i, pairs, self.PER)

    def pair(self, i, s, stage):
        d = s - self.lag[stage]
        if isinstance(i, int) and not 0 <= i * self.PER + d < PAIRS:
            return None
        return i + d // self.PER, d % self.PER

    def run(self, engine, step):
        PER = self.PER
        for s in range(self.fill):
            step(s // PER, s % PER)
        with engine.Fori(self.fill // PER, PAIRS // PER) as i:
            for s in range(PER):
                step(i, s)
        for s in range(PAIRS, PAIRS + max(self.lag.values())):
            step(s // PER, s % PER)


def self_attention_phase(k):
    nc = k.nc
    HP = H0 // 2
    steps = PairSteps(project=0, scores=1, transpose=2, attend=3, output=4, norm=5)
    PER, pair, n = steps.PER, steps.pair, steps.count
    with ExitStack() as ctx:
        t = Tail(k, ctx, "sa", per=PER)
        sem = lambda name: k.sem(ctx, "sa_" + name)
        xdup = k.sb(ctx, "sa_xdup", [128, PER, 2, 2, S])
        xbo = k.sb(ctx, "sa_xbo", [128, PER, D])
        qs = k.sb(ctx, "sa_qs", [128, PER, 2, SP])
        kf = k.sb(ctx, "sa_kf", [128, PER, 2, S])
        kexp = k.sb(ctx, "sa_kexp", [128, PER, 2, H0, S])
        vexp = k.sb(ctx, "sa_vexp", [2 * S, PER, 2, D])
        sm = k.sb(ctx, "sa_sm", [128, PER, H0, S])
        pr = k.sb(ctx, "sa_pr", [128, PER, H0, S])
        mx = k.sb(ctx, "sa_mx", [128, PER, H0])
        rs = k.sb(ctx, "sa_rs", [128, PER, H0])
        rinv = k.sb(ctx, "sa_rinv", [128, PER, H0])
        prT = k.sb(ctx, "sa_prT", [2 * S, PER, HP, 128])
        on = k.sb(ctx, "sa_on", [128, PER, D])
        oT = k.sb(ctx, "sa_oT", [128, PER, 128])
        psum = ctx.enter_context(nc.psum_tensor("sa_psum", [128, 8, 512], fp32))
        late_weights_loaded = sem("late_weights_loaded")
        qs_zeroed, kq_ready, v_ready = sem("qs_zeroed"), sem("kq_ready"), sem("v_ready")
        q_kept, k_kept, v_kept, xdup_ready = sem("q_kept"), sem("k_kept"), sem("v_kept"), sem("xdup_ready")
        xbo_ready, keys_ready, scores_ready = sem("xbo_ready"), sem("keys_ready"), sem("scores_ready")
        masked, max_ready, shifted = sem("masked"), sem("max_ready"), sem("shifted")
        exp_ready, sum_ready, rinv_ready = sem("exp_ready"), sem("sum_ready"), sem("rinv_ready")
        prT_ready, prT_kept = sem("prT_ready"), sem("prT_kept")
        o_ready, o_kept, oT_ready, oT_kept, y_ready = sem("o_ready"), sem("o_kept"), sem("oT_ready"), sem("oT_kept"), sem("y_ready")
        block = ctx.enter_context(nc.Block())

        @block.sync
        def _(sp):
            for name, dst in k.late_loads:
                sp.dma_start(dst, k.dram[name]).then_inc(late_weights_loaded, 16)
            for p in range(2):
                sp.dma_start(k.ctxT[:, p, :, :], k.dram["ctxT"][2 * p:2 * p + 2, :, :].rearrange("b d c -> d b c"))\
                    .then_inc(k.ctxT_loaded[p], 16)
                sp.dma_start(k.ctxN[:, p, :, :], k.dram["ctxN"][2 * p:2 * p + 2, :, :, :].rearrange("b q t d -> q b (t d)"))\
                    .then_inc(k.ctxN_loaded[p], 16)
            sp.wait_ge(late_weights_loaded, 16 * len(k.late_loads))

        @block.gpsimd
        def _(pool):
            open_sems(pool, PER, xbo_ready, keys_ready)
            t.open_pool(pool)

            def step(i, s):
                at = pair(i, s, "norm")
                if at:
                    t.pool_store(pool, *at)
                at = pair(i, s, "project")
                if at:
                    j, p = at
                    pool.wait_ge(k_kept, this(j, p + 1, PER))
                    pool.wait_ge(scores_ready, last(j, p + 1, PER))
                    for half in range(2):
                        done = pool.tensor_tensor(kexp[:, p, half, :, :],
                                                  kf[:, p, half, :].unsqueeze(1).to_broadcast([128, H0, S]),
                                                  k.head_mask[:, :].unsqueeze(2).to_broadcast([128, H0, S]), ALU.mult)
                    done.then_inc(keys_ready, 1)
                at = pair(i, s, "attend")
                if at:
                    j, p = at
                    pool.wait_ge(t.r_ready, last(j, p + 1, PER))
                    pool.tensor_tensor(xbo[:, p:p + 1, :], k.x_tok[:, bass.ds(j * PER + p, 1), :],
                                       k.bo_row0[:, :].unsqueeze(1), ALU.add).then_inc(xbo_ready, 1)
                at = pair(i, s, "output")
                if at:
                    t.pool_rstd(pool, *at)

            steps.run(pool, step)

        @block.tensor
        def _(pe):
            open_sems(pe, PER, kq_ready, v_ready, scores_ready, prT_ready, o_ready, oT_ready, y_ready)
            t.open_tensor(pe)
            pe.wait_ge(qs_zeroed, 1)

            def step(i, s):
                at = pair(i, s, "project")
                if at:
                    j, p = at
                    x = k.x_feat[:, bass.ds(2 * (j * PER + p), 2), :]
                    pe.wait_ge(q_kept, this(j, p, PER))
                    nc.tensor.matmul(psum[:, 3, 0:2 * S], k.wkT0[:, :], x, start=True, stop=True)
                    nc.tensor.matmul(psum[:, 3, 2 * S:4 * S], k.wqT0[:, :], x, start=True, stop=True).then_inc(kq_ready, 1)
                at = pair(i, s, "scores")
                if at:
                    j, p = at
                    pe.wait_ge(q_kept, this(j, p + 1, PER))
                    pe.wait_ge(keys_ready, this(j, p + 1, PER))
                    pe.wait_ge(masked, this(j, p, PER))
                    for half in range(2):
                        for hh in range(2):
                            done = nc.tensor.matmul(psum[half * SP:(half + 1) * SP, hh, 0:8 * S], qs[:, p, half, :],
                                                    kexp[:, p, half, hh * 8:(hh + 1) * 8, :], start=True, stop=True)
                    done.then_inc(scores_ready, 1)
                at = pair(i, s, "output")
                if at:
                    j, p = at
                    pe.wait_ge(o_kept, this(j, p + 1, PER))
                    pe.wait_ge(t.r_ready, this(j, p, PER))
                    nc.tensor.transpose(psum[:, 7, 0:128], on[:, p, :], k.ident[:, :]).then_inc(oT_ready, 1)
                at = pair(i, s, "transpose")
                if at:
                    j, p = at
                    pe.wait_ge(exp_ready, this(j, p + 1, PER))
                    pe.wait_ge(prT_kept, this(j, p, PER))
                    for hp in range(HP):
                        done = nc.tensor.transpose(psum[0:2 * S, 4 + hp // 4, (hp % 4) * 128:(hp % 4 + 1) * 128],
                                                   pr[:, p, 2 * hp:2 * hp + 2, :], k.ident[:, :])
                    done.then_inc(prT_ready, 1)
                    pe.wait_ge(xdup_ready, this(j, p + 1, PER))
                    pe.wait_ge(v_kept, this(j, p, PER))
                    for half in range(2):
                        done = nc.tensor.matmul(psum[0:2 * S, 2, half * D:(half + 1) * D],
                                                xdup[:, p, half, :, :], k.wvT0[:, :], start=True, stop=True)
                    done.then_inc(v_ready, 1)
                at = pair(i, s, "norm")
                if at:
                    pe.wait_ge(oT_kept, n(i, s, 4))
                    pe.wait_ge(t.r_ready, n(i, s, 5))
                    t.tensor_transpose(pe, *at, psum[:, 7, 256:384])
                at = pair(i, s, "output")
                if at:
                    j, p = at
                    pe.wait_ge(oT_kept, this(j, p + 1, PER))
                    pe.wait_ge(t.feat_stored, n(i, s, 5))
                    nc.tensor.matmul(psum[:, 7, 128:256], oT[:, p, :], k.woT0[:, :], start=True, stop=True)\
                        .then_inc(y_ready, 1)
                at = pair(i, s, "attend")
                if at:
                    j, p = at
                    pe.wait_ge(prT_kept, this(j, p + 1, PER))
                    pe.wait_ge(v_kept, this(j, p + 1, PER))
                    pe.wait_ge(o_kept, this(j, p, PER))
                    for half in range(2):
                        for hp in range(HP):
                            done = nc.tensor.matmul(psum[half * SP:(half + 1) * SP, 6, hp * 16:(hp + 1) * 16],
                                                    prT[:, p, hp, half * SP:(half + 1) * SP],
                                                    vexp[:, p, half, hp * 16:(hp + 1) * 16], start=True, stop=True)
                    done.then_inc(o_ready, 1)

            steps.run(pe, step)

        @block.vector
        def _(dve):
            open_sems(dve, PER, masked, max_ready, shifted, sum_ready, rinv_ready, o_kept, v_kept)
            t.open_vector(dve)
            dve.memset(qs[:, :, :, :], 0.0).then_inc(qs_zeroed, 1)

            def step(i, s):
                at = pair(i, s, "norm")
                if at:
                    t.vector_normalise(dve, *at)
                at = pair(i, s, "scores")
                if at:
                    j, p = at
                    dve.wait_ge(scores_ready, this(j, p + 1, PER))
                    dve.wait_ge(exp_ready, last(j, p + 1, PER))
                    nc.vector.tensor_tensor(sm[:, p, :, :].rearrange("p (a h) s -> p a h s", a=2),
                                            psum[:, 0:2, 0:8 * S].rearrange("p a (h s) -> p a h s", h=8),
                                            k.window_mask[:, :].unsqueeze(1).unsqueeze(1)
                                            .to_broadcast([128, 2, 8, S]), ALU.add).then_inc(masked, 1)
                    dve.wait_ge(masked, this(j, p + 1, PER))
                    nc.vector.reduce_max(mx[:, p, :], sm[:, p, :, :], AX.X).then_inc(max_ready, 1)
                    dve.wait_ge(max_ready, this(j, p + 1, PER))
                    nc.vector.tensor_tensor(sm[:, p, :, :], sm[:, p, :, :],
                                            mx[:, p, :].unsqueeze(2).to_broadcast([128, H0, S]),
                                            ALU.subtract).then_inc(shifted, 1)
                at = pair(i, s, "transpose")
                if at:
                    j, p = at
                    dve.wait_ge(exp_ready, this(j, p + 1, PER))
                    nc.vector.reduce_sum(rs[:, p, :], pr[:, p, :, :], AX.X).then_inc(sum_ready, 1)
                    dve.wait_ge(sum_ready, this(j, p + 1, PER))
                    nc.vector.reciprocal(rinv[:, p, :], rs[:, p, :]).then_inc(rinv_ready, 1)
                    dve.wait_ge(v_ready, this(j, p + 1, PER))
                    dve.wait_ge(o_ready, last(j, p + 1, PER))
                    nc.vector.tensor_tensor(vexp[:, p, :, :],
                                            psum[0:2 * S, 2, 0:2 * D].rearrange("p (b d) -> p b d", b=2),
                                            k.value_mask[0:2 * S, :, :, :].rearrange("p a c j -> p (a c j)")
                                            .unsqueeze(1).to_broadcast([2 * S, 2, D]), ALU.mult).then_inc(v_kept, 1)
                at = pair(i, s, "output")
                if at:
                    j, p = at
                    dve.wait_ge(y_ready, this(j, p + 1, PER))
                    dve.wait_ge(xbo_ready, this(j, p + 1, PER))
                    nc.vector.tensor_tensor(t.r[:, p, :], psum[:, 7, 128:256], xbo[:, p, :], ALU.add)\
                        .then_inc(t.r_ready, 1)
                    t.vector_moments(dve, j, p)
                at = pair(i, s, "attend")
                if at:
                    j, p = at
                    dve.wait_ge(rinv_ready, this(j, p + 1, PER))
                    dve.wait_ge(o_ready, this(j, p + 1, PER))
                    dve.wait_ge(oT_ready, last(j, p + 1, PER))
                    nc.vector.tensor_tensor(on[:, p, :].rearrange("p (h d) -> p h d", h=H0),
                                            psum[:, 6, 0:128].rearrange("p (h d) -> p h d", h=H0),
                                            rinv[:, p, :].unsqueeze(2).to_broadcast([128, H0, DH0]),
                                            ALU.mult).then_inc(o_kept, 1)

            steps.run(dve, step)

        @block.scalar
        def _(act):
            open_sems(act, PER, exp_ready, prT_kept, oT_kept, k_kept, q_kept, xdup_ready)
            t.open_scalar(act)
            act.wait_ge(qs_zeroed, 1)

            def step(i, s):
                at = pair(i, s, "project")
                if at:
                    j, p = at
                    act.wait_ge(kq_ready, this(j, p + 1, PER))
                    act.wait_ge(keys_ready, last(j, p + 1, PER))
                    nc.scalar.activation(kf[:, p, :, :], psum[:, 3, 0:2 * S].rearrange("p (b s) -> p b s", b=2),
                                         ACT.Identity, bias=k.bk0[:, :]).then_inc(k_kept, 1)
                    act.wait_ge(scores_ready, last(j, p + 1, PER))
                    nc.scalar.activation(qs[:, p, :, 0:S], psum[:, 3, 2 * S:4 * S].rearrange("p (b s) -> p b s", b=2),
                                         ACT.Identity, bias=k.bq0_scaled[:, :], scale=DH0 ** -0.5).then_inc(q_kept, 1)
                at = pair(i, s, "output")
                if at:
                    j, p = at
                    act.wait_ge(oT_ready, this(j, p + 1, PER))
                    act.wait_ge(y_ready, last(j, p + 1, PER))
                    nc.scalar.activation(oT[:, p, :], psum[:, 7, 0:128], ACT.Identity, bias=k.bv0[:, :])\
                        .then_inc(oT_kept, 1)
                at = pair(i, s, "scores")
                if at:
                    j, p = at
                    act.wait_ge(v_ready, last(j, p + 1, PER))
                    nc.scalar.activation(xdup[:, p, :, :, :], k.x_feat[:, bass.ds(2 * (j * PER + p), 2), :]
                                         .unsqueeze(2).to_broadcast([128, 2, 2, S]), ACT.Copy).then_inc(xdup_ready, 1)
                at = pair(i, s, "transpose")
                if at:
                    j, p = at
                    act.wait_ge(prT_ready, this(j, p + 1, PER))
                    act.wait_ge(o_ready, last(j, p + 1, PER))
                    nc.scalar.activation(prT[:, p, :, :].rearrange("p (a h) s -> p a (h s)", a=2),
                                         psum[0:2 * S, 4:6, :], ACT.Copy).then_inc(prT_kept, 1)
                at = pair(i, s, "norm")
                if at:
                    t.scalar_store(act, *at, psum[:, 7, 256:384])
                at = pair(i, s, "scores")
                if at:
                    j, p = at
                    act.wait_ge(shifted, this(j, p + 1, PER))
                    act.wait_ge(prT_ready, last(j, p + 1, PER))
                    act.wait_ge(sum_ready, last(j, p + 1, PER))
                    nc.scalar.activation(pr[:, p, :, :], sm[:, p, :, :], ACT.Exp).then_inc(exp_ready, 1)

            steps.run(act, step)


def context_attention_phase(k):
    nc = k.nc
    Q4 = C // 4
    steps = PairSteps(project=0, scores=1, transpose=2, values=3, output=4, norm=5)
    PER, pair, n = steps.PER, steps.pair, steps.count
    with ExitStack() as ctx:
        t = Tail(k, ctx, "ca", router=k.router0, per=PER)
        sem = lambda name: k.sem(ctx, "ca_" + name)
        qp = k.sb(ctx, "ca_qp", [128, 2, S])
        qk = k.sb(ctx, "ca_qk", [128, 2, 2, SP])
        ctxT, ctxN, ctxT_loaded, ctxN_loaded = k.ctxT, k.ctxN, k.ctxT_loaded, k.ctxN_loaded
        pr = k.sb(ctx, "ca_pr", [128, 2, C])
        prT = k.sb(ctx, "ca_prT", [KP, 2, KT, 128])
        negmax = k.sb(ctx, "ca_negmax", [128, 2, 1])
        rs = k.sb(ctx, "ca_rs", [128, 2, 1])
        rinv = k.sb(ctx, "ca_rinv", [128, 2, 1])
        xb = k.sb(ctx, "ca_xb", [128, 2, D])
        o_tok = k.sb(ctx, "ca_o_tok", [128, 2, 128])
        oT = k.sb(ctx, "ca_oT", [128, 2, 128])
        psum = ctx.enter_context(nc.psum_tensor("ca_psum", [128, 8, 512], fp32))
        qk_zeroed, qp_ready, qp_kept, qk_ready, qk_kept = sem("qk_zeroed"), sem("qp_ready"), sem("qp_kept"), sem("qk_ready"), sem("qk_kept")
        scores_ready, max_ready, exp_ready, rinv_ready = sem("scores_ready"), sem("max_ready"), sem("exp_ready"), sem("rinv_ready")
        prT_ready, even_kept, odd_kept = sem("prT_ready"), sem("even_kept"), sem("odd_kept")
        pv_ready, o_kept, oT_ready, oT_kept, y_ready, xb_ready = (
            sem("pv_ready"), sem("o_kept"), sem("oT_ready"), sem("oT_kept"), sem("y_ready"), sem("xb_ready"))
        k.used += k.context_semaphores
        block = ctx.enter_context(nc.Block())

        @block.sync
        def _(sp):
            def load_T(i, p):
                sp.wait_ge(scores_ready, last(i, p + 1, PER))
                sp.dma_start(ctxT[:, p, :, :],
                             k.dram["ctxT"][bass.ds(4 * i + 2 * p, 2), :, :].rearrange("b d c -> d b c"))\
                    .then_inc(ctxT_loaded[p], 16)

            def load_N(i, p):
                sp.wait_ge(pv_ready, last(i, p + 1, PER))
                sp.dma_start(ctxN[:, p, :, :],
                             k.dram["ctxN"][bass.ds(4 * i + 2 * p, 2), :, :, :].rearrange("b q t d -> q b (t d)"))\
                    .then_inc(ctxN_loaded[p], 16)

            for p in range(PER):
                load_T(1, p)
            with sp.Fori(1, PAIRS // PER - 1) as i:
                for p in range(PER):
                    load_T(i + 1, p)
                    load_N(i, p)
            for p in range(PER):
                load_N(PAIRS // PER - 1, p)

        @block.gpsimd
        def _(pool):
            open_sems(pool, PER, xb_ready)
            t.open_pool(pool)

            def step(i, s):
                at = pair(i, s, "norm")
                if at:
                    t.pool_store(pool, *at)
                at = pair(i, s, "values")
                if at:
                    j, p = at
                    pool.wait_ge(t.r_ready, last(j, p + 1, PER))
                    pool.tensor_tensor(xb[:, p:p + 1, :], k.x_tok[:, bass.ds(j * PER + p, 1), :],
                                       k.cross_row[:, :].unsqueeze(1), ALU.add).then_inc(xb_ready, 1)
                at = pair(i, s, "output")
                if at:
                    t.pool_rstd(pool, *at)

            steps.run(pool, step)

        @block.tensor
        def _(pe):
            open_sems(pe, PER, qp_ready, qk_ready, scores_ready, pv_ready, oT_ready, y_ready)
            open_sems(pe, 3 * PER, prT_ready)
            t.open_tensor(pe)
            pe.wait_ge(qk_zeroed, 1)

            def transposes(j, p, r):
                for c in range(4):
                    kt = 4 * r + c
                    done = nc.tensor.transpose(psum[0:KP, 4 + r % 2, c * 128:(c + 1) * 128],
                                               pr[:, p, kt * KP:(kt + 1) * KP], k.ident[:, :])
                done.then_inc(prT_ready, 1)

            def values(p, half):
                for kt in range(KT):
                    done = nc.tensor.matmul(psum[half * SP:(half + 1) * SP, 6, 0:D], prT[:, p, kt, half * SP:(half + 1) * SP],
                                            ctxN[:, p, half, kt * D:(kt + 1) * D], start=(kt == 0), stop=(kt == KT - 1))
                return done

            def step(i, s):
                at = pair(i, s, "project")
                if at:
                    j, p = at
                    pe.wait_ge(qk_kept, n(i, s, 1))
                    pe.wait_ge(t.r_ready, n(i, s, 5))
                    pe.wait_ge(t.logits_kept, n(i, s, 6))
                    nc.tensor.matmul(psum[:, 7, 0:2 * S], k.wqT0x[:, :], k.x_feat[:, bass.ds(2 * (j * PER + p), 2), :],
                                     start=True, stop=True).then_inc(qp_ready, 1)
                at = pair(i, s, "scores")
                if at:
                    j, p = at
                    pe.wait_ge(qk_kept, this(j, p + 1, PER))
                    pe.wait_ge(ctxT_loaded[p], (j + 1) * 16)
                    pe.wait_ge(exp_ready, this(j, p, PER))
                    for half in range(2):
                        for c in range(4):
                            done = nc.tensor.matmul(psum[half * SP:(half + 1) * SP, c, 0:Q4], qk[:, p, half, :],
                                                    ctxT[:, p, half, c * Q4:(c + 1) * Q4], start=True, stop=True)
                    done.then_inc(scores_ready, 1)
                at = pair(i, s, "output")
                if at:
                    j, p = at
                    pe.wait_ge(o_kept, this(j, p + 1, PER))
                    pe.wait_ge(qp_kept, n(i, s, 0))
                    pe.wait_ge(t.logits_kept, n(i, s, 6))
                    nc.tensor.transpose(psum[:, 7, 0:128], o_tok[:, p, :], k.ident[:, :])\
                        .then_inc(oT_ready, 1)
                at = pair(i, s, "transpose")
                if at:
                    j, p = at
                    pe.wait_ge(exp_ready, this(j, p + 1, PER))
                    pe.wait_ge(even_kept, this(j, 2 * p, 2 * PER))
                    transposes(j, p, 0)
                    pe.wait_ge(odd_kept, this(j, p, PER))
                    transposes(j, p, 1)
                at = pair(i, s, "norm")
                if at:
                    pe.wait_ge(qp_kept, n(i, s, 0))
                    pe.wait_ge(oT_kept, n(i, s, 4))
                    t.tensor_transpose(pe, *at, psum[:, 7, 256:384])
                at = pair(i, s, "values")
                if at:
                    j, p = at
                    pe.wait_ge(ctxN_loaded[p], (j + 1) * 16)
                    pe.wait_ge(even_kept, this(j, 2 * p + 2, 2 * PER))
                    pe.wait_ge(odd_kept, this(j, p + 1, PER))
                    pe.wait_ge(o_kept, this(j, p, PER))
                    values(p, 0)
                at = pair(i, s, "project")
                if at:
                    j, p = at
                    pe.wait_ge(qp_kept, this(j, p + 1, PER))
                    pe.wait_ge(oT_kept, n(i, s, 4))
                    pe.wait_ge(t.feat_stored, n(i, s, 5))
                    nc.tensor.matmul(psum[:, 7, 0:2 * S], k.wk0x[:, :], qp[:, :, :], start=True, stop=True)\
                        .then_inc(qk_ready, 1)
                at = pair(i, s, "values")
                if at:
                    values(at[1], 1).then_inc(pv_ready, 1)
                at = pair(i, s, "output")
                if at:
                    j, p = at
                    pe.wait_ge(oT_kept, this(j, p + 1, PER))
                    pe.wait_ge(qk_kept, n(i, s, 0))
                    pe.wait_ge(t.feat_stored, n(i, s, 5))
                    nc.tensor.matmul(psum[:, 7, 128:256], oT[:, p, :], k.value_out0[:, :], start=True, stop=True)\
                        .then_inc(y_ready, 1)
                at = pair(i, s, "transpose")
                if at:
                    j, p = at
                    pe.wait_ge(even_kept, this(j, 2 * p + 1, 2 * PER))
                    transposes(j, p, 2)
                at = pair(i, s, "norm")
                if at:
                    pe.wait_ge(t.feat_stored, n(i, s, 5))
                    pe.wait_ge(t.r_ready, n(i, s, 4))
                    pe.wait_ge(qk_kept, n(i, s, 0))
                    t.tensor_logits(pe, *at, psum[:, 7, 384:384 + E])

            steps.run(pe, step)

        @block.vector
        def _(dve):
            open_sems(dve, PER, max_ready, rinv_ready, qp_kept)
            open_sems(dve, 2 * PER, even_kept)
            t.open_vector(dve)
            dve.memset(qk[:, :, :, :], 0.0).then_inc(qk_zeroed, 1)

            def step(i, s):
                at = pair(i, s, "norm")
                if at:
                    t.vector_normalise(dve, *at)
                at = pair(i, s, "project")
                if at:
                    j, p = at
                    dve.wait_ge(qp_ready, this(j, p + 1, PER))
                    dve.wait_ge(qk_ready, this(j, p, PER))
                    nc.vector.tensor_scalar(qp[:, :, :].rearrange("p b s -> p (b s)"), psum[:, 7, 0:2 * S], k.bq0x[:, :],
                                            D ** -0.5, ALU.add, ALU.mult).then_inc(qp_kept, 1)
                at = pair(i, s, "scores")
                if at:
                    j, p = at
                    dve.wait_ge(scores_ready, this(j, p + 1, PER))
                    nc.vector.tensor_reduce(negmax[:, p, :], psum[:, 0:4, 0:Q4], AX.XY, ALU.max, negate=True)\
                        .then_inc(max_ready, 1)
                at = pair(i, s, "transpose")
                if at:
                    j, p = at
                    dve.wait_ge(prT_ready, this(j, 3 * p + 1, 3 * PER))
                    dve.wait_ge(pv_ready, last(j, p + 1, PER))
                    nc.vector.tensor_copy(prT[:, p, 0:4, :].rearrange("p a b -> p (a b)"), psum[0:KP, 4, :])\
                        .then_inc(even_kept, 1)
                at = pair(i, s, "output")
                if at:
                    j, p = at
                    dve.wait_ge(y_ready, this(j, p + 1, PER))
                    dve.wait_ge(xb_ready, this(j, p + 1, PER))
                    nc.vector.scalar_tensor_tensor(t.r[:, p, :], psum[:, 7, 128:256], rinv[:, p, :], xb[:, p, :],
                                                   ALU.mult, ALU.add).then_inc(t.r_ready, 1)
                    t.vector_moments(dve, j, p)
                at = pair(i, s, "transpose")
                if at:
                    j, p = at
                    dve.wait_ge(t.r_ready, last(j, p + 1, PER))
                    dve.wait_ge(exp_ready, this(j, p + 1, PER))
                    nc.vector.reciprocal(rinv[:, p, :], rs[:, p, :]).then_inc(rinv_ready, 1)
                at = pair(i, s, "norm")
                if at:
                    t.vector_logits(dve, *at, psum[:, 7, 384:384 + E])
                at = pair(i, s, "transpose")
                if at:
                    j, p = at
                    dve.wait_ge(prT_ready, this(j, 3 * p + 3, 3 * PER))
                    nc.vector.tensor_copy(prT[:, p, 8:12, :].rearrange("p a b -> p (a b)"), psum[0:KP, 4, :])\
                        .then_inc(even_kept, 1)
            steps.run(dve, step)

        @block.scalar
        def _(act):
            open_sems(act, PER, exp_ready, odd_kept, o_kept, qk_kept, oT_kept)
            t.open_scalar(act)
            act.wait_ge(qk_zeroed, 1)

            def step(i, s):
                at = pair(i, s, "output")
                if at:
                    j, p = at
                    act.wait_ge(oT_ready, this(j, p + 1, PER))
                    act.wait_ge(y_ready, last(j, p + 1, PER))
                    nc.scalar.activation(oT[:, p, :], psum[:, 7, 0:128], ACT.Copy).then_inc(oT_kept, 1)
                at = pair(i, s, "transpose")
                if at:
                    j, p = at
                    act.wait_ge(prT_ready, this(j, 3 * p + 2, 3 * PER))
                    act.wait_ge(pv_ready, last(j, p + 1, PER))
                    nc.scalar.activation(prT[:, p, 4:8, :].rearrange("p a b -> p (a b)"), psum[0:KP, 5, :],
                                         ACT.Copy).then_inc(odd_kept, 1)
                at = pair(i, s, "norm")
                if at:
                    t.scalar_store(act, *at, psum[:, 7, 256:384])
                at = pair(i, s, "scores")
                if at:
                    j, p = at
                    act.wait_ge(max_ready, this(j, p + 1, PER))
                    act.wait_ge(prT_ready, last(j, 3 * p + 3, 3 * PER))
                    act.wait_ge(rinv_ready, last(j, p + 1, PER))
                    nc.scalar.activation(pr[:, p, :].rearrange("p (a c) -> p a c", a=4), psum[:, 0:4, 0:Q4],
                                         ACT.Exp, bias=negmax[:, p, :], accum_out=rs[:, p, :]).then_inc(exp_ready, 1)
                at = pair(i, s, "project")
                if at:
                    j, p = at
                    act.wait_ge(qk_ready, this(j, p + 1, PER))
                    act.wait_ge(scores_ready, last(j, p + 1, PER))
                    nc.scalar.activation(qk[:, p, :, 0:S], psum[:, 7, 0:2 * S].rearrange("p (b s) -> p b s", b=2),
                                         ACT.Copy).then_inc(qk_kept, 1)
                at = pair(i, s, "values")
                if at:
                    j, p = at
                    act.wait_ge(pv_ready, this(j, p + 1, PER))
                    act.wait_ge(oT_ready, last(j, p + 1, PER))
                    nc.scalar.activation(o_tok[:, p, :], psum[:, 6, 0:128], ACT.Copy).then_inc(o_kept, 1)

            steps.run(act, step)


def routing_phase(k, layer):
    nc = k.nc
    with ExitStack() as ctx:
        sem = lambda name: k.sem(ctx, f"route{layer}_{name}")
        sb = lambda name, shape, dt=fp32: k.sb(ctx, f"route{layer}_{name}", shape, dt)
        best = sb("best", [128, PAIRS, 8])
        index_u = sb("index_u", [128, PAIRS, 8], u32)
        index = sb("index", [128, PAIRS, 2])
        gap, e2, total, inv, w2 = (sb(x, [128, PAIRS, 1]) for x in ("gap", "e2", "total", "inv", "w2"))
        hot = sb("hot", [128, PAIRS, E])
        first = sb("first", [128, PAIRS, E])
        biased = sb("biased", [128, PAIRS, E])
        step_done, exp_ready, biased_ready, gap_ready = sem("step_done"), sem("exp_ready"), sem("biased_ready"), sem("gap_ready")
        fold_loaded = [sem("query_key_loaded"), sem("value_out_loaded")]
        fold_ready, fold_kept = sem("fold_ready"), sem("fold_kept")
        psum = ctx.enter_context(nc.psum_tensor(f"route{layer}_psum", [128, 8, 512], fp32))
        high_kept, low_kept, dve_low_kept = {name: sem(name + "_high_kept") for name in k.parts}, sem("low_kept"), sem("dve_low_kept")
        block = ctx.enter_context(nc.Block())
        FOLDS = 2 * H1 // 4 if layer == 0 else 0
        if layer == 0:
            wqT1, wkT1, wvT1, wo1 = (sb(x, [2 * DH1, H1 // 2, D]) for x in ("wqT1", "wkT1", "wvT1", "wo1"))
            fold_loads = ("L1_wqT", wqT1), ("L1_wkT", wkT1), ("L1_wvT", wvT1), ("L1_wo", wo1)
        NE = E if layer == 0 else E + 1
        POOL_PARTS = ("up",) if layer == 0 else ("gate",)
        if layer == 1:
            loaded = {name: sem(name + "_loaded") for name in k.expert_loads}

        def split_ready(engine, name):
            if layer == 1:
                engine.wait_ge(loaded[name], 16 * len(k.expert_loads[name]))

        flat = lambda v: v.rearrange("p a b -> p (a b)") if len(v.shape) == 3 else v

        @block.sync
        def _(sp):
            if layer == 0:
                for x, (name, dst) in enumerate(fold_loads):
                    sp.dma_start(dst[:, :, :], k.dram[name]).then_inc(fold_loaded[x // 2], 16)
                return
            for name, loads in k.expert_loads.items():
                for array, dst in loads:
                    sp.dma_start(dst, k.dram[array]).then_inc(loaded[name], 16)

        wide = lambda v: v.to_broadcast([128, PAIRS, E])
        experts = k.expert_index[:, :].unsqueeze(1).to_broadcast([128, PAIRS, E])

        @block.gpsimd
        def _(pool):
            n = 0
            for name, (source, high, low) in k.parts.items():
                if name not in POOL_PARTS:
                    continue
                split_ready(pool, name)
                for e in range(NE):
                    n += 1
                    pool.wait_ge(high_kept[name], e + 1)
                    pool.tensor_tensor(flat(low[:, e]), flat(source[:, e]), flat(high[:, e]).bitcast(fp32), ALU.subtract)\
                        .then_inc(low_kept, 1)
            pool.wait_ge(low_kept, n)

        @block.vector
        def _(dve):
            n = 0

            def step(instruction):
                nonlocal n
                n += 1
                instruction.then_inc(step_done, 1)
                dve.wait_ge(step_done, n)

            values = k.logits
            if layer == 1:
                nc.vector.tensor_tensor(biased[:, :, :], k.logits[:, :, :],
                                        k.router_bias_row1[:, :].unsqueeze(1).to_broadcast([128, PAIRS, E]),
                                        ALU.add).then_inc(biased_ready, 1)
                dve.wait_ge(exp_ready, 1)
                values = first
            for g in range(PAIRS):
                last_max = nc.vector.max(best[:, g, :], values[:, g, :])
            step(last_max)
            for g in range(PAIRS):
                last_index = nc.vector.max_index(index_u[:, g, :], best[:, g, :], values[:, g, :])
            step(last_index)
            step(nc.vector.tensor_copy(index[:, :, :], index_u[:, :, 0:2]))
            if layer == 0:
                nc.vector.tensor_tensor(gap[:, :, :], best[:, :, 1:2], best[:, :, 0:1], ALU.subtract).then_inc(gap_ready, 1)
                dve.wait_ge(exp_ready, 1)
                step(nc.vector.tensor_scalar(total[:, :, :], e2[:, :, :], 1.0, None, ALU.add))
                step(nc.vector.reciprocal(inv[:, :, :], total[:, :, :]))
                w1 = inv
                step(nc.vector.tensor_tensor(w2[:, :, :], e2[:, :, :], inv[:, :, :], ALU.mult))
            else:
                step(nc.vector.tensor_tensor(total[:, :, :], best[:, :, 1:2], best[:, :, 0:1], ALU.add))
                step(nc.vector.reciprocal(inv[:, :, :], total[:, :, :]))
                w1 = gap
                step(nc.vector.tensor_tensor(gap[:, :, :], best[:, :, 0:1], inv[:, :, :], ALU.mult))
                step(nc.vector.tensor_tensor(w2[:, :, :], best[:, :, 1:2], inv[:, :, :], ALU.mult))
            step(nc.vector.tensor_tensor(hot[:, :, :], experts, wide(index[:, :, 0:1]), ALU.is_equal))
            step(nc.vector.tensor_tensor(biased[:, :, :], hot[:, :, :], wide(w1[:, :, :]), ALU.mult))
            step(nc.vector.tensor_tensor(hot[:, :, :], experts, wide(index[:, :, 1:2]), ALU.is_equal))
            step(nc.vector.tensor_tensor(first[:, :, :], hot[:, :, :], wide(w2[:, :, :]), ALU.mult))
            step(nc.vector.tensor_tensor(k.expert_weights[:, :, :], biased[:, :, :], first[:, :, :], ALU.add))
            for name, (source, high, low) in k.parts.items():
                if name in POOL_PARTS:
                    continue
                split_ready(dve, name)
                for e in range(NE):
                    dve.wait_ge(high_kept[name], e + 1)
                    nc.vector.tensor_tensor(flat(low[:, e]), flat(source[:, e]), flat(high[:, e]).bitcast(fp32), ALU.subtract)\
                        .then_inc(dve_low_kept, 1)

        @block.tensor
        def _(pe):
            for g in range(FOLDS):
                if g % (FOLDS // 2) == 0:
                    pe.wait_ge(fold_loaded[g // (FOLDS // 2)], 2 * 16)
                a, b = (wqT1, wkT1) if g < FOLDS // 2 else (wvT1, wo1)
                for j in range(4):
                    h = 4 * (g % (FOLDS // 2)) + j
                    rows, h = slice(h // 8 * DH1, (h // 8 + 1) * DH1), h % 8
                    done = nc.tensor.matmul(psum[:, g, j * D:(j + 1) * D], a[rows, h, :], b[rows, h, :], start=True, stop=True)
                done.then_inc(fold_ready, 1)

        @block.scalar
        def _(act):
            if layer == 1:
                act.wait_ge(biased_ready, 1)
                nc.scalar.activation(first[:, :, :], biased[:, :, :], ACT.Sigmoid).then_inc(exp_ready, 1)
            else:
                act.wait_ge(gap_ready, 1)
                nc.scalar.activation(e2[:, :, :], gap[:, :, :], ACT.Exp).then_inc(exp_ready, 1)
            for name, (source, high, low) in k.parts.items():
                split_ready(act, name)
                for e in range(NE):
                    nc.scalar.activation(high[:, e], source[:, e], ACT.Copy).then_inc(high_kept[name], 1)
            for g in range(FOLDS):
                dst = k.key_query if g < FOLDS // 2 else k.value_out
                h = 4 * (g % (FOLDS // 2))
                act.wait_ge(fold_ready, g + 1)
                nc.scalar.activation(dst[:, h:h + 4, :], psum[:, g, :].rearrange("p (h n) -> p h n", h=4), ACT.Copy)\
                    .then_inc(fold_kept, 1)


def expert_phase(k, layer):
    nc = k.nc
    HT = (U0 if layer == 0 else I1) // 128
    NE = E if layer == 0 else E + 1
    part_of = lambda name, e, cols: [v[:, e, cols] for v in k.parts[name][1:]]
    with ExitStack() as ctx:
        tag = f"moe{layer}"
        inner = (k.ln_g1[:, :], k.ln_b1[:, :]) if layer == 0 else None
        final = layer == 1
        t = Tail(k, ctx, tag, inner=inner, final=final)
        sem = lambda name: k.sem(ctx, f"{tag}_{name}")
        sb = lambda name, shape, dt=fp32: k.sb(ctx, f"{tag}_{name}", shape, dt)
        x_hi, x_lo = sb("x_hi", [128, CT], fp32r), sb("x_lo", [128, CT], fp32r)
        wc = sb("wc", [128, CK, E])
        spread = sb("spread", [128, 3, CT])
        HR = 4
        hid = sb("hid", [128, HR, CT])
        hid_hi, hid_lo = sb("hid_hi", [128, 2, HT, CT], fp32r), sb("hid_lo", [128, 2, HT, CT], fp32r)
        act_out = sb("act_out", [128, 2, CT])
        part = sb("part", [128, 2, CT])
        acc = sb("acc", [128, CB, S])
        mixed = sb("mixed", [128, CB, SP])
        psum = ctx.enter_context(nc.psum_tensor(f"{tag}_psum", [128, 8, 512], fp32))
        mixed_zeroed, x_hi_ready, x_lo_ready, wc_ready, spread_ready, spread_kept = (
            sem("mixed_zeroed"), sem("x_hi_ready"), sem("x_lo_ready"), sem("wc_ready"), sem("spread_ready"), sem("spread_kept"))
        up_ready, hid_ready, silu_ready, down_ready, part_ready, acc_ready, y_ready = (
            sem("up_ready"), sem("hid_ready"), sem("silu_ready"), sem("down_ready"), sem("part_ready"),
            sem("acc_ready"), sem("y_ready"))
        out_stored, hi_ready, lo_ready = sem("out_stored"), sem("hi_ready"), sem("lo_ready")
        block = ctx.enter_context(nc.Block())

        def run(engine, chunk, tail):
            chunk(0, lambda e, at: None, first=True)
            with engine.Fori(1, CHUNKS - 1) as i:
                chunk(i, lambda e, at: tail(i - 1, e, at))
            chunk(CHUNKS - 1, lambda e, at: tail(CHUNKS - 2, e, at), end=True)
            for e in range(1, CK + 3):
                for at in range(-1, 3):
                    tail(CHUNKS - 1, e, at, after=True)

        n = lambda i, p: this(i, p + 1, CK)
        b = lambda i, p: last(i, p + 1, CK)
        NT = NE * HT

        def slot(i, e):
            if e >= 2:
                return this(i, e - 1, NE)
            return last(i, NE if (NE - 1) % 2 == e else NE - 1, NE)

        def hid_tile(i, j, back=0):
            return this(i, j + 1 - back, NT) if j >= back else last(i, NT + j + 1 - back, NT)

        @block.gpsimd
        def _(pool):
            open_sems(pool, 1, wc_ready)
            open_sems(pool, NE - 1, acc_ready)
            t.open_pool(pool)
            pool.memset(mixed[:, :, :], 0.0).then_inc(mixed_zeroed, 1)
            pool.wait_ge(mixed_zeroed, 1)

            def chunk(i, tail, first=False, end=False):
                pool.wait_ge(spread_ready, last(i, E, E))
                pool.tensor_copy(wc[:, :, :], k.expert_weights[:, bass.ds(i * CK, CK), :]).then_inc(wc_ready, 1)
                for e in range(1, NE):
                    if e == 1:
                        tail(1, 1)
                    if e + 1 < NE:
                        tail(e + 1, 1)
                    pool.wait_ge(part_ready, this(i, e + 1, NE))
                    if e > 1:
                        pool.wait_ge(acc_ready, this(i, e - 1, NE - 1))
                    total = acc[:, :, :]
                    if e == NE - 1:
                        pool.wait_ge(y_ready, b(i, CK - 1))
                        total = mixed[:, :, 0:S]
                    pool.tensor_tensor(total, acc[:, :, :], part[:, e % 2, :].rearrange("p (b s) -> p b s", b=CB), ALU.add)\
                        .then_inc(acc_ready, 1)

            def tail(i, e, at, after=False):
                if at != 1:
                    return
                if 0 <= e - 1 < CK:
                    t.pool_rstd(pool, i, e - 1)
                if 0 <= e - 2 < CK:
                    if inner:
                        t.pool_inner_rstd(pool, i, e - 2)
                    if not final:
                        t.pool_store(pool, i, e - 2)

            run(pool, chunk, tail)

        @block.sync
        def _(sp):
            if not final:
                return
            with sp.Fori(0, CHUNKS) as i:
                sp.wait_ge(t.xn_ready, n(i, CK - 1))
                for h in range(2):
                    sp.dma_start(k.out[bass.ds(i * CB, CB), :, :].rearrange("(g h) s d -> h s g d", h=2)[h],
                                 k.x_tok[h * SP:h * SP + S, bass.ds(i * CK, CK), :]).then_inc(out_stored, 16)
            sp.wait_ge(out_stored, CHUNKS * 2 * 16)

        @block.tensor
        def _(pe):
            open_sems(pe, E, spread_ready)
            open_sems(pe, NT * (1 if layer == 0 else 2), up_ready)
            open_sems(pe, NE, down_ready)
            open_sems(pe, CK, y_ready)
            t.open_tensor(pe)

            def split_product(out, w, x, start, stop):
                (w_hi, w_lo), (m_hi, m_lo) = w, x
                nc.tensor.matmul(out, w_hi, m_hi, start=start, stop=False)
                nc.tensor.matmul(out, w_hi, m_lo, start=False, stop=False)
                return nc.tensor.matmul(out, w_lo, m_hi, start=False, stop=stop)

            def chunk(i, tail, first=False, end=False):
                x = (x_hi[:, :], x_lo[:, :])

                def spread_weights(e):
                    if e >= 2:
                        pe.wait_ge(spread_kept, this(i, e - 1, E))
                    if not first:
                        if 0 <= e - 3 < CK:
                            pe.wait_ge(t.r_ready, last(i, e - 2, CK))
                    for p in range(CK):
                        done = nc.tensor.transpose(psum[:, 6 + e % 2, p * 128:(p + 1) * 128],
                                                   wc[:, p, e:e + 1].to_broadcast([128, 128]), k.ident[:, :])
                    done.then_inc(spread_ready, 1)

                def hidden(e):
                    for j in range(HT):
                        u = e * HT + j
                        if layer == 0:
                            pe.wait_ge(hi_ready, hid_tile(i, u, 4))
                            split_product(psum[:, u % 4, 0:CT], part_of("up", e, slice(j * 128, (j + 1) * 128)), x,
                                          True, True).then_inc(up_ready, 1)
                        else:
                            pe.wait_ge(hid_ready, hid_tile(i, u, 2))
                            for c, w in enumerate(("gate", "up")):
                                split_product(psum[:, 2 * c + u % 2, 0:CT], part_of(w, e, slice(j * 128, (j + 1) * 128)), x,
                                              True, True).then_inc(up_ready, 1)

                def project(e):
                    pe.wait_ge(part_ready, slot(i, e))
                    if not first and not final and 0 <= e - 3:
                        pe.wait_ge(t.feat_stored, last(i, min(e - 2, CK), CK))
                    for j in range(HT):
                        pe.wait_ge(lo_ready, this(i, e * HT + j + 1, NT))
                        done = split_product(psum[:, 4 + e % 2, 0:CT], part_of("down", e, j),
                                             (hid_hi[:, e % 2, j, :], hid_lo[:, e % 2, j, :]), j == 0, j == HT - 1)
                    done.then_inc(down_ready, 1)

                pe.wait_ge(x_lo_ready, this(i))
                hidden(0)
                pe.wait_ge(wc_ready, this(i))
                pe.wait_ge(spread_kept, last(i, E, E))
                if not first:
                    pe.wait_ge(t.r_ready, last(i, 0, CK))
                spread_weights(0)
                spread_weights(1)
                for e in range(1, NE):
                    hidden(e)
                    if e + 1 < E:
                        spread_weights(e + 1)
                    tail(e, 0)
                    project(e - 1)
                    tail(e, 2)
                project(NE - 1)

            def tail(i, e, at, after=False):
                if at == 0 and 0 <= e - 1 < CK:
                    if e == 1:
                        pe.wait_ge(acc_ready, this(i, NE - 1, NE - 1))
                    if after:
                        pe.wait_ge(spread_kept, this(i, E, E))
                        if e >= 3:
                            pe.wait_ge(t.r_ready, this(i, e - 2, CK))
                    else:
                        pe.wait_ge(spread_kept, this(i + 1, e + 1, E))
                    nc.tensor.transpose(psum[:, 6 + e % 2, 0:128], mixed[:, 2 * (e - 1):2 * e, :], k.ident[:, :])\
                        .then_inc(y_ready, 1)
                if at == 2 and 0 <= e - 3 < CK and not final:
                    if after:
                        pe.wait_ge(part_ready, this(i, NE, NE))
                        if e >= 5:
                            pe.wait_ge(t.feat_stored, this(i, e - 4, CK))
                    else:
                        pe.wait_ge(part_ready, this(i + 1, e - 1, NE))
                    t.tensor_transpose(pe, i, e - 3, psum[:, 4 + e % 2, 128:256])

            run(pe, chunk, tail)

        @block.vector
        def _(dve):
            open_sems(dve, NE, part_ready)
            open_sems(dve, E, spread_kept)
            open_sems(dve, 1, x_lo_ready)
            open_sems(dve, NT, lo_ready)
            if layer == 1:
                open_sems(dve, NT, hid_ready)
            t.open_vector(dve)

            def x_low(i):
                dve.wait_ge(x_hi_ready, this(i))
                nc.vector.tensor_tensor(x_lo[:, :].rearrange("p (b s) -> p b s", b=CB), k.x_feat[:, bass.ds(i * CB, CB), :],
                                        x_hi[:, :].bitcast(fp32).rearrange("p (b s) -> p b s", b=CB), ALU.subtract)\
                    .then_inc(x_lo_ready, 1)

            def low(i, u):
                dve.wait_ge(hi_ready, this(i, u + 1, NT))
                e, j = u // HT, u % HT
                if j == 0:
                    dve.wait_ge(down_ready, slot(i, e))
                nc.vector.tensor_tensor(hid_lo[:, e % 2, j, :], hid[:, u % HR, :], hid_hi[:, e % 2, j, :].bitcast(fp32),
                                        ALU.subtract).then_inc(lo_ready, 1)

            x_low(0)

            def chunk(i, tail, first=False, end=False):
                def keep_spread(e):
                    dve.wait_ge(spread_ready, this(i, e + 1, E))
                    dve.wait_ge(part_ready, this(i, e - 2, NE) if e >= 3 else last(i, E, NE))
                    nc.vector.tensor_copy(spread[:, e % 3, :].rearrange("p (b s) -> p b s", b=CB),
                                          psum[:, 6 + e % 2, :].rearrange("p (b s) -> p b s", b=CB)[:, :, 0:S])\
                        .then_inc(spread_kept, 1)

                def hidden(e):
                    for j in range(HT):
                        u = e * HT + j
                        if layer == 0:
                            low(i, u)
                            continue
                        dve.wait_ge(silu_ready, this(i, u + 1, NT))
                        dve.wait_ge(up_ready, this(i, 2 * u + 2, 2 * NT))
                        dve.wait_ge(hi_ready, hid_tile(i, u, HR))
                        dve.wait_ge(lo_ready, hid_tile(i, u, HR))
                        nc.vector.tensor_tensor(hid[:, u % HR, :], act_out[:, u % 2, :], psum[:, 2 + u % 2, 0:CT],
                                                ALU.mult).then_inc(hid_ready, 1)
                        if j:
                            low(i, u - 1)
                    if layer == 1:
                        low(i, e * HT + HT - 1)

                def weigh(e):
                    dve.wait_ge(down_ready, this(i, e + 1, NE))
                    src = psum[:, 4 + e % 2, 0:CT]
                    if e == 0:
                        dve.wait_ge(acc_ready, last(i, NE - 1, NE - 1))
                        dve.wait_ge(spread_kept, this(i, 1, E))
                        split = lambda v: v.rearrange("p (b s) -> p b s", b=CB)
                        if layer == 0:
                            nc.vector.scalar_tensor_tensor(acc[:, :, :], split(src), k.down_bias0[:, 0:1],
                                                           split(spread[:, 0, :]), ALU.add, ALU.mult)\
                                .then_inc(part_ready, 1)
                        else:
                            nc.vector.tensor_tensor(acc[:, :, :], split(src), split(spread[:, 0, :]), ALU.mult)\
                                .then_inc(part_ready, 1)
                        return
                    dve.wait_ge(acc_ready, this(i, e - 2, NE - 1) if e > 2 else last(i, NE - 1, NE - 1))
                    if layer == 0:
                        dve.wait_ge(spread_kept, this(i, e + 1, E))
                        nc.vector.scalar_tensor_tensor(part[:, e % 2, :], src, k.down_bias0[:, e:e + 1],
                                                       spread[:, e % 3, :], ALU.add, ALU.mult).then_inc(part_ready, 1)
                    elif e < E:
                        dve.wait_ge(spread_kept, this(i, e + 1, E))
                        nc.vector.tensor_tensor(part[:, e % 2, :], src, spread[:, e % 3, :], ALU.mult).then_inc(part_ready, 1)
                    else:
                        nc.vector.tensor_copy(part[:, e % 2, :], src).then_inc(part_ready, 1)

                hidden(0)
                keep_spread(0)
                keep_spread(1)
                for e in range(1, NE):
                    if layer == 0:
                        tail(e, -1)
                    hidden(e)
                    if layer == 1:
                        tail(e, -1)
                    if e + 1 < E:
                        keep_spread(e + 1)
                    tail(e, 1)
                    weigh(e - 1)
                if not end:
                    x_low(i + 1)
                weigh(NE - 1)

            def tail(i, e, at, after=False):
                p = e - 1
                if at == 1 and 0 <= p < CK:
                    dve.wait_ge(y_ready, n(i, p))
                    nc.vector.tensor_tensor(t.r[:, p:p + 1, :], psum[:, 6 + e % 2, 0:128].unsqueeze(1),
                                            k.x_tok[:, bass.ds(i * CK + p, 1), :], ALU.add).then_inc(t.r_ready, 1)
                    t.vector_moments(dve, i, p)
                if at != -1:
                    return
                p = e - 2
                if 0 <= p < CK:
                    t.vector_normalise(dve, i, p)
                    if inner:
                        t.vector_inner_moments(dve, i, p)
                p = e - 3
                if inner and 0 <= p < CK:
                    t.vector_inner_normalise(dve, i, p)

            run(dve, chunk, tail)

        @block.scalar
        def _(act):
            open_sems(act, NT, hi_ready)
            open_sems(act, 1, x_hi_ready)
            if layer == 1:
                open_sems(act, NT, silu_ready)
            t.open_scalar(act)

            def x_high(i):
                act.wait_ge(up_ready, last(i, NT, NT) if layer == 0 else last(i, 2 * NT, 2 * NT))
                nc.scalar.activation(x_hi[:, :].rearrange("p (b s) -> p b s", b=CB), k.x_feat[:, bass.ds(i * CB, CB), :],
                                     ACT.Copy).then_inc(x_hi_ready, 1)

            x_high(0)

            def chunk(i, tail, first=False, end=False):
                def high(u):
                    e, j = u // HT, u % HT
                    act.wait_ge(hid_ready, this(i, u + 1, NT))
                    if j == 0:
                        act.wait_ge(down_ready, slot(i, e))
                    nc.scalar.activation(hid_hi[:, e % 2, j, :], hid[:, u % HR, :], ACT.Copy).then_inc(hi_ready, 1)

                for e in range(NE):
                    for j in range(HT):
                        u = e * HT + j
                        if layer == 0:
                            act.wait_ge(up_ready, this(i, u + 1, NT))
                            act.wait_ge(lo_ready, hid_tile(i, u, HR))
                            gelu = dict(func=ACT.Gelu, bias=k.up_bias0[:, e, j:j + 1])
                            nc.scalar.activation(hid[:, u % HR, :], psum[:, u % 4, 0:CT], **gelu)
                            if j == 0:
                                act.wait_ge(down_ready, slot(i, e))
                            nc.scalar.activation(hid_hi[:, e % 2, j, :], psum[:, u % 4, 0:CT], **gelu).then_inc(hi_ready, 1)
                            if j == 1:
                                tail(e - 1, 2)
                        else:
                            act.wait_ge(up_ready, this(i, 2 * u + 1, 2 * NT))
                            act.wait_ge(hid_ready, hid_tile(i, u, 2))
                            nc.scalar.activation(act_out[:, u % 2, :], psum[:, u % 2, 0:CT], ACT.Silu)\
                                .then_inc(silu_ready, 1)
                            if j:
                                high(u - 1)
                    if layer == 1:
                        high(e * HT + HT - 1)
                    if e == NE - 1 and not end:
                        x_high(i + 1)

            def tail(i, e, at, after=False):
                if at == 2 and 0 <= e - 3 < CK and not final:
                    t.scalar_store(act, i, e - 3, psum[:, 4 + e % 2, 128:256])

            run(act, chunk, tail)


def expert_phase0(k):
    routing_phase(k, 0)
    k.clear_semaphores()
    expert_phase(k, 0)


def expert_phase1(k):
    routing_phase(k, 1)
    k.clear_semaphores()
    expert_phase(k, 1)


def state_space_phase(k):
    nc = k.nc
    N1 = 32
    with ExitStack() as ctx:
        sem = lambda name: k.sem(ctx, "ss_" + name)
        sb = lambda name, shape: k.sb(ctx, "ss_" + name, shape)
        hp = sb("hp", [128, CB, S + 2])
        tap0, tap1, mixed = sb("tap0", [128, CT]), sb("tap1", [128, CT]), sb("mixed", [128, CT])
        u, g = sb("u", [128, CT]), sb("g", [128, CT])
        xs, decay, sel = sb("xs", [N1, CT]), sb("decay", [N1, CT]), sb("sel", [N1, CT])
        keep, drive, states, chosen = sb("keep", [N1, CT]), sb("drive", [N1, CT]), sb("states", [N1, CT]), sb("chosen", [N1, CT])
        diff, gdiff = sb("diff", [128, CT]), sb("gdiff", [128, CT])
        z = sb("z", [128, CB, SP])
        xb, xb2, r = sb("xb", [128, CK, D]), sb("xb2", [128, CK, D]), sb("r", [128, CK, D])
        norms = [(sb("moments" + c, [128, CK, 6]), sb("mean_var" + c, [128, CK, 2]), sb("var_eps" + c, [128, CK, 1]),
                  sb("rstd" + c, [128, CK, 1]), sb("xn" + c, [128, CK, D])) for c in ("", "_inner")]
        psum = ctx.enter_context(nc.psum_tensor("ss_psum", [128, 8, 512], fp32))
        zeroed, h_ready, xb_ready, xb2_ready = sem("zeroed"), sem("h_ready"), sem("xb_ready"), sem("xb2_ready")
        step_done, proj_ready, act_ready = sem("step_done"), sem("proj_ready"), sem("act_ready")
        state_out_ready, out_ready, r_ready = sem("state_out_ready"), sem("out_ready"), sem("r_ready")
        moments_ready, mean_var_ready, var_eps_ready, rstd_ready, xn_ready = (
            [sem(name), sem(name + "_inner")] for name in
            ("moments_ready", "mean_var_ready", "var_eps_ready", "rstd_ready", "xn_ready"))
        xT_ready, feat_stored, tok_stored = sem("xT_ready"), sem("feat_stored"), sem("tok_stored")
        aggregating, storing = sem("aggregating"), sem("storing")
        block = ctx.enter_context(nc.Block())
        TAP0, TAP1, MIXED, ONE_MINUS, DRIVE, RESET, STATES, CHOSEN, DIFF, GDIFF, Z = range(1, 12)
        NV = Z
        DECAY, SEL, XS, U, G = range(5)
        PROJECTIONS = ((DECAY, k.wd1, decay, ACT.Sigmoid, k.bd1), (SEL, k.wsel1, sel, ACT.Sigmoid, k.bsel1),
                       (XS, k.wsin1, xs, ACT.Tanh, k.bsin1), (U, k.wi1, u, ACT.Tanh, k.bi1), (G, k.wg1, g, ACT.Sigmoid, k.bg1))
        split = lambda v: v.rearrange("p (b s) -> p b s", b=CB)

        def run(engine, chunk, tail):
            chunk(0, None)
            with engine.Fori(1, CHUNKS) as i:
                chunk(i, i - 1)
            tail(CHUNKS - 1)

        @block.gpsimd
        def _(pool):
            open_sems(pool, 1, h_ready, xb_ready, xb2_ready, tok_stored, *var_eps_ready, *rstd_ready)
            pool.memset(hp[:, :, :], 0.0).then_inc(zeroed, 1)
            pool.memset(z[:, :, :], 0.0).then_inc(zeroed, 1)
            pool.wait_ge(zeroed, 2)

            def tail(i):
                for c in range(2):
                    _, mean_var, var_eps, rstd, _ = norms[c]
                    pool.wait_ge(mean_var_ready[c], this(i, CK, CK))
                    pool.tensor_tensor(var_eps[:, :, :], mean_var[:, :, 1:2],
                                       k.eps[:, :].unsqueeze(1).to_broadcast([128, CK, 1]), ALU.add).then_inc(var_eps_ready[c], 1)
                    pool.wait_ge(var_eps_ready[c], this(i))
                    pool.wait_ge(xn_ready[c], last(i, CK, CK))
                    pool.tensor_tensor(rstd[:, :, :], var_eps[:, :, :],
                                       k.minus_half[:, :].unsqueeze(1).to_broadcast([128, CK, 1]), ALU.pow)\
                        .then_inc(rstd_ready[c], 1)
                pool.wait_ge(xn_ready[0], this(i, CK, CK))
                pool.sem_inc(storing, 1)
                pool.tensor_copy(k.x_tok[:, bass.ds(i * CK, CK), :], norms[0][4][:, :, :]).then_inc(tok_stored, 1)

            def chunk(i, previous):
                pool.wait_ge(step_done, last(i, MIXED, NV))
                pool.tensor_copy(hp[:, :, 1:S + 1], k.x_feat[:, bass.ds(i * CB, CB), :]).then_inc(h_ready, 1)
                if previous is not None:
                    tail(previous)
                x = k.x_tok[:, bass.ds(i * CK, CK), :]
                pool.tensor_tensor(xb[:, :, :], x, k.bout_row1[:, :].unsqueeze(1).to_broadcast([128, CK, D]), ALU.add)\
                    .then_inc(xb_ready, 1)
                pool.wait_ge(xb_ready, this(i))
                pool.sem_inc(storing, 1)
                pool.tensor_tensor(xb2[:, :, :], xb[:, :, :], x, ALU.add).then_inc(xb2_ready, 1)

            run(pool, chunk, tail)

        @block.tensor
        def _(pe):
            open_sems(pe, 5, proj_ready)
            open_sems(pe, 1, state_out_ready, out_ready, xT_ready)

            def outputs(i):
                pe.wait_ge(step_done, this(i, Z, NV))
                pe.wait_ge(r_ready, last(i))
                for p in range(CK):
                    done = nc.tensor.matmul(psum[:, 6, p * D:(p + 1) * D], z[:, 2 * p:2 * p + 2, :], k.wout1[:, :],
                                            start=True, stop=True)
                done.then_inc(out_ready, 1)

            def tail(i, alone=True):
                if alone:
                    outputs(i)
                pe.wait_ge(feat_stored, last(i))
                pe.wait_ge(xn_ready[1], this(i, CK, CK))
                for p in range(CK):
                    done = nc.tensor.transpose(psum[:, 7, p * 128:(p + 1) * 128], norms[1][4][:, p, :], k.ident[:, :])
                done.then_inc(xT_ready, 1)

            def chunk(i, previous):
                if previous is not None:
                    outputs(previous)
                pe.wait_ge(step_done, this(i, MIXED, NV))
                pe.wait_ge(act_ready, last(i, 5, 5))
                for bank, w, dst, _, _ in PROJECTIONS:
                    nc.tensor.matmul(psum[0:dst.shape[0], bank, 0:CT], w[:, :], mixed[:, :], start=True, stop=True)\
                        .then_inc(proj_ready, 1)
                if previous is not None:
                    tail(previous, alone=False)
                pe.wait_ge(step_done, this(i, CHOSEN, NV))
                nc.tensor.matmul(psum[:, 5, 0:CT], k.wso1[:, :], chosen[:, :], start=True, stop=True)\
                    .then_inc(state_out_ready, 1)

            run(pe, chunk, tail)

        @block.vector
        def _(dve):
            open_sems(dve, NV, step_done)
            open_sems(dve, 1, r_ready)
            open_sems(dve, CK, *moments_ready, *mean_var_ready, *xn_ready)
            dve.wait_ge(zeroed, 2)

            def measure(i, c, source):
                moments, mean_var = norms[c][0:2]
                for p in range(CK):
                    nc.vector.bn_stats(moments[:, p, :], source[:, p, :]).then_inc(moments_ready[c], 1)
                for p in range(CK):
                    dve.wait_ge(moments_ready[c], this(i, p + 1, CK))
                    dve.sem_inc(aggregating, 1)
                    nc.vector.bn_aggr(mean_var[:, p, :], moments[:, p, :]).then_inc(mean_var_ready[c], 1)

            def normalise(i, c, source):
                _, mean_var, _, rstd, xn = norms[c]
                dve.wait_ge(rstd_ready[c], this(i))
                dve.wait_ge(tok_stored if c == 0 else xT_ready, last(i))
                for p in range(CK):
                    nc.vector.tensor_scalar(xn[:, p, :], source[:, p, :], mean_var[:, p, 0:1], rstd[:, p, :],
                                            ALU.subtract, ALU.mult).then_inc(xn_ready[c], 1)

            def tail(i, between=lambda: None):
                dve.wait_ge(out_ready, this(i))
                dve.wait_ge(xb2_ready, this(i))
                nc.vector.tensor_tensor(r[:, :, :], psum[:, 6, :].rearrange("p (c d) -> p c d", c=CK), xb2[:, :, :], ALU.add)\
                    .then_inc(r_ready, 1)
                dve.wait_ge(r_ready, this(i))
                measure(i, 0, r)
                normalise(i, 0, r)
                dve.wait_ge(xn_ready[0], this(i, CK, CK))
                measure(i, 1, norms[0][4])
                between()
                normalise(i, 1, norms[0][4])

            def chunk(i, previous):
                def follows(step):
                    dve.wait_ge(step_done, this(i, step, NV))

                dve.wait_ge(h_ready, this(i))
                nc.vector.tensor_scalar(tap0[:, :], hp[:, :, 0:S], k.mix_w1[:, 0:1], k.mix_b1[:, :], ALU.mult, ALU.add)\
                    .then_inc(step_done, 1)
                follows(TAP0)
                nc.vector.scalar_tensor_tensor(split(tap1[:, :]), hp[:, :, 1:S + 1], k.mix_w1[:, 1:2], split(tap0[:, :]),
                                               ALU.mult, ALU.add).then_inc(step_done, 1)
                follows(TAP1)
                dve.wait_ge(proj_ready, last(i, 5, 5))
                nc.vector.scalar_tensor_tensor(split(mixed[:, :]), hp[:, :, 2:S + 2], k.mix_w1[:, 2:3], split(tap1[:, :]),
                                               ALU.mult, ALU.add).then_inc(step_done, 1)

                def recurrence():
                    dve.wait_ge(act_ready, this(i, DECAY + 1, 5))
                    nc.vector.tensor_scalar(keep[:, :], decay[:, :], -1.0, 1.0, ALU.mult, ALU.add).then_inc(step_done, 1)
                    follows(ONE_MINUS)
                    dve.wait_ge(act_ready, this(i, XS + 1, 5))
                    nc.vector.tensor_tensor(drive[:, :], keep[:, :], xs[:, :], ALU.mult).then_inc(step_done, 1)
                    nc.vector.memset(split(decay[:, :])[:, :, 0:1], 0.0).then_inc(step_done, 1)
                    follows(RESET)
                    nc.vector.tensor_tensor_scan(states[:, :], decay[:, :], drive[:, :], 0.0, ALU.mult, ALU.add)\
                        .then_inc(step_done, 1)
                    follows(STATES)
                    dve.wait_ge(state_out_ready, last(i))
                    nc.vector.tensor_tensor(chosen[:, :], states[:, :], sel[:, :], ALU.mult).then_inc(step_done, 1)

                if previous is None:
                    recurrence()
                else:
                    tail(previous, recurrence)
                dve.wait_ge(state_out_ready, this(i))
                dve.wait_ge(act_ready, this(i, 5, 5))
                nc.vector.scalar_tensor_tensor(diff[:, :], psum[:, 5, 0:CT], k.bso1[:, :], u[:, :],
                                               ALU.add, ALU.subtract).then_inc(step_done, 1)
                follows(DIFF)
                nc.vector.tensor_tensor(gdiff[:, :], diff[:, :], g[:, :], ALU.mult).then_inc(step_done, 1)
                follows(GDIFF)
                dve.wait_ge(out_ready, last(i))
                nc.vector.tensor_tensor(z[:, :, 0:S], split(gdiff[:, :]), split(u[:, :]), ALU.add).then_inc(step_done, 1)

            run(dve, chunk, tail)

        @block.scalar
        def _(act):
            open_sems(act, 5, act_ready)
            open_sems(act, 1, feat_stored)

            def tail(i):
                act.wait_ge(xT_ready, this(i))
                nc.scalar.activation(k.x_feat[:, bass.ds(i * CB, CB), :],
                                     psum[:, 7, :].rearrange("p (b s) -> p b s", b=CB)[:, :, 0:S],
                                     ACT.Identity, bias=k.beta1[:, :], scale=k.gamma1[:, :]).then_inc(feat_stored, 1)

            def chunk(i, previous):
                act.wait_ge(step_done, last(i, Z, NV))
                for bank, _, dst, f, bias in PROJECTIONS:
                    act.wait_ge(proj_ready, this(i, bank + 1, 5))
                    nc.scalar.activation(dst[:, :], psum[0:dst.shape[0], bank, 0:CT], f, bias=bias[:, :]).then_inc(act_ready, 1)
                if previous is not None:
                    tail(previous)

            run(act, chunk, tail)


def cross_attention_phase(k):
    nc = k.nc
    WIDTH = (2 * (C // 8) + 2, C // 2 - 2 * (C // 8) - 2)
    FIRST = (0, 2 * WIDTH[0])
    UQ = 128 // H1
    UPS = S // UQ
    NU = 2 * UPS
    GROUPS = [[h * UPS + u for u in g] for h in range(2) for g in ((0, 1), (2, 3), (4, 5), (6,))]
    NG = len(GROUPS)
    GROUP_END = [3, 5, 7, 8, 10, 12, 14, 15]
    SPREAD_AT = [2, 5, 7, 8, 10, 12, 14, 15]
    SLOT = {u: 2 * (j % 2) + e for j, g in enumerate([g for g in GROUPS if len(g) == 2]) for e, u in enumerate(g)}
    SINGLE = [g[0] for g in GROUPS if len(g) == 1]
    HB = 4
    NB = H1 // HB
    PROJECTED = {8: 0, 9: 1, 10: 2, 11: 3}
    SCALE = DH1 ** -0.5
    NLO = 3 * (NU - len(SINGLE))
    with ExitStack() as ctx:
        t = Tail(k, ctx, "xa", router=k.router1, per=1)
        sem = lambda name: k.sem(ctx, "xa_" + name)
        sb = lambda name, shape, dt=fp32: k.sb(ctx, "xa_" + name, shape, dt)
        q_hi, q_lo = sb("q_hi", [128, 2, S, H1], fp32r), sb("q_lo", [128, 2, S, H1], fp32r)
        q_second = sb("q_second", [128, S, H1])
        ctxT = sb("ctxT", [128, C])
        c_hi, c_lo = sb("c_hi", [128, 2, C], fp32r), sb("c_lo", [128, 2, C], fp32r)
        ctxN = sb("ctxN", [KP, 2, KT * D])
        n_hi, n_lo = sb("n_hi", [KP, 2, KT * D], fp32r), sb("n_lo", [KP, 2, KT * D], fp32r)
        pr = sb("pr", [128, 2, C])
        prT_hi, prT_lo = sb("prT_hi", [KP, 4, KT, 128], fp32r), sb("prT_lo", [KP, 4, KT, 128], fp32r)
        prT_single = sb("prT_single", [KP, KT, 128])
        halfmax = sb("halfmax", [128, 2, 2])
        negmax = sb("negmax", [128, 2, 1])
        rs = sb("rs", [128, 2, 2])
        total = sb("total", [128, 2, 1])
        rinv = sb("rinv", [128, NU, 1])
        rb = sb("rb", [128, 2, 256])
        on = sb("on", [128, H1, 2, SP])
        ybo = sb("ybo", [128, D])
        psum = ctx.enter_context(nc.psum_tensor("xa_psum", [128, 8, 512], fp32))
        ctxT_loaded, ctxN_loaded = sem("ctxT_loaded"), [sem("ctxN_loaded0"), sem("ctxN_loaded1")]
        q_ready, q_hi_kept, q_lo_kept = sem("q_ready"), sem("q_hi_kept"), sem("q_lo_kept")
        second_hi_ready, second_lo_ready = sem("second_hi_ready"), sem("second_lo_ready")
        c_hi_ready, c_lo_ready, splitting = sem("c_hi_ready"), sem("c_lo_ready"), sem("splitting")
        n_hi_ready, n_lo_ready = sem("n_hi_ready"), sem("n_lo_ready")
        scores_ready, halfmax_ready, max_ready, exp_ready = sem("scores_ready"), sem("halfmax_ready"), sem("max_ready"), sem("exp_ready")
        total_ready, rinv_ready, rb_ready, rb_kept = sem("total_ready"), sem("rinv_ready"), sem("rb_ready"), sem("rb_kept")
        prT_ready, hi_kept, lo_kept, pv_ready, on_kept = sem("prT_ready"), sem("hi_kept"), sem("lo_kept"), sem("pv_ready"), sem("on_kept")
        on_zeroed, y_ready, ybo_ready = sem("on_zeroed"), sem("y_ready"), sem("ybo_ready")
        block = ctx.enter_context(nc.Block())

        n = lambda i, u: this(i, u + 1, NU)

        def q_count(i, c):
            return this(i, c + 1, NB)

        def lo_count(i, u, r):
            return this(i, 3 * sum(v not in SINGLE for v in range(u)) + r + 1, NLO)

        def groups_before(i, s):
            return this(i, sum(e < s for e in GROUP_END[:NG - 2]) + min(0, s - 2), NG)

        def spreads_before(i, s):
            return this(i, sum(e < s for e in SPREAD_AT[:NG - 2]) + min(0, s - 2), NG)

        def group_at(steps, i, s, first):
            if s in steps:
                return i, steps.index(s)
            if s + NU in steps and not first:
                return i - 1, steps.index(s + NU)
            return None

        def run(engine, step, prologue, epilogue):
            prologue()
            for s in range(UPS):
                step(0, s, first=True)
            with engine.Fori(0, PAIRS - 1) as i:
                for s in range(UPS, NU):
                    step(i, s)
                for s in range(UPS):
                    step(i + 1, s)
            for s in range(UPS, NU):
                step(PAIRS - 1, s, end=True)
            epilogue()

        @block.sync
        def _(sp):
            with sp.Fori(0, PAIRS) as i:
                for h in range(2):
                    sp.wait_ge(c_lo_ready, this(i, h, 2))
                    sp.dma_start(ctxT[:, :].unsqueeze(1),
                                 k.dram["ctxT"][bass.ds(2 * i + h, 1), :, :].rearrange("b d c -> d b c"))\
                        .then_inc(ctxT_loaded, 16)
                    sp.wait_ge(pv_ready, last(i, (h + 1) * NG // 2, NG))
                    sp.dma_start(ctxN[:, h:h + 1, :],
                                 k.dram["ctxN"][bass.ds(2 * i + h, 1), :, :, :].rearrange("b q t d -> q b (t d)"))\
                        .then_inc(ctxN_loaded[h], 16)

        @block.gpsimd
        def _(pool):
            open_sems(pool, 2, c_hi_ready, c_lo_ready, n_hi_ready, n_lo_ready)
            open_sems(pool, 1, second_hi_ready, second_lo_ready)
            t.open_pool(pool)
            pool.memset(on[:, :, :, :], 0.0).then_inc(on_zeroed, 1)
            def split(i):
                for h in range(2):
                    pool.wait_ge(ctxT_loaded, i * 32 + 16 * (h + 1))
                    pool.wait_ge(scores_ready, last(i, 2 * (h + 1) * UPS, 2 * NU))
                    pool.sem_inc(splitting, 1)
                    pool.tensor_copy(c_hi[:, h, :], ctxT[:, :]).then_inc(c_hi_ready, 1)
                    pool.wait_ge(c_hi_ready, this(i, h + 1, 2))
                    pool.tensor_tensor(c_lo[:, h, :], ctxT[:, :], c_hi[:, h, :].bitcast(fp32), ALU.subtract)\
                        .then_inc(c_lo_ready, 1)
                    if h:
                        pool.wait_ge(q_hi_kept, q_count(i, NB - 1))
                        pool.sem_inc(splitting, 1)
                        pool.tensor_copy(q_hi[:, 1, :, :], q_second[:, :, :]).then_inc(second_hi_ready, 1)
                        pool.wait_ge(second_hi_ready, this(i))
                        pool.tensor_tensor(q_lo[:, 1, :, :], q_second[:, :, :], q_hi[:, 1, :, :].bitcast(fp32),
                                           ALU.subtract).then_inc(second_lo_ready, 1)
                    pool.wait_ge(ctxN_loaded[h], (i + 1) * 16)
                    pool.wait_ge(pv_ready, last(i, (h + 1) * NG // 2, NG))
                    pool.sem_inc(splitting, 1)
                    pool.tensor_copy(n_hi[:, h, :], ctxN[:, h, :]).then_inc(n_hi_ready, 1)
                    pool.wait_ge(n_hi_ready, this(i, h + 1, 2))
                    pool.tensor_tensor(n_lo[:, h, :], ctxN[:, h, :], n_hi[:, h, :].bitcast(fp32), ALU.subtract)\
                        .then_inc(n_lo_ready, 1)

            split(0)
            with pool.Fori(1, PAIRS) as i:
                split(i)
                t.pool_rstd(pool, i - 1, 0)
                t.pool_store(pool, i - 1, 0)
            t.pool_rstd(pool, PAIRS - 1, 0)
            t.pool_store(pool, PAIRS - 1, 0)

        @block.tensor
        def _(pe):
            open_sems(pe, NB, q_ready)
            open_sems(pe, 2 * NU, scores_ready)
            open_sems(pe, 3 * NU, prT_ready)
            open_sems(pe, NG, pv_ready, rb_ready)
            open_sems(pe, 1, y_ready)
            t.open_tensor(pe)

            def project(i, c):
                for j in range(HB):
                    done = nc.tensor.matmul(psum[:, 7, j * 2 * S:(j + 1) * 2 * S], k.key_query[:, c * HB + j, :],
                                            k.x_feat[:, bass.ds(2 * i, 2), :], start=True, stop=True)
                done.then_inc(q_ready, 1)

            def scores(i, u):
                h, p0 = u // UPS, (u % UPS) * UQ
                if u % UPS == 0:
                    if h == 0:
                        pe.wait_ge(q_lo_kept, q_count(i, NB - 1))
                    else:
                        pe.wait_ge(second_lo_ready, this(i))
                    pe.wait_ge(c_lo_ready, this(i, h + 1, 2))
                qh = q_hi[:, h, p0:p0 + UQ, :].rearrange("p a b -> p (a b)")
                ql = q_lo[:, h, p0:p0 + UQ, :].rearrange("p a b -> p (a b)")
                for half in range(2):
                    pe.wait_ge(exp_ready, this(i, 2 * (u - 1) + half + 1, 2 * NU))
                    for j in range(2 * half, 2 * half + 2):
                        w = WIDTH[half]
                        keys = slice(FIRST[half] + (j % 2) * w, FIRST[half] + (j % 2 + 1) * w)
                        nc.tensor.matmul(psum[:, j, 0:w], qh, c_hi[:, h, keys], start=True, stop=False)
                        nc.tensor.matmul(psum[:, j, 0:w], qh, c_lo[:, h, keys], start=False, stop=False)
                        done = nc.tensor.matmul(psum[:, j, 0:w], ql, c_hi[:, h, keys], start=False, stop=True)
                    done.then_inc(scores_ready, 1)

            def transposes(i, u, r):
                pe.wait_ge(exp_ready, this(i, 2 * u + (1 if r == 0 else 2), 2 * NU))
                v, q = (u, 0) if r == 2 else (u - 1, 2 if r == 0 else 1)
                if v % NU in SINGLE:
                    pe.wait_ge(hi_kept, this(i, 3 * v + q + 1, 3 * NU))
                else:
                    pe.wait_ge(lo_kept, lo_count(i, v, q))
                for j in range(4):
                    kt = 4 * r + j
                    done = nc.tensor.transpose(psum[0:KP, 4 + r % 2, j * 128:(j + 1) * 128],
                                               pr[:, u % 2, kt * KP:(kt + 1) * KP], k.ident[:, :])
                done.then_inc(prT_ready, 1)

            def spread(i, g):
                pe.wait_ge(rinv_ready, n(i, GROUPS[g][-1]))
                for e, u in enumerate(GROUPS[g]):
                    done = nc.tensor.transpose(psum[:, 7, 256 + 128 * e:384 + 128 * e],
                                               rinv[:, u, :].to_broadcast([128, 128]), k.ident[:, :])
                done.then_inc(rb_ready, 1)

            def values_pair(i, g, part):
                u, h = GROUPS[g][1], GROUPS[g][0] // UPS
                if part == 0:
                    pe.wait_ge(n_lo_ready, this(i, h + 1, 2))
                    pe.wait_ge(on_kept, this(i, g, NG))
                pe.wait_ge(lo_kept, lo_count(i, u, 1 + part))
                out = psum[:, 6, 0:256].rearrange("p (a b) -> p a b", a=2)
                s0 = SLOT[u] - 1
                for kt in range(part * KT // 2, (part + 1) * KT // 2):
                    nh, nl = (v[:, h, kt * D:(kt + 1) * D] for v in (n_hi, n_lo))
                    ph, pl = (v[:, s0:s0 + 2, kt, :] for v in (prT_hi, prT_lo))
                    nc.tensor.matmul(out, nh, ph, start=(kt == 0), stop=False)
                    nc.tensor.matmul(out, nh, pl, start=False, stop=False)
                    done = nc.tensor.matmul(out, nl, ph, start=False, stop=(kt == KT - 1))
                if part:
                    done.then_inc(pv_ready, 1)

            def values_single(i, g):
                u, h = GROUPS[g][0], GROUPS[g][0] // UPS
                pe.wait_ge(ctxN_loaded[h], (i + 1) * 16)
                pe.wait_ge(on_kept, this(i, g, NG))
                pe.wait_ge(hi_kept, this(i, 3 * u + 3, 3 * NU))
                for kt in range(KT):
                    done = nc.tensor.matmul(psum[:, 6, 0:128], ctxN[:, h, kt * D:(kt + 1) * D], prT_single[:, kt, :],
                                            start=(kt == 0), stop=(kt == KT - 1))
                done.then_inc(pv_ready, 1)

            def values(i, s, first):
                for j, e in ((i, 0), (i - 1, NU)) if not first else ((i, 0),):
                    for g, end in enumerate(GROUP_END):
                        if len(GROUPS[g]) == 1 and s + e == end:
                            values_single(j, g)
                        elif len(GROUPS[g]) == 2 and s + e in (end - 1, end):
                            values_pair(j, g, s + e - end + 1)

            def outputs(i, half):
                if half == 0:
                    pe.wait_ge(on_kept, this(i, NG, NG))
                for h in range(half * H1 // 2, (half + 1) * H1 // 2):
                    done = nc.tensor.matmul(psum[:, 7, 0:128], on[:, h, :, :], k.value_out[:, h, :],
                                            start=(h == 0), stop=(h == H1 - 1))
                if half:
                    done.then_inc(y_ready, 1)

            def step(i, s, first=False, end=False):
                if s in PROJECTED and not end:
                    c = PROJECTED[s]
                    pe.wait_ge(rb_kept, spreads_before(i, s))
                    pe.wait_ge(q_lo_kept, q_count(i + 1, c - 1))
                    project(i + 1, c)
                if s + 1 < NU or not end:
                    scores(i, s + 1) if s + 1 < NU else scores(i + 1, 0)
                g = group_at(SPREAD_AT, i, s, first)
                if g:
                    if s in PROJECTED and not end:
                        pe.wait_ge(q_lo_kept, q_count(i + 1, PROJECTED[s]))
                    else:
                        pe.wait_ge(rb_kept, spreads_before(i, s))
                        if s == 12 and not end:
                            pe.wait_ge(q_lo_kept, q_count(i + 1, NB - 1))
                        if s == 5:
                            pe.wait_ge(ybo_ready, this(i, 0, 1))
                        if s == 7:
                            pe.wait_ge(t.logits_kept, this(i, 0, 1))
                    spread(*g)
                transposes(i, s, 0)
                transposes(i, s, 1)
                if s in (2, 3) and not first:
                    pe.wait_ge(rb_kept, spreads_before(i, 3))
                    outputs(i - 1, s - 2)
                if s == 6 and not first:
                    pe.wait_ge(rb_kept, spreads_before(i, s))
                    t.tensor_transpose(pe, i - 1, 0, psum[:, 7, 128:256])
                values(i, s, first)
                if s == 6 and not first:
                    pe.wait_ge(t.feat_stored, this(i, 0, 1))
                    t.tensor_logits(pe, i - 1, 0, psum[:, 7, 0:E])
                transposes(i, s, 2)

            def prologue():
                for c in range(NB):
                    if c:
                        pe.wait_ge(q_lo_kept, q_count(0, c - 1))
                    project(0, c)
                scores(0, 0)

            def epilogue():
                i = PAIRS - 1
                for e in range(2):
                    pe.wait_ge(rb_kept, this(i, NG - 2 + e, NG))
                    spread(i, NG - 2 + e)
                    if e == 0:
                        values_pair(i, NG - 2, 1)
                    else:
                        values_single(i, NG - 1)
                pe.wait_ge(rb_kept, this(i, NG, NG))
                for half in range(2):
                    outputs(i, half)
                pe.wait_ge(ybo_ready, this(i))
                t.tensor_transpose(pe, i, 0, psum[:, 7, 128:256])
                pe.wait_ge(t.feat_stored, this(i))
                t.tensor_logits(pe, i, 0, psum[:, 7, 0:E])

            run(pe, step, prologue, epilogue)

        @block.vector
        def _(dve):
            open_sems(dve, NB, q_lo_kept)
            open_sems(dve, 2 * NU, halfmax_ready)
            open_sems(dve, NLO, lo_kept)
            open_sems(dve, NU, max_ready, total_ready, rinv_ready)
            open_sems(dve, NG, on_kept)
            open_sems(dve, 1, ybo_ready)
            t.open_vector(dve)
            dve.wait_ge(on_zeroed, 1)

            def q_split(i, c):
                dve.wait_ge(q_hi_kept, q_count(i, c))
                nc.vector.scalar_tensor_tensor(
                    q_lo[:, 0, :, c * HB:(c + 1) * HB].rearrange("p s h -> p h s"),
                    psum[:, 7, 0:HB * 2 * S].rearrange("p (h b s) -> p h b s", h=HB, b=2)[:, :, 0, :],
                    SCALE, q_hi[:, 0, :, c * HB:(c + 1) * HB].bitcast(fp32).rearrange("p s h -> p h s"),
                    ALU.mult, ALU.subtract).then_inc(q_lo_kept, 1)

            def maxima(i, u):
                for half in range(2):
                    dve.wait_ge(scores_ready, this(i, 2 * u + half + 1, 2 * NU))
                    nc.vector.tensor_reduce(halfmax[:, u % 2, half:half + 1], psum[:, 2 * half:2 * half + 2, 0:WIDTH[half]],
                                            AX.XY, ALU.max, negate=True).then_inc(halfmax_ready, 1)
                dve.wait_ge(halfmax_ready, this(i, 2 * u + 2, 2 * NU))
                nc.vector.tensor_tensor(negmax[:, u % 2, :], halfmax[:, u % 2, 0:1], halfmax[:, u % 2, 1:2],
                                        ALU.min).then_inc(max_ready, 1)

            def low_part(i, u, r):
                if u not in SINGLE:
                    dve.wait_ge(hi_kept, this(i, 3 * u + r + 1, 3 * NU))
                    tiles = slice(4 * r, 4 * r + 4)
                    nc.vector.tensor_tensor(prT_lo[:, SLOT[u], tiles, :].rearrange("p a b -> p (a b)"), psum[0:KP, 4 + r % 2, :],
                                            prT_hi[:, SLOT[u], tiles, :].rearrange("p a b -> p (a b)").bitcast(fp32),
                                            ALU.subtract).then_inc(lo_kept, 1)

            def inverse(i, u):
                dve.wait_ge(exp_ready, this(i, 2 * u + 2, 2 * NU))
                nc.vector.tensor_tensor(total[:, u % 2, :], rs[:, u % 2, 0:1], rs[:, u % 2, 1:2], ALU.add)\
                    .then_inc(total_ready, 1)
                dve.wait_ge(total_ready, n(i, u))
                nc.vector.reciprocal(rinv[:, u, :], total[:, u % 2, :]).then_inc(rinv_ready, 1)

            def normalise(i, g):
                dve.wait_ge(pv_ready, this(i, g + 1, NG))
                dve.wait_ge(rb_kept, this(i, g + 1, NG))
                if g == 0:
                    dve.wait_ge(y_ready, this(i, 0, 1))
                u, m = GROUPS[g][0], len(GROUPS[g])
                h, p0 = u // UPS, (u % UPS) * UQ
                nc.vector.tensor_tensor(on[:, :, h, p0:p0 + m * UQ],
                                        psum[:, 6, 0:128 * m].rearrange("p (s h) -> p h s", h=H1),
                                        rb[:, g % 2, 0:128 * m].rearrange("p (s h) -> p h s", h=H1), ALU.mult)\
                    .then_inc(on_kept, 1)

            def residual(i):
                dve.wait_ge(y_ready, this(i))
                nc.vector.tensor_tensor(ybo[:, :], psum[:, 7, 0:128], k.bout_row1x[:, :], ALU.add).then_inc(ybo_ready, 1)
                dve.wait_ge(ybo_ready, this(i))
                nc.vector.scalar_tensor_tensor(t.r[:, :, :], ybo[:, :].unsqueeze(1), k.gate_tanh[:, :],
                                               k.x_tok[:, bass.ds(i, 1), :], ALU.mult, ALU.add).then_inc(t.r_ready, 1)
                t.vector_moments(dve, i, 0)

            def step(i, s, first=False, end=False):
                if s:
                    low_part(i, s - 1, 2)
                elif not first:
                    low_part(i - 1, NU - 1, 2)
                if s in PROJECTED and not end:
                    q_split(i + 1, PROJECTED[s])
                if s + 1 < NU or not end:
                    maxima(i, s + 1) if s + 1 < NU else maxima(i + 1, 0)
                inverse(i, s)
                low_part(i, s, 0)
                low_part(i, s, 1)
                if s == 3 and not first:
                    residual(i - 1)
                if s == 5 and not first:
                    t.vector_normalise(dve, i - 1, 0)
                if s == 6 and not first:
                    t.vector_logits(dve, i - 1, 0, psum[:, 7, 0:E])
                g = group_at(GROUP_END, i, s, first)
                if g:
                    normalise(*g)

            def prologue():
                for c in range(NB):
                    q_split(0, c)
                maxima(0, 0)

            def epilogue():
                i = PAIRS - 1
                low_part(i, NU - 1, 2)
                normalise(i, NG - 2)
                normalise(i, NG - 1)
                residual(i)
                t.vector_normalise(dve, i, 0)
                t.vector_logits(dve, i, 0, psum[:, 7, 0:E])

            run(dve, step, prologue, epilogue)

        @block.scalar
        def _(act):
            open_sems(act, NB, q_hi_kept)
            open_sems(act, 2 * NU, exp_ready)
            open_sems(act, 3 * NU, hi_kept)
            open_sems(act, NG, rb_kept)
            t.open_scalar(act)

            def q_high(i, c):
                if c == 0:
                    act.wait_ge(scores_ready, last(i, 2 * UPS, 2 * NU))
                    act.wait_ge(second_lo_ready, last(i))
                act.wait_ge(q_ready, q_count(i, c))
                for b_, dst in enumerate((q_hi[:, 0, :, :], q_second[:, :, :])):
                    done = nc.scalar.activation(
                        dst[:, :, c * HB:(c + 1) * HB].rearrange("p s h -> p h s"),
                        psum[:, 7, 0:HB * 2 * S].rearrange("p (h b s) -> p h b s", h=HB, b=2)[:, :, b_, :],
                        ACT.Copy, scale=SCALE)
                done.then_inc(q_hi_kept, 1)

            def high_part(i, u, r):
                act.wait_ge(prT_ready, this(i, 3 * u + r + 1, 3 * NU))
                act.wait_ge(pv_ready, groups_before(i, u))
                dst = prT_single[:, 4 * r:4 * r + 4, :] if u in SINGLE else prT_hi[:, SLOT[u], 4 * r:4 * r + 4, :]
                nc.scalar.activation(dst.rearrange("p a b -> p (a b)"), psum[0:KP, 4 + r % 2, :], ACT.Copy)\
                    .then_inc(hi_kept, 1)

            def exponentials(i, u):
                act.wait_ge(max_ready, n(i, u))
                act.wait_ge(prT_ready, this(i, 3 * (u - 1), 3 * NU))
                act.wait_ge(total_ready, n(i, u - 2))
                for half in range(2):
                    keys = slice(FIRST[half], FIRST[half] + 2 * WIDTH[half])
                    nc.scalar.activation(pr[:, u % 2, keys].rearrange("p (a c) -> p a c", a=2),
                                         psum[:, 2 * half:2 * half + 2, 0:WIDTH[half]], ACT.Exp, bias=negmax[:, u % 2, :],
                                         accum_out=rs[:, u % 2, half:half + 1]).then_inc(exp_ready, 1)

            def keep_spread(i, g):
                act.wait_ge(rb_ready, this(i, g + 1, NG))
                act.wait_ge(on_kept, this(i, g - 1, NG))
                m = 128 * len(GROUPS[g])
                nc.scalar.activation(rb[:, g % 2, 0:m], psum[:, 7, 256:256 + m], ACT.Copy).then_inc(rb_kept, 1)

            def step(i, s, first=False, end=False):
                if s:
                    high_part(i, s - 1, 2)
                elif not first:
                    high_part(i - 1, NU - 1, 2)
                if s in PROJECTED and not end:
                    q_high(i + 1, PROJECTED[s])
                g = group_at(SPREAD_AT, i, s, first)
                if g:
                    keep_spread(*g)
                high_part(i, s, 0)
                high_part(i, s, 1)
                if s == 6 and not first:
                    t.scalar_store(act, i - 1, 0, psum[:, 7, 128:256])
                if s + 1 < NU or not end:
                    exponentials(i, s + 1) if s + 1 < NU else exponentials(i + 1, 0)

            def prologue():
                for c in range(NB):
                    q_high(0, c)
                exponentials(0, 0)

            def epilogue():
                i = PAIRS - 1
                high_part(i, NU - 1, 2)
                keep_spread(i, NG - 2)
                keep_spread(i, NG - 1)
                t.scalar_store(act, i, 0, psum[:, 7, 128:256])

            run(act, step, prologue, epilogue)


def declare(k, ctx):
    sb = lambda name, shape, dt=fp32: k.sb(ctx, name, shape, dt)
    k.x_tok = sb("x_tok", [128, PAIRS, D])
    k.x_feat = sb("x_feat", [128, B, S])
    k.ident = sb("ident", [128, 128])
    k.window_mask = sb("window_mask", [128, S])
    k.head_mask = sb("head_mask", [128, H0])
    k.value_mask = sb("value_mask", [128, H0 // 2, 2, DH0])
    k.minus_half = sb("minus_half", [128, 1])
    k.eps = sb("eps", [128, 1])
    k.expert_index_u = sb("expert_index_u", [128, E], u32)
    k.expert_index = sb("expert_index", [128, E])
    k.wqT0, k.wkT0, k.wvT0, k.woT0 = (sb(n, [128, D]) for n in ("wqT0", "wkT0", "wvT0", "woT0"))
    k.bq0, k.bk0, k.bv0 = (sb(n, [128, 1]) for n in ("bq0", "bk0", "bv0"))
    k.bq0_scaled = sb("bq0_scaled", [128, 1])
    k.bo_row0 = sb("bo_row0", [128, D])
    k.wqT0x, k.wk0x, k.wv0x, k.woT0x, k.value_out0 = (sb(n, [128, D]) for n in ("wqT0x", "wk0x", "wv0x", "woT0x", "value_out0"))
    k.bq0x, k.bv0x = (sb(n, [128, 1]) for n in ("bq0x", "bv0x"))
    k.bo_row0x = sb("bo_row0x", [128, D])
    k.cross_row = sb("cross_row", [128, D])
    k.router0 = sb("router0", [128, E])
    k.ln_g1, k.ln_b1, k.mix_b1, k.bi1, k.bg1, k.bso1 = (sb(n, [128, 1]) for n in ("ln_g1", "ln_b1", "mix_b1", "bi1", "bg1", "bso1"))
    k.mix_w1 = sb("mix_w1", [128, 3])
    k.wi1, k.wg1, k.wout1 = (sb(n, [128, D]) for n in ("wi1", "wg1", "wout1"))
    k.wsin1, k.wd1, k.wsel1 = (sb(n, [128, 32]) for n in ("wsin1", "wd1", "wsel1"))
    k.wso1 = sb("wso1", [32, D])
    k.bsin1, k.bd1, k.bsel1 = (sb(n, [32, 1]) for n in ("bsin1", "bd1", "bsel1"))
    k.bout_row1 = sb("bout_row1", [128, D])
    k.gamma1, k.beta1 = (sb(n, [128, 1]) for n in ("gamma1", "beta1"))
    k.key_query = sb("key_query", [128, H1, D])
    k.value_out = sb("value_out", [128, H1, D])
    k.bout_row1x = sb("bout_row1x", [128, D])
    k.gate_in, k.gate_tanh = sb("gate_in", [128, 1]), sb("gate_tanh", [128, 1])
    k.router1 = sb("router1", [128, E])
    k.router_bias_row1 = sb("router_bias_row1", [128, E])
    k.logits = sb("logits", [128, PAIRS, E])
    k.expert_weights = sb("expert_weights", [128, PAIRS, E])
    sem = lambda name: k.sem(ctx, name)
    k.weights_loaded = sem("weights_loaded")
    k.loads = [
        ("L0_wqT", k.wqT0[:, :]), ("L0_wkT", k.wkT0[:, :]), ("L0_wvT", k.wvT0[:, :]), ("L0_woT", k.woT0[:, :]),
        ("L0_bq", k.bq0[:, :]), ("L0_bk", k.bk0[:, :]), ("L0_bv", k.bv0[:, :]), ("L0_bo", k.bo_row0[:, :]),
        ("X0_wqT", k.wqT0x[:, :]), ("X0_wk", k.wk0x[:, :]), ("X0_wv", k.wv0x[:, :]), ("X0_woT", k.woT0x[:, :]),
        ("X0_bq", k.bq0x[:, :]), ("X0_bv", k.bv0x[:, :]), ("X0_bo", k.bo_row0x[:, :]), ("gate", k.gate_in[:, :]),
    ]
    k.late_loads = [
        ("F0_router", k.router0[:, :]),
        ("L1_ln_g", k.ln_g1[:, :]), ("L1_ln_b", k.ln_b1[:, :]), ("L1_mix_b", k.mix_b1[:, :]),
        ("L1_bi", k.bi1[:, :]), ("L1_bg", k.bg1[:, :]), ("L1_bso", k.bso1[:, :]), ("L1_mix_w", k.mix_w1[:, :]),
        ("L1_wi", k.wi1[:, :]), ("L1_wg", k.wg1[:, :]), ("L1_wout", k.wout1[:, :]),
        ("L1_wsin", k.wsin1[:, :]), ("L1_wd", k.wd1[:, :]), ("L1_wsel", k.wsel1[:, :]), ("L1_wso", k.wso1[:, :]),
        ("L1_bsin", k.bsin1[:, :]), ("L1_bd", k.bd1[:, :]), ("L1_bsel", k.bsel1[:, :]), ("L1_bout", k.bout_row1[:, :]),
        ("L1_gamma", k.gamma1[:, :]), ("L1_beta", k.beta1[:, :]), ("X1_bout", k.bout_row1x[:, :]),
        ("F1_router", k.router1[:, :]), ("F1_router_bias", k.router_bias_row1[:, :]),
    ]


def declare_weights0(k, ctx):
    sb = lambda name, shape: k.sb(ctx, name, shape)
    k.up0 = sb("up0", [128, E, U0])
    k.up_bias0 = sb("up_bias0", [128, E, U0 // 128])
    k.down0 = sb("down0", [128, E, U0 // 128, D])
    k.down_bias0 = sb("down_bias0", [128, E])
    k.late_loads += [("F0_up", k.up0[:, :, :]), ("F0_up_bias", k.up_bias0[:, :, :]),
                     ("F0_down", k.down0[:, :, :, :]), ("F0_down_bias", k.down_bias0[:, :])]


def declare_context_ring(k, ctx):
    k.ctxT = k.sb(ctx, "ctxT", [128, 2, 2, C])
    k.ctxN = k.sb(ctx, "ctxN", [KP, 2, 2, KT * D])
    k.ctxT_loaded = [ctx.enter_context(k.nc.semaphore(f"ctxT_loaded{p}")) for p in range(2)]
    k.ctxN_loaded = [ctx.enter_context(k.nc.semaphore(f"ctxN_loaded{p}")) for p in range(2)]
    k.context_semaphores = [s.num for s in k.ctxT_loaded + k.ctxN_loaded]


def declare_parts(k, ctx, layer, **weights):
    k.parts = {}
    for name, source in weights.items():
        shape = list(source.shape)
        k.parts[name] = (source, k.sb(ctx, f"{name}_hi{layer}", shape, fp32r), k.sb(ctx, f"{name}_lo{layer}", shape, fp32r))


def declare_weights1(k, ctx):
    sb = lambda name, shape: k.sb(ctx, name, shape)
    k.gate1 = sb("gate1", [128, E + 1, I1])
    k.up1 = sb("up1", [128, E + 1, I1])
    k.down1 = sb("down1", [128, E + 1, I1 // 128, D])
    k.expert_loads = {
        "gate": [("F1_gate", k.gate1[:, 0:E, :]), ("F1_gate_s", k.gate1[:, E, :])],
        "up": [("F1_up", k.up1[:, 0:E, :]), ("F1_up_s", k.up1[:, E, :])],
        "down": [("F1_down", k.down1[:, 0:E, :, :]), ("F1_down_s", k.down1[:, E, :, :])],
    }


ROWS = ("L0_bo", "X0_bo", "L1_bout", "X1_bout", "F1_router_bias", "gate")


def layouts(a):
    c = np.ascontiguousarray
    col = lambda v: c(v.reshape(-1, 1))
    ctx = a["ctx_1024"]
    w_kv = a["L1_xattn_w_kv"]
    halves = lambda w: c(w.reshape(DH1, 2, H1 // 2, D).transpose(1, 0, 2, 3).reshape(2 * DH1, H1 // 2, D))
    heads = lambda w: halves(w.reshape(D, H1, DH1).transpose(2, 1, 0))
    out = {
        "x_pairs": c(a["x"].reshape(PAIRS, 2, S, D).transpose(1, 2, 0, 3)),
        "xT": c(a["x"].transpose(2, 0, 1)),
        "ctxT": c(ctx.transpose(0, 2, 1)),
        "ctxN": c(ctx.reshape(B, KT, KP, D).transpose(0, 2, 1, 3)),
        "L0_wqT": c(a["L0_attn_wq"].T), "L0_wkT": c(a["L0_attn_wk"].T),
        "L0_wvT": c(a["L0_attn_wv"].T), "L0_woT": c(a["L0_attn_wo"].T),
        "L0_bq": col(a["L0_attn_bq"]), "L0_bk": col(a["L0_attn_bk"]), "L0_bv": col(a["L0_attn_bv"]), "L0_bo": a["L0_attn_bo"],
        "X0_wqT": c(a["L0_xattn_Wq"].T), "X0_wk": a["L0_xattn_Wk"], "X0_wv": a["L0_xattn_Wv"],
        "X0_woT": c(a["L0_xattn_Wo"].T), "X0_bq": col(a["L0_xattn_bq"]), "X0_bv": col(a["L0_xattn_bv"]), "X0_bo": a["L0_xattn_bo"],
        "F0_router": c(a["L0_ffn_w_router"].T), "F0_up": c(a["L0_ffn_w_up"].transpose(2, 0, 1)),
        "F0_up_bias": c(a["L0_ffn_b_up"].reshape(E, U0 // 128, 128).transpose(2, 0, 1)),
        "F0_down": c(a["L0_ffn_w_down"].reshape(E, D, U0 // 128, 128).transpose(3, 0, 2, 1)),
        "F0_down_bias": c(a["L0_ffn_b_down"].T),
        "L1_ln_g": col(a["L1_attn_ln_g"]), "L1_ln_b": col(a["L1_attn_ln_b"]), "L1_mix_b": col(a["L1_attn_mix_b"]),
        "L1_mix_w": c(a["L1_attn_mix_w"].reshape(D, 3)),
        "L1_wi": a["L1_attn_Wi"], "L1_wg": a["L1_attn_Wg"], "L1_wout": a["L1_attn_Wout"], "L1_wsin": a["L1_attn_Wsin"],
        "L1_wd": a["L1_attn_Wd"], "L1_wsel": a["L1_attn_Wsel"], "L1_wso": a["L1_attn_Wso"],
        "L1_bi": col(a["L1_attn_bi"]), "L1_bg": col(a["L1_attn_bg"]), "L1_bso": col(a["L1_attn_bso"]),
        "L1_bsin": col(a["L1_attn_bsin"]), "L1_bd": col(a["L1_attn_bd"]), "L1_bsel": col(a["L1_attn_bsel"]),
        "L1_bout": a["L1_attn_bout"],
        "L1_gamma": col(a["L1_xattn_ln_gamma"]), "L1_beta": col(a["L1_xattn_ln_beta"]),
        "L1_wqT": heads(a["L1_xattn_w_q"]), "L1_wkT": heads(c(w_kv[:, :H1 * DH1])), "L1_wvT": heads(c(w_kv[:, H1 * DH1:])),
        "L1_wo": halves(a["L1_xattn_w_out"].reshape(H1, DH1, D).transpose(1, 0, 2)),
        "X1_bout": a["L1_xattn_b_out"], "gate": a["L1_xattn_gate"],
        "F1_router": c(a["L1_ffn_router_w"].T), "F1_router_bias": a["L1_ffn_routing_bias"],
        "F1_gate": c(a["L1_ffn_gate_w"].transpose(1, 0, 2)), "F1_up": c(a["L1_ffn_up_w"].transpose(1, 0, 2)),
        "F1_down": c(a["L1_ffn_down_w"].reshape(E, I1 // 128, 128, D).transpose(2, 0, 1, 3)),
        "F1_gate_s": c(a["L1_ffn_shared_gate"].T), "F1_up_s": c(a["L1_ffn_shared_up"].T),
        "F1_down_s": c(a["L1_ffn_shared_down"].reshape(D, I1 // 128, 128).transpose(2, 1, 0)),
    }
    return {name: c(v) for name, v in out.items()}
def build(nc, dram, out):
    with ExitStack() as ctx:
        k = Core(nc, ctx, dram)
        k.out = out
        declare(k, ctx)

        def run(*phases):
            for phase in phases:
                phase(k)
                k.clear_semaphores()

        with ExitStack() as layer0:
            declare_weights0(k, layer0)
            with ExitStack() as ring:
                declare_context_ring(k, ring)
                run(setup_phase, self_attention_phase, context_attention_phase)
            with ExitStack() as parts:
                declare_parts(k, parts, 0, up=k.up0, down=k.down0)
                run(expert_phase0)
        run(state_space_phase, cross_attention_phase)
        with ExitStack() as layer1:
            declare_weights1(k, layer1)
            declare_parts(k, layer1, 1, gate=k.gate1, up=k.up1, down=k.down1)
            run(expert_phase1)


def kernel(**inputs):
    import concourse.bacc as bacc
    from concourse.bass_utils import run_bass_kernel_spmd

    arrays = {"in_" + name: a for name, a in layouts({n: np.asarray(v) for n, v in inputs.items()}).items()}
    nc = bacc.Bacc("TRN2", target_bir_lowering=False, num_devices=1)
    dram = {}
    for name, a in arrays.items():
        ap = nc.dram_tensor(name, list(a.shape), fp32, kind="ExternalInput").ap()
        name = name[3:]
        dram[name] = ap.partition_broadcast(128) if name in ROWS else ap
    out = nc.dram_tensor("out_0", [B, S, D], fp32, kind="ExternalOutput").ap()
    build(nc, dram, out)
    r = run_bass_kernel_spmd(nc, [arrays], core_ids=[0])
    return r.results[0]["out_0"]
```
